# Optimizing a Trainium2 kernel written in Bass

```python
import numpy as np
import jax
import jax.numpy as jnp

def _softmax(x, axis=-1):
    return jax.nn.softmax(x, axis=axis)

def _gelu(x):
    return jax.nn.gelu(x, approximate=True)

def _silu(x):
    return jax.nn.silu(x)

def _sigmoid(x):
    return jax.nn.sigmoid(x)

def _layernorm(x, axis=-1, eps=1e-05):
    m = jnp.mean(x, axis=axis, keepdims=True)
    v = jnp.var(x, axis=axis, keepdims=True)
    return (x - m) / jnp.sqrt(v + eps)

def _scatter_add(tgt, idx, src, axis=0):
    return tgt.at[idx].add(src)

def _segment_sum(src, seg, n):
    return jax.ops.segment_sum(src, seg, n)
kernel_name = 'mk_adj_ffn_d4_adj_r2_d1497d'

def setup_inputs(seed: int=0):
    np.random.seed(seed)
    _w = jnp.asarray

    def _rec_inputs():
        import jax
        import jax.numpy as jnp
        _gk = jax.random.key(seed)
        x = 7.22e-05 + 1 * jax.random.normal(jax.random.fold_in(_gk, 1), (32, 256, 128), jnp.float32)
        _a = jax.random.bernoulli(jax.random.fold_in(_gk, 2), 0.0078125, (32, 256, 256))
        _a = jnp.logical_or(_a, jnp.swapaxes(_a, -1, -2))
        _a = jnp.logical_or(_a, jnp.eye(256, dtype=bool))
        _af = _a.astype(jnp.float32)
        _af = _af * jax.random.uniform(jax.random.fold_in(_gk, 3), (32, 256, 256), jnp.float32, 0.05, 1)
        adj = _af
        _nm = jnp.ones((32, 256), dtype=bool)
        nodemask = jnp.where(_nm, 1.0, 0.0).astype(jnp.int32)
        return (x, adj, nodemask)
    x, adj, nodemask = _rec_inputs()

    def _L0_gnn_setup():
        import jax, jax.numpy as jnp
        import numpy as np
        MIN_VALUE = 1e-10
        key = jax.random.key(seed)
        k1, k2, k3, k4, k5 = jax.random.split(key, 5)
        B, N, F, P = (32, 512, 128, 128)
        x = jax.random.normal(k1, (B, N, F), dtype=jnp.float32)
        adjacency_matrix = jax.random.uniform(k2, (B, N, N), dtype=jnp.float32)
        bound = 1.0 / np.sqrt(F)
        W = jax.random.uniform(k3, (P, F), minval=-bound, maxval=bound, dtype=jnp.float32)
        b = jax.random.uniform(k4, (P,), minval=-bound, maxval=bound, dtype=jnp.float32)
        alpha = jax.random.uniform(k5, (1,), dtype=jnp.float32)
        return {'x': x, 'adjacency_matrix': adjacency_matrix, 'W': W, 'b': b, 'alpha': alpha}
    _L0_gnn_all = _L0_gnn_setup()
    _L0_gnn_in = {k: v for k, v in _L0_gnn_all.items() if k in ('W', 'b', 'alpha')}
    del _L0_gnn_all

    def _L0_ffn_setup():
        import jax, jax.numpy as jnp
        import numpy as np
        B, S, D, F, E, K = (8, 1024, 128, 512, 8, 2)
        key = jax.random.key(seed)
        ks = jax.random.split(key, 10)
        s = 0.02
        return {'x': jax.random.normal(ks[0], (B, S, D), dtype=jnp.float32), 'Wr': jax.random.normal(ks[1], (D, E), dtype=jnp.float32) * s, 'W1s': jax.random.normal(ks[2], (D, F), dtype=jnp.float32) * s, 'b1s': jnp.zeros((F,), dtype=jnp.float32), 'W2s': jax.random.normal(ks[3], (F, D), dtype=jnp.float32) * s, 'b2s': jnp.zeros((D,), dtype=jnp.float32), 'W1p': jax.random.normal(ks[4], (E, D, F), dtype=jnp.float32) * s, 'b1p': jnp.zeros((E, F), dtype=jnp.float32), 'W2p': jax.random.normal(ks[5], (E, F, D), dtype=jnp.float32) * s, 'b2p': jnp.zeros((E, D), dtype=jnp.float32)}
    _L0_ffn_all = _L0_ffn_setup()
    _L0_ffn_in = {k: v for k, v in _L0_ffn_all.items() if k in ('Wr', 'W1s', 'b1s', 'W2s', 'b2s', 'W1p', 'b1p', 'W2p', 'b2p')}
    del _L0_ffn_all

    def _L1_gnn_setup():
        import jax, jax.numpy as jnp
        import numpy as np
        B, N = (1, 2048)
        D_IN, D_OUT, H = (128, 128, 8)
        HD = D_OUT // H
        NEG = -9000000000000000.0

        def _xavier(key, shape):
            lim = np.sqrt(6.0 / (shape[0] + shape[1])).astype(np.float32)
            return jax.random.uniform(key, shape, jnp.float32, -lim, lim)
        key = jax.random.key(seed)
        ks = jax.random.split(key, 8)
        x = jax.random.normal(ks[0], (B, N, D_IN), jnp.float32)
        adj = (jax.random.uniform(ks[1], (B, N, N)) < 0.05).astype(jnp.float32)
        idx = jnp.arange(N)
        adj = adj.at[:, idx, idx].set(1.0)
        Wq = _xavier(ks[2], (D_IN, D_OUT))
        bq = jnp.zeros((D_OUT,), jnp.float32)
        Wk = _xavier(ks[3], (D_IN, D_OUT))
        bk = jnp.zeros((D_OUT,), jnp.float32)
        Wv = _xavier(ks[4], (D_IN, D_OUT))
        bv = jnp.zeros((D_OUT,), jnp.float32)
        Wo = _xavier(ks[5], (D_OUT, D_OUT))
        bo = jnp.zeros((D_OUT,), jnp.float32)
        return dict(x=x, adj=adj, Wq=Wq, bq=bq, Wk=Wk, bk=bk, Wv=Wv, bv=bv, Wo=Wo, bo=bo)
    _L1_gnn_all = _L1_gnn_setup()
    _L1_gnn_in = {k: v for k, v in _L1_gnn_all.items() if k in ('Wq', 'bq', 'Wk', 'bk', 'Wv', 'bv', 'Wo', 'bo')}
    del _L1_gnn_all

    def _L1_ffn_setup():
        import math
        import jax, jax.numpy as jnp
        import numpy as np
        CAPACITY_FACTOR = 1.25
        TOP_K = 2
        LN_EPS = 1e-05

        def _layer_norm(x, gamma, beta):
            mu = jnp.mean(x, axis=-1, keepdims=True)
            var = jnp.var(x, axis=-1, keepdims=True)
            return (x - mu) * jax.lax.rsqrt(var + LN_EPS) * gamma + beta
        key = jax.random.key(seed)
        ks = jax.random.split(key, 4)
        B, S, D, F, E = (8, 2048, 128, 256, 8)
        x = jax.random.normal(ks[0], (B, S, D), dtype=jnp.float32)
        Wr = jax.random.normal(ks[1], (D, E), dtype=jnp.float32) / np.sqrt(D)
        br = jnp.zeros((E,), jnp.float32)
        W1 = jax.random.normal(ks[2], (E, D, F), dtype=jnp.float32) / np.sqrt(D)
        b1 = jnp.zeros((E, F), jnp.float32)
        W2 = jax.random.normal(ks[3], (E, F, D), dtype=jnp.float32) / np.sqrt(F)
        b2 = jnp.zeros((E, D), jnp.float32)
        gamma = jnp.ones((D,), jnp.float32)
        beta = jnp.zeros((D,), jnp.float32)
        return {'x': x, 'Wr': Wr, 'br': br, 'W1': W1, 'b1': b1, 'W2': W2, 'b2': b2, 'gamma': gamma, 'beta': beta}
    _L1_ffn_all = _L1_ffn_setup()
    _L1_ffn_in = {k: v for k, v in _L1_ffn_all.items() if k in ('Wr', 'br', 'W1', 'b1', 'W2', 'b2', 'gamma', 'beta')}
    del _L1_ffn_all

    def _L2_gnn_setup():
        import jax, jax.numpy as jnp
        import numpy as np
        NEG_SLOPE = -0.2
        MASK_VAL = -9000000000000000.0
        key = jax.random.key(seed)
        k1, k2, k3, k4 = jax.random.split(key, 4)
        B, N, F, O = (8, 1024, 128, 128)
        x = jax.random.normal(k1, (B, N, F), dtype=jnp.float32)
        adj = jax.random.normal(k2, (B, N, N), dtype=jnp.float32)
        bw = 1.414 * np.sqrt(6.0 / (F + O))
        W_a = jax.random.uniform(k3, (F, O), minval=-bw, maxval=bw, dtype=jnp.float32)
        bb = 1.414 * np.sqrt(6.0 / (1 + O))
        bias = jax.random.uniform(k4, (1, O), minval=-bb, maxval=bb, dtype=jnp.float32)
        return {'x': x, 'adj': adj, 'W_a': W_a, 'bias': bias}
    _L2_gnn_all = _L2_gnn_setup()
    _L2_gnn_in = {k: v for k, v in _L2_gnn_all.items() if k in ('W_a', 'bias')}
    del _L2_gnn_all

    def _L2_ffn_setup():
        import jax, jax.numpy as jnp
        import numpy as np
        B, S, H, NH, NE = (4, 512, 128, 4, 4)
        D = H // NH
        EPS = 1e-08

        def layernorm(x, g, b):
            m = jnp.mean(x, axis=-1, keepdims=True)
            v = jnp.mean((x - m) ** 2, axis=-1, keepdims=True)
            return (x - m) / jnp.sqrt(v + EPS) * g + b
        key = jax.random.key(seed)
        ks = jax.random.split(key, 18)
        sc = 0.05
        return {'x': jax.random.normal(ks[0], (B, S, H), jnp.float32), 'hl_w': jax.random.normal(ks[1], (NH, D, H), jnp.float32) * sc, 'hl_b': jax.random.normal(ks[2], (NH, D), jnp.float32) * sc, 'wq': jax.random.normal(ks[3], (NH, NE, D, D), jnp.float32) * sc, 'wk': jax.random.normal(ks[4], (NH, D, D), jnp.float32) * sc, 'wv': jax.random.normal(ks[5], (NH, D, D), jnp.float32) * sc, 'gate_w': jax.random.normal(ks[6], (NH, NE, NE * D), jnp.float32) * sc, 'gate_b': jax.random.normal(ks[7], (NH, NE), jnp.float32) * sc, 'ln_g': jnp.ones((D,), jnp.float32), 'ln_b': jnp.zeros((D,), jnp.float32), 'fc1_w': jax.random.normal(ks[8], (D, D), jnp.float32) * sc, 'fc1_b': jax.random.normal(ks[9], (D,), jnp.float32) * sc, 'fc2_w': jax.random.normal(ks[10], (D, D), jnp.float32) * sc, 'fc2_b': jax.random.normal(ks[11], (D,), jnp.float32) * sc, 'fnorm_g': jnp.ones((D,), jnp.float32), 'fnorm_b': jnp.zeros((D,), jnp.float32), 'fgate_w': jax.random.normal(ks[12], (NH, H), jnp.float32) * sc}
    _L2_ffn_all = _L2_ffn_setup()
    _L2_ffn_in = {k: v for k, v in _L2_ffn_all.items() if k in ('hl_w', 'hl_b', 'wq', 'wk', 'wv', 'gate_w', 'gate_b', 'ln_g', 'ln_b', 'fc1_w', 'fc1_b', 'fc2_w', 'fc2_b', 'fnorm_g', 'fnorm_b', 'fgate_w')}
    del _L2_ffn_all

    def _L3_gnn_setup():
        import jax, jax.numpy as jnp
        import numpy as np
        HIDDEN = 128
        NEG_INF = -1e+30
        key = jax.random.key(seed)
        k1, k2, k3, k4 = jax.random.split(key, 4)
        B, S, H = (4, 2048, HIDDEN)
        matrix = jax.random.normal(k1, (B, S, H), dtype=jnp.float32)
        mask = jax.random.randint(k2, (B, S), 0, 2, dtype=jnp.int32)
        adj = jax.random.uniform(k3, (B, S, S), dtype=jnp.float32)
        limit = float(np.sqrt(6.0 / (H + H)))
        W = jax.random.uniform(k4, (H, H), dtype=jnp.float32, minval=-limit, maxval=limit)
        return {'matrix': matrix, 'mask': mask, 'adj': adj, 'W': W}
    _L3_gnn_all = _L3_gnn_setup()
    _L3_gnn_in = {k: v for k, v in _L3_gnn_all.items() if k in ('W',)}
    del _L3_gnn_all

    def _L3_ffn_setup():
        import jax, jax.numpy as jnp
        import numpy as np
        E, D, H, TOP_K = (6, 128, 128, 2)
        ROUTER_H = D // 2
        key = jax.random.key(seed)
        ks = jax.random.split(key, 12)
        s = 1.0 / np.sqrt(D)
        sh = 1.0 / np.sqrt(H)
        sr = 1.0 / np.sqrt(ROUTER_H)
        return {'features': jax.random.normal(ks[0], (8, 2048, D), dtype=jnp.float32), 'router_w1': jax.random.uniform(ks[1], (D, ROUTER_H), jnp.float32, -s, s), 'router_b1': jnp.zeros((ROUTER_H,), jnp.float32), 'router_w2': jax.random.uniform(ks[2], (ROUTER_H, E), jnp.float32, -sr, sr), 'router_b2': jnp.zeros((E,), jnp.float32), 'expert_w1': jax.random.uniform(ks[3], (E, D, H), jnp.float32, -s, s), 'expert_b1': jnp.zeros((E, H), jnp.float32), 'expert_w2': jax.random.uniform(ks[4], (E, H, H), jnp.float32, -sh, sh), 'expert_b2': jnp.zeros((E, H), jnp.float32), 'expert_w3': jax.random.uniform(ks[5], (E, H, D), jnp.float32, -sh, sh), 'expert_b3': jnp.zeros((E, D), jnp.float32)}
    _L3_ffn_all = _L3_ffn_setup()
    _L3_ffn_in = {k: v for k, v in _L3_ffn_all.items() if k in ('router_w1', 'router_b1', 'router_w2', 'router_b2', 'expert_w1', 'expert_b1', 'expert_w2', 'expert_b2', 'expert_w3', 'expert_b3')}
    del _L3_ffn_all
    return {'x': x, 'adj': adj, 'nodemask': nodemask, 'L0_gnn_W': _L0_gnn_in['W'], 'L0_gnn_b': _L0_gnn_in['b'], 'L0_gnn_alpha': _L0_gnn_in['alpha'], 'L0_ffn_Wr': _L0_ffn_in['Wr'], 'L0_ffn_W1s': _L0_ffn_in['W1s'], 'L0_ffn_b1s': _L0_ffn_in['b1s'], 'L0_ffn_W2s': _L0_ffn_in['W2s'], 'L0_ffn_b2s': _L0_ffn_in['b2s'], 'L0_ffn_W1p': _L0_ffn_in['W1p'], 'L0_ffn_b1p': _L0_ffn_in['b1p'], 'L0_ffn_W2p': _L0_ffn_in['W2p'], 'L0_ffn_b2p': _L0_ffn_in['b2p'], 'L1_gnn_Wq': _L1_gnn_in['Wq'], 'L1_gnn_bq': _L1_gnn_in['bq'], 'L1_gnn_Wk': _L1_gnn_in['Wk'], 'L1_gnn_bk': _L1_gnn_in['bk'], 'L1_gnn_Wv': _L1_gnn_in['Wv'], 'L1_gnn_bv': _L1_gnn_in['bv'], 'L1_gnn_Wo': _L1_gnn_in['Wo'], 'L1_gnn_bo': _L1_gnn_in['bo'], 'L1_ffn_Wr': _L1_ffn_in['Wr'], 'L1_ffn_br': _L1_ffn_in['br'], 'L1_ffn_W1': _L1_ffn_in['W1'], 'L1_ffn_b1': _L1_ffn_in['b1'], 'L1_ffn_W2': _L1_ffn_in['W2'], 'L1_ffn_b2': _L1_ffn_in['b2'], 'L1_ffn_gamma': _L1_ffn_in['gamma'], 'L1_ffn_beta': _L1_ffn_in['beta'], 'L2_gnn_W_a': _L2_gnn_in['W_a'], 'L2_gnn_bias': _L2_gnn_in['bias'], 'L2_ffn_hl_w': _L2_ffn_in['hl_w'], 'L2_ffn_hl_b': _L2_ffn_in['hl_b'], 'L2_ffn_wq': _L2_ffn_in['wq'], 'L2_ffn_wk': _L2_ffn_in['wk'], 'L2_ffn_wv': _L2_ffn_in['wv'], 'L2_ffn_gate_w': _L2_ffn_in['gate_w'], 'L2_ffn_gate_b': _L2_ffn_in['gate_b'], 'L2_ffn_ln_g': _L2_ffn_in['ln_g'], 'L2_ffn_ln_b': _L2_ffn_in['ln_b'], 'L2_ffn_fc1_w': _L2_ffn_in['fc1_w'], 'L2_ffn_fc1_b': _L2_ffn_in['fc1_b'], 'L2_ffn_fc2_w': _L2_ffn_in['fc2_w'], 'L2_ffn_fc2_b': _L2_ffn_in['fc2_b'], 'L2_ffn_fnorm_g': _L2_ffn_in['fnorm_g'], 'L2_ffn_fnorm_b': _L2_ffn_in['fnorm_b'], 'L2_ffn_fgate_w': _L2_ffn_in['fgate_w'], 'L3_gnn_W': _L3_gnn_in['W'], 'L3_ffn_router_w1': _L3_ffn_in['router_w1'], 'L3_ffn_router_b1': _L3_ffn_in['router_b1'], 'L3_ffn_router_w2': _L3_ffn_in['router_w2'], 'L3_ffn_router_b2': _L3_ffn_in['router_b2'], 'L3_ffn_expert_w1': _L3_ffn_in['expert_w1'], 'L3_ffn_expert_b1': _L3_ffn_in['expert_b1'], 'L3_ffn_expert_w2': _L3_ffn_in['expert_w2'], 'L3_ffn_expert_b2': _L3_ffn_in['expert_b2'], 'L3_ffn_expert_w3': _L3_ffn_in['expert_w3'], 'L3_ffn_expert_b3': _L3_ffn_in['expert_b3']}

def reference(x, adj, nodemask, L0_gnn_W, L0_gnn_b, L0_gnn_alpha, L0_ffn_Wr, L0_ffn_W1s, L0_ffn_b1s, L0_ffn_W2s, L0_ffn_b2s, L0_ffn_W1p, L0_ffn_b1p, L0_ffn_W2p, L0_ffn_b2p, L1_gnn_Wq, L1_gnn_bq, L1_gnn_Wk, L1_gnn_bk, L1_gnn_Wv, L1_gnn_bv, L1_gnn_Wo, L1_gnn_bo, L1_ffn_Wr, L1_ffn_br, L1_ffn_W1, L1_ffn_b1, L1_ffn_W2, L1_ffn_b2, L1_ffn_gamma, L1_ffn_beta, L2_gnn_W_a, L2_gnn_bias, L2_ffn_hl_w, L2_ffn_hl_b, L2_ffn_wq, L2_ffn_wk, L2_ffn_wv, L2_ffn_gate_w, L2_ffn_gate_b, L2_ffn_ln_g, L2_ffn_ln_b, L2_ffn_fc1_w, L2_ffn_fc1_b, L2_ffn_fc2_w, L2_ffn_fc2_b, L2_ffn_fnorm_g, L2_ffn_fnorm_b, L2_ffn_fgate_w, L3_gnn_W, L3_ffn_router_w1, L3_ffn_router_b1, L3_ffn_router_w2, L3_ffn_router_b2, L3_ffn_expert_w1, L3_ffn_expert_b1, L3_ffn_expert_w2, L3_ffn_expert_b2, L3_ffn_expert_w3, L3_ffn_expert_b3):
    import jax
    import jax.numpy as jnp

    def _L0_gnn_ref(x, adjacency_matrix, W, b, alpha):
        import jax, jax.numpy as jnp
        import numpy as np
        MIN_VALUE = 1e-10
        deg = adjacency_matrix.sum(axis=-1)
        deg = jnp.where(deg != 0, deg, 1.0)
        d_inv_sqrt = deg ** (-0.5)
        norm_adj = d_inv_sqrt[:, :, None] * adjacency_matrix * d_inv_sqrt[:, None, :]
        alpha_eff = jnp.maximum(alpha[0], MIN_VALUE)
        N = adjacency_matrix.shape[1]
        a_plus = norm_adj + alpha_eff * jnp.eye(N, dtype=adjacency_matrix.dtype)
        h = jnp.einsum('bnm,bmf->bnf', a_plus, x)
        return jnp.einsum('bnf,pf->bnp', h, W) + b

    def _L0_ffn_ref(x, Wr, W1s, b1s, W2s, b2s, W1p, b1p, W2p, b2p):
        import jax, jax.numpy as jnp
        import numpy as np
        B, S, D, F, E, K = (8, 1024, 128, 512, 8, 2)
        gelu = lambda t: jax.nn.gelu(t, approximate=False)
        shared = gelu(x @ W1s + b1s) @ W2s + b2s
        rw = jax.nn.softmax(x @ Wr, axis=-1)
        topw, topi = jax.lax.top_k(rw, K)
        topw = topw / jnp.sum(topw, axis=-1, keepdims=True)
        mask = jnp.sum(jax.nn.one_hot(topi, E, dtype=topw.dtype) * topw[..., None], axis=-2)
        h = gelu(jnp.einsum('bsd,edf->bsef', x, W1p) + b1p)
        priv = jnp.einsum('bsef,efd->bsed', h, W2p) + b2p
        routed = jnp.einsum('bsed,bse->bsd', priv, mask)
        return shared + routed

    def _L1_gnn_ref(x, adj, Wq, bq, Wk, bk, Wv, bv, Wo, bo):
        import jax, jax.numpy as jnp
        import numpy as np
        B, N = (1, 2048)
        D_IN, D_OUT, H = (128, 128, 8)
        HD = D_OUT // H
        NEG = -9000000000000000.0

        def _xavier(key, shape):
            lim = np.sqrt(6.0 / (shape[0] + shape[1])).astype(np.float32)
            return jax.random.uniform(key, shape, jnp.float32, -lim, lim)
        b, n, _ = x.shape

        def split_heads(t):
            return t.reshape(b, n, H, HD).transpose(0, 2, 1, 3)
        q = split_heads(x @ Wq + bq)
        k = split_heads(x @ Wk + bk)
        v = split_heads(x @ Wv + bv)
        scores = jnp.einsum('bhqd,bhkd->bhqk', q, k) / np.float32(np.sqrt(HD))
        scores = jnp.where(adj[:, None, :, :] > 0, scores, jnp.float32(NEG))
        attn = jax.nn.softmax(scores, axis=-1)
        out = jnp.einsum('bhqk,bhkd->bhqd', attn, v)
        out = out.transpose(0, 2, 1, 3).reshape(b, n, D_OUT)
        return out @ Wo + bo

    def _L1_ffn_ref(x, Wr, br, W1, b1, W2, b2, gamma, beta):
        import math
        import jax, jax.numpy as jnp
        import numpy as np
        CAPACITY_FACTOR = 1.25
        TOP_K = 2
        LN_EPS = 1e-05

        def _layer_norm(x, gamma, beta):
            mu = jnp.mean(x, axis=-1, keepdims=True)
            var = jnp.var(x, axis=-1, keepdims=True)
            return (x - mu) * jax.lax.rsqrt(var + LN_EPS) * gamma + beta
        B, S, D = x.shape
        E = Wr.shape[1]
        N = B * S
        K = TOP_K
        logits = jnp.mean(x, axis=1) @ Wr + br
        routing_weights = jax.nn.softmax(logits, axis=-1)
        capacity = float(math.ceil(N * CAPACITY_FACTOR / E))
        expected_loads = routing_weights.sum(axis=0) * (N / B)
        scale = jnp.where(expected_loads > capacity, capacity / expected_loads, 1.0)
        routing_weights = jax.nn.softmax(routing_weights * scale, axis=-1)
        rw_tok = jnp.broadcast_to(routing_weights[:, None, :], (B, S, E)).reshape(N, E)
        top_w, top_i = jax.lax.top_k(rw_tok, K)
        top_w = jax.nn.softmax(top_w, axis=-1)
        xf = x.reshape(N, D)
        h = jax.nn.gelu(jnp.einsum('nd,edf->enf', xf, W1) + b1[:, None, :], approximate=False)
        y = jnp.einsum('enf,efd->end', h, W2) + b2[:, None, :]
        w_dense = jnp.zeros((N, E), x.dtype).at[jnp.arange(N)[:, None], top_i].add(top_w)
        out = jnp.einsum('ne,end->nd', w_dense, y).reshape(B, S, D)
        out = _layer_norm(out + x, gamma, beta)
        return out

    def _L2_gnn_ref(x, adj, W_a, bias):
        import jax, jax.numpy as jnp
        import numpy as np
        NEG_SLOPE = -0.2
        MASK_VAL = -9000000000000000.0
        Xp = jnp.einsum('bnf,fo->bno', x, W_a)
        A = jnp.einsum('bno,bmo->bnm', Xp, Xp)
        mag = jnp.linalg.norm(A, axis=2, keepdims=True)
        A = A / (mag * jnp.swapaxes(mag, 1, 2))
        e = jnp.where(A >= 0, A, NEG_SLOPE * A)
        att = jnp.where(adj > 0, e, MASK_VAL)
        att = jax.nn.softmax(att, axis=2)
        h = jnp.einsum('bnm,bmf->bnf', att, x) + bias
        return jax.nn.elu(h)

    def _L2_ffn_ref(x, hl_w, hl_b, wq, wk, wv, gate_w, gate_b, ln_g, ln_b, fc1_w, fc1_b, fc2_w, fc2_b, fnorm_g, fnorm_b, fgate_w):
        import jax, jax.numpy as jnp
        import numpy as np
        B, S, H, NH, NE = (4, 512, 128, 4, 4)
        D = H // NH
        EPS = 1e-08

        def layernorm(x, g, b):
            m = jnp.mean(x, axis=-1, keepdims=True)
            v = jnp.mean((x - m) ** 2, axis=-1, keepdims=True)
            return (x - m) / jnp.sqrt(v + EPS) * g + b
        b, s, h = x.shape
        nh, d, _ = wk.shape
        ne = wq.shape[1]
        sx = jnp.einsum('bsh,ndh->bnsd', x, hl_w) + hl_b[None, :, None, :]
        pad = sx == 0
        q = jnp.einsum('bnsd,neod->bneso', sx, wq)
        k = jnp.einsum('bnsd,nod->bnso', sx, wk)
        v = jnp.einsum('bnsd,nod->bnso', sx, wv)
        causal = jnp.where(jnp.tril(jnp.ones((s, s), bool)), 0.0, -jnp.inf).astype(x.dtype)
        scores = jnp.einsum('bnesd,bntd->bnest', q, k) * d ** 0.5 + causal
        att = jax.nn.softmax(scores, axis=-1)
        qkv = jnp.einsum('bnest,bntd->bnesd', att, v)
        qkv = jnp.where(pad[:, :, None], 0.0, qkv)
        out = jnp.transpose(qkv, (0, 1, 3, 2, 4)).reshape(b, nh, s, ne * d)
        gs = jax.nn.softmax(jnp.einsum('bnsf,nef->bnse', out, gate_w) + gate_b[None, :, None, :], axis=-1)
        mixed = jnp.einsum('bnsed,bnse->bnsd', out.reshape(b, nh, s, ne, d), gs)
        resid = sx[jnp.arange(nh), jnp.arange(nh)]
        hn = layernorm(mixed + resid, ln_g, ln_b)
        f_n = jnp.transpose(hn, (0, 2, 1, 3)).reshape(b, s, h)
        fx = f_n.reshape(b, s, nh, d)
        pm = fx == 0
        hx = jnp.where(pm, 0.0, fx @ fc1_w.T + fc1_b)
        hx = jax.nn.relu(hx)
        hx = jnp.where(pm, 0.0, hx @ fc2_w.T + fc2_b)
        hx = layernorm(hx + fx, fnorm_g, fnorm_b)
        fout = hx.reshape(b, s, h)
        fg = jax.nn.softmax(fout @ fgate_w.T, axis=-1)
        return (fout.reshape(b, s, nh, d) * fg[..., None]).reshape(b, s, h)

    def _L3_gnn_ref(matrix, mask, adj, W):
        import jax, jax.numpy as jnp
        import numpy as np
        HIDDEN = 128
        NEG_INF = -1e+30
        intermediate = jnp.einsum('bsh,hd->bsd', matrix, W)
        similarities = jnp.einsum('bsd,btd->bst', intermediate, matrix)
        similarities = similarities * adj
        key_mask = mask[:, None, :].astype(bool)
        masked = jnp.where(key_mask, similarities, NEG_INF)
        attn = jax.nn.softmax(masked, axis=-1)
        output = jnp.einsum('bst,bth->bsh', attn, matrix)
        return output

    def _L3_ffn_ref(features, router_w1, router_b1, router_w2, router_b2, expert_w1, expert_b1, expert_w2, expert_b2, expert_w3, expert_b3):
        import jax, jax.numpy as jnp
        import numpy as np
        E, D, H, TOP_K = (6, 128, 128, 2)
        ROUTER_H = D // 2
        rh = jax.nn.relu(features @ router_w1 + router_b1)
        expert_logits = jax.nn.softmax(rh @ router_w2 + router_b2, axis=-1)
        top_w, top_i = jax.lax.top_k(expert_logits, TOP_K)
        routing_weights = jax.nn.softmax(top_w, axis=-1)
        h1 = jax.nn.relu(jnp.einsum('bsd,edh->bseh', features, expert_w1) + expert_b1)
        h2 = jax.nn.relu(jnp.einsum('bseh,ehf->bsef', h1, expert_w2) + expert_b2)
        expert_out = jnp.einsum('bsef,efo->bseo', h2, expert_w3) + expert_b3
        sel = jnp.take_along_axis(expert_out, top_i[:, :, :, None], axis=2)
        combined = jnp.sum(sel * routing_weights[..., None], axis=2)
        return combined
    x = x + _L0_gnn_ref(_layernorm(x, axis=-1), adj, L0_gnn_W, L0_gnn_b, L0_gnn_alpha)
    x = x + _L0_ffn_ref(_layernorm(x, axis=-1), L0_ffn_Wr, L0_ffn_W1s, L0_ffn_b1s, L0_ffn_W2s, L0_ffn_b2s, L0_ffn_W1p, L0_ffn_b1p, L0_ffn_W2p, L0_ffn_b2p)
    x = x + _L1_gnn_ref(_layernorm(x, axis=-1), adj, L1_gnn_Wq, L1_gnn_bq, L1_gnn_Wk, L1_gnn_bk, L1_gnn_Wv, L1_gnn_bv, L1_gnn_Wo, L1_gnn_bo)
    x = x + _L1_ffn_ref(_layernorm(x, axis=-1), L1_ffn_Wr, L1_ffn_br, L1_ffn_W1, L1_ffn_b1, L1_ffn_W2, L1_ffn_b2, L1_ffn_gamma, L1_ffn_beta)
    x = x + _L2_gnn_ref(_layernorm(x, axis=-1), adj, L2_gnn_W_a, L2_gnn_bias)
    x = x + _L2_ffn_ref(_layernorm(x, axis=-1), L2_ffn_hl_w, L2_ffn_hl_b, L2_ffn_wq, L2_ffn_wk, L2_ffn_wv, L2_ffn_gate_w, L2_ffn_gate_b, L2_ffn_ln_g, L2_ffn_ln_b, L2_ffn_fc1_w, L2_ffn_fc1_b, L2_ffn_fc2_w, L2_ffn_fc2_b, L2_ffn_fnorm_g, L2_ffn_fnorm_b, L2_ffn_fgate_w)
    x = x + _L3_gnn_ref(_layernorm(x, axis=-1), nodemask, adj, L3_gnn_W)
    x = x + _L3_ffn_ref(_layernorm(x, axis=-1), L3_ffn_router_w1, L3_ffn_router_b1, L3_ffn_router_w2, L3_ffn_router_b2, L3_ffn_expert_w1, L3_ffn_expert_b1, L3_ffn_expert_w2, L3_ffn_expert_b2, L3_ffn_expert_w3, L3_ffn_expert_b3)
    return x

_drawn_inputs = setup_inputs


def setup_inputs(seed=0):
    import zlib

    import numpy as np

    out = dict(_drawn_inputs(seed))
    spreads = {'L0_ffn_b1s': (0.0, 0.1),
     'L0_ffn_b2s': (0.0, 0.1),
     'L0_ffn_b1p': (0.0, 0.335),
     'L0_ffn_b2p': (0.0, 0.1),
     'L1_gnn_bq': (0.0, 0.1),
     'L1_gnn_bk': (0.0, 2.0),
     'L1_gnn_bv': (0.0, 0.1),
     'L1_gnn_bo': (0.0, 0.1),
     'L1_ffn_br': (0.0, 0.1),
     'L1_ffn_b1': (0.0, 0.274),
     'L1_ffn_b2': (0.0, 0.1),
     'L1_ffn_gamma': (1.0, 0.2),
     'L1_ffn_beta': (0.0, 0.1),
     'L2_ffn_ln_g': (1.0, 0.593),
     'L2_ffn_ln_b': (0.0, 0.614),
     'L2_ffn_fnorm_g': (1.0, 0.6),
     'L2_ffn_fnorm_b': (0.0, 0.581),
     'L3_ffn_router_b1': (0.0, 0.563),
     'L3_ffn_router_b2': (0.0, 0.456),
     'L3_ffn_expert_b1': (0.0, 0.8),
     'L3_ffn_expert_b2': (0.0, 0.796),
     'L3_ffn_expert_b3': (0.0, 0.331)}
    factors = {'L2_gnn_W_a': 200.0,
     'L2_ffn_hl_b': 3.478,
     'L2_ffn_wq': 8.0,
     'L2_ffn_wk': 8.0,
     'L2_ffn_wv': 4.068,
     'L2_ffn_gate_w': 8.0,
     'L2_ffn_gate_b': 8.0,
     'L2_ffn_fc1_w': 8.0,
     'L2_ffn_fc1_b': 8.0,
     'L2_ffn_fc2_w': 7.807,
     'L2_ffn_fc2_b': 7.586,
     'L3_ffn_expert_w1': 3.214,
     'L3_ffn_expert_w2': 2.737}
    for name, (base, spread) in spreads.items():
        noise = np.random.default_rng([zlib.crc32(name.encode()), seed]).standard_normal(out[name].shape)
        drawn = base * np.exp(spread * noise) if base else spread * noise
        out[name] = jnp.asarray(drawn.astype(out[name].dtype))
    for name, factor in factors.items():
        out[name] = (out[name] * factor).astype(out[name].dtype)
    return out
```

```python
from contextlib import ExitStack

import numpy as np
import concourse.bass as bass
from concourse import mybir

F32 = mybir.dt.float32
I32 = mybir.dt.int32
U32 = mybir.dt.uint32
ALU = mybir.AluOpType
ACT = mybir.ActivationFunctionType
AX = mybir.AxisListType
P = 128
D = 128
B, N = 32, 256
TILES = B * N // P
GT = 4
GROUPS = TILES // GT
GW = GT * D
LN_EPS = 1e-5


def span(g, width, start=0, size=None):
    return bass.ds(g * width + start, width if size is None else size)


def named_semaphores(nc, stack, phase, names):
    handles = {n: stack.enter_context(nc.semaphore(f"{phase}_{n}")) for n in names.split()}
    stack.callback(zero_semaphores, nc, list(handles.values()))
    return handles


def zero_semaphores(nc, handles):
    with nc.Block() as block:
        @block.gpsimd
        def _(e):
            for h in handles:
                e.sem_clear(h)


NORM_SEMS = "stats_done var_ready veps_ready rstd_ready xn_ready xt_psum xt_ready"
DONE_SEMS = "pe_done act_done dve_done pool_done"


def give_credits(e, done):
    e.sem_inc(done, 2)


def wait_groups_before(e, g, *dones):
    for d in dones:
        e.wait_ge(d, g + 1)


def wait_apart(e, w, semaphore, value):
    e.wait_ge(semaphore, value)
    e.sem_inc(w.passed, 1)


class Resident:

    def __init__(self, nc, c):
        def sb(n, shape):
            return c.enter_context(nc.sbuf_tensor(n, shape, F32))
        self.passed = c.enter_context(nc.semaphore("passed"))
        self.stored = c.enter_context(nc.semaphore("stored"))
        self.scratch_stored = c.enter_context(nc.semaphore("scratch_stored"))
        self.x = sb("x", [P, TILES * D])
        self.adj = sb("adj", [P, TILES * N])
        self.xn = sb("xn", [P, 2, GT, D])
        self.xt = sb("xt", [P, 2, GW])
        self.stats = sb("stats", [P, 2, GT, 6])
        self.meanvar = sb("meanvar", [P, 2, GT, 2])
        self.veps = sb("veps", [P, 2, GT])
        self.rstd = sb("rstd", [P, 2, GT])
        self.ident = sb("ident", [P, P])
        self.ones = sb("ones", [P, P])
        self.minus_half = sb("minus_half", [P, 64])
        self.ln_eps = sb("ln_eps", [P, 16])


def norm_stats(e, s, w, g, p):
    for t in range(GT):
        last = e.bn_stats(w.stats[:, p, t, :], w.x[:, span(g, GW, t * D, D)])
    last.then_inc(s["stats_done"], 1)
    wait_apart(e, w, s["stats_done"], g + 1)
    for t in range(GT):
        last = e.bn_aggr(w.meanvar[:, p, t, :], w.stats[:, p, t, :])
    last.then_inc(s["var_ready"], 1)


def norm_rstd(e, s, w, g, p):
    e.wait_ge(s["var_ready"], g + 1)
    e.tensor_tensor(w.veps[:, p, :], w.meanvar[:, p, :, 1], w.ln_eps[:, 0:GT], ALU.add).then_inc(s["veps_ready"], 1)
    e.wait_ge(s["veps_ready"], g + 1)
    e.tensor_tensor(w.rstd[:, p, :], w.veps[:, p, :], w.minus_half[:, 0:GT], ALU.pow).then_inc(s["rstd_ready"], 1)


def norm_apply(e, s, w, g, p):
    e.wait_ge(s["rstd_ready"], g + 1)
    for t in range(GT):
        last = e.tensor_scalar(w.xn[:, p, t, :], w.x[:, span(g, GW, t * D, D)], w.meanvar[:, p, t, 0:1],
                               w.rstd[:, p, t:t + 1], ALU.subtract, ALU.mult)
    last.then_inc(s["xn_ready"], 1)


def norm_transpose(e, s, w, g, p, out):
    e.wait_ge(s["xn_ready"], g + 1)
    for t in range(GT):
        last = e.transpose(out[:, t * P:(t + 1) * P], w.xn[:, p, t, :], w.ident[:, :])
    last.then_inc(s["xt_psum"], 1)


def norm_copy(e, s, w, g, p, src):
    e.wait_ge(s["xt_psum"], g + 1)
    e.activation(w.xt[:, p, :], src, ACT.Copy).then_inc(s["xt_ready"], 1)


def over_groups(e, body):
    with e.Fori(0, GROUPS - 2, 2) as i:
        body(i, 0, True)
        body(i + 1, 1, True)
    body(GROUPS - 2, 0, True)
    body(GROUPS - 1, 1, False)
NEG_MASK = 9e15
KEY_MASK = 1e30
BIG = 3e38


def constants(nc, w):
    with ExitStack() as c:
        s = named_semaphores(nc, c, "const", "ones zero ident")
        with nc.Block() as block:
            @block.gpsimd
            def _(e):
                e.memset(w.ident[:, :], 0.0).then_inc(s["zero"], 1)
                e.memset(w.ones[:, :], 1.0).then_inc(s["ones"], 1)
                e.memset(w.minus_half[:, :], -0.5).then_inc(s["ones"], 1)
                e.memset(w.ln_eps[:, :], LN_EPS).then_inc(s["ones"], 1)
                e.wait_ge(s["zero"], 1)
                e.affine_select(out=w.ident[:, :], in_=w.ident[:, :], compare_op=ALU.not_equal, fill=1.0,
                                base=0, pattern=[[-1, P]], channel_multiplier=1).then_inc(s["ident"], 1)
                e.wait_ge(s["ident"], 1)
                e.wait_ge(s["ones"], 3)

def l0_gnn(nc, w, a):
    with ExitStack() as c:
        sb = lambda n, shape: c.enter_context(nc.sbuf_tensor("l0g_" + n, shape, F32))
        ps = lambda n, shape: c.enter_context(nc.psum_tensor("l0g_" + n, shape, F32))
        adj_t = sb("adj_t", [P, 2, 2, 2, N])
        deg_is0 = sb("deg_is0", [P, 2, GT])
        deg = sb("deg", [P, 2, GT])
        dinv = sb("dinv", [P, 2, GT])
        alpha_deg = sb("alpha_deg", [P, 2, GT])
        alpha = sb("alpha", [P, 1])
        alpha_eff = sb("alpha_eff", [P, 1])
        w_t = sb("w_t", [D, D])
        bias = sb("bias", [P, D])
        xd = sb("xd", [P, 2, GT, D])
        xb = sb("xb", [P, 2, GT, D])
        h_t = sb("h_t", [P, 2, GW])
        ps_t = ps("ps_t", [P, 2, 512])
        ps_deg = ps("ps_deg", [P, 2, 512])
        ps_h = ps("ps_h", [P, 2, 512])
        ps_y = ps("ps_y", [P, 2, 512])
        s = named_semaphores(nc, c, "l0g", NORM_SEMS + " " + DONE_SEMS + " weights alpha loaded0 loaded1 deg_psum is0 deg_ready"
                             " dinv_ready alpha_deg_ready xd_ready xb_ready h_psum h_ready y_psum")
        loaded = [s["loaded0"], s["loaded1"]]
        x_dram = a["x"].rearrange("b (h p) d -> p (b h) d", p=P)
        adj_dram = a["adj"].rearrange("b (h p) m -> p (b h) m", p=P)
        adj_t_dram = a["adj_t"].rearrange("b (h p) n -> p b h n", p=P)
        with nc.Block() as block:
            @block.sync
            def _(e):
                e.dma_start(w_t[:, :], a["L0_gnn_Wt"]).then_inc(s["weights"], 16)
                e.dma_start(bias[:, :], a["L0_gnn_b"].partition_broadcast(P)).then_inc(s["weights"], 16)
                e.dma_start(alpha[:, :], a["L0_gnn_alpha"].partition_broadcast(P)).then_inc(s["weights"], 16)

                def body(g, p, has_next):
                    wait_groups_before(e, g, s["pe_done"], s["dve_done"])
                    e.dma_start(w.x[:, span(g, GW)].rearrange("p (t d) -> p t d", d=D),
                                x_dram[:, bass.ds(g * GT, GT), :]).then_inc(loaded[p], 16)
                    e.dma_start(adj_t[:, p], adj_t_dram[:, bass.ds(g * 2, 2)]).then_inc(loaded[p], 16)
                    e.dma_start(w.adj[:, span(g, GT * N)].rearrange("p (t m) -> p t m", m=N),
                                adj_dram[:, bass.ds(g * GT, GT), :]).then_inc(loaded[p], 16)
                over_groups(e, body)

            def wait_loaded(e, g, p):
                e.wait_ge(loaded[p], g * 24 + (48 if p == 0 else 24))

            @block.vector
            def _(e):
                give_credits(e, s["dve_done"])
                e.wait_ge(s["weights"], 48)
                e.tensor_scalar(alpha_eff[:, :], alpha[:, :], 1e-10, None, ALU.max).then_inc(s["alpha"], 1)
                e.wait_ge(s["alpha"], 1)

                def stats(g, p):
                    wait_loaded(e, g, p)
                    wait_groups_before(e, g, s["pool_done"])
                    norm_stats(e, s, w, g, p)

                def body(g, p, has_next):
                    e.wait_ge(s["deg_psum"], g + 1)
                    e.tensor_scalar(deg_is0[:, p, :], ps_deg[:, p, 0:GT], 0.0, None, ALU.is_equal).then_inc(s["is0"], 1)
                    e.wait_ge(s["is0"], g + 1)
                    e.tensor_tensor(deg[:, p, :], ps_deg[:, p, 0:GT], deg_is0[:, p, :], ALU.add).then_inc(s["deg_ready"], 1)
                    e.wait_ge(s["deg_ready"], g + 1)
                    e.tensor_scalar(alpha_deg[:, p, :], deg[:, p, :], alpha_eff[:, 0:1], None, ALU.mult).then_inc(s["alpha_deg_ready"], 1)
                    e.wait_ge(s["alpha_deg_ready"], g + 1)
                    for t in range(GT):
                        diag = adj_t[:, p, t // 2, t % 2, (t % 2) * P:(t % 2 + 1) * P]
                        e.scalar_tensor_tensor(diag, w.ident[:, :], alpha_deg[:, p, t:t + 1], diag, ALU.mult, ALU.add)
                    e.wait_ge(s["dinv_ready"], g + 1)
                    for t in range(GT):
                        last = e.tensor_scalar(xd[:, p, t, :], w.xn[:, p, t, :], dinv[:, p, t:t + 1], None, ALU.mult)
                    last.then_inc(s["xd_ready"], 1)
                    if has_next:
                        stats(g + 1, 1 - p)
                    e.wait_ge(s["xb_ready"], g + 1)
                    e.wait_ge(s["y_psum"], g + 1)
                    for t in range(GT):
                        last = e.scalar_tensor_tensor(w.x[:, span(g, GW, t * D, D)], ps_y[:, p, t * D:(t + 1) * D],
                                                      dinv[:, p, t:t + 1], xb[:, p, t, :], ALU.mult, ALU.add)
                    last.then_inc(s["dve_done"], 1)
                    if has_next:
                        wait_groups_before(e, g + 1, s["pe_done"], s["pool_done"])
                        norm_apply(e, s, w, g + 1, 1 - p)
                stats(0, 0)
                norm_apply(e, s, w, 0, 0)
                over_groups(e, body)

            @block.gpsimd
            def _(e):
                give_credits(e, s["pool_done"])
                e.wait_ge(s["weights"], 48)

                def body(g, p, has_next):
                    e.wait_ge(s["xn_ready"], g + 1)
                    for t in range(GT):
                        last = e.tensor_tensor(xb[:, p, t, :], w.x[:, span(g, GW, t * D, D)], bias[:, :], ALU.add)
                    last.then_inc(s["xb_ready"], 1)
                    e.wait_ge(s["deg_ready"], g + 1)
                    e.tensor_tensor(dinv[:, p, :], deg[:, p, :], w.minus_half[:, 0:GT], ALU.pow).then_inc(s["dinv_ready"], 1)
                    if has_next:
                        wait_groups_before(e, g + 1, s["dve_done"])
                        norm_rstd(e, s, w, g + 1, 1 - p)
                    e.drain().then_inc(s["pool_done"], 1)
                norm_rstd(e, s, w, 0, 0)
                over_groups(e, body)

            @block.tensor
            def _(e):
                give_credits(e, s["pe_done"])
                e.wait_ge(s["weights"], 48)

                def body(g, p, has_next):
                    wait_groups_before(e, g, s["dve_done"], s["act_done"])
                    wait_loaded(e, g, p)
                    for t in range(GT):
                        for m in range(2):
                            last = e.matmul(ps_deg[:, p, t:t + 1], adj_t[:, p, t // 2, m, (t % 2) * P:(t % 2 + 1) * P],
                                            w.ones[:, 0:1], start=m == 0, stop=m == 1)
                    last.then_inc(s["deg_psum"], 1)
                    e.wait_ge(s["xd_ready"], g + 1)
                    for b in range(2):
                        for m in range(2):
                            last = e.matmul(ps_h[:, p, b * N:(b + 1) * N], xd[:, p, 2 * b + m, :], adj_t[:, p, b, m, :],
                                            start=m == 0, stop=m == 1)
                    last.then_inc(s["h_psum"], 1)
                    e.wait_ge(s["h_ready"], g + 1)
                    for t in range(GT):
                        last = e.matmul(ps_y[:, p, t * D:(t + 1) * D], h_t[:, p, t * P:(t + 1) * P], w_t[:, :],
                                        start=True, stop=True)
                    last.then_inc(s["y_psum"], 1)
                    e.drain().then_inc(s["pe_done"], 1)
                over_groups(e, body)

            @block.scalar
            def _(e):
                give_credits(e, s["act_done"])

                def body(g, p, has_next):
                    wait_groups_before(e, g, s["pe_done"])
                    e.wait_ge(s["h_psum"], g + 1)
                    e.activation(h_t[:, p, :], ps_h[:, p, :], ACT.Copy).then_inc(s["h_ready"], 1)
                    e.drain().then_inc(s["act_done"], 1)
                over_groups(e, body)


E0 = 8
EA = E0 + 1
F0 = 512
C0 = F0 // P


def l0_ffn(nc, w, a):
    with ExitStack() as c:
        sb = lambda n, shape, dt=F32: c.enter_context(nc.sbuf_tensor("l0f_" + n, shape, dt))
        ps = lambda n, shape: c.enter_context(nc.psum_tensor("l0f_" + n, shape, F32))
        w1 = sb("w1", [P, EA, F0])
        w2 = sb("w2", [P, EA, C0, D])
        b1 = sb("b1", [P, EA, C0])
        b2 = sb("b2", [EA, D])
        wr = sb("wr", [P, E0])
        iota = sb("iota", [P, E0])
        logits = sb("logits", [P, 2, GT, E0])
        row_max = sb("row_max", [P, 2, GT])
        expo = sb("expo", [P, 2, GT, E0])
        best = sb("best", [P, 2, GT, 8])
        best_at = sb("best_at", [P, 2, GT, 8], U32)
        best_f = sb("best_f", [P, 2, GT, 8])
        total = sb("total", [P, 2, GT])
        inv_total = sb("inv_total", [P, 2, GT])
        weight = sb("weight", [P, 2, GT, 2])
        hit = sb("hit", [P, 2, 2, GT, E0])
        mask = sb("mask", [P, 2, GT, EA])
        mask_t = sb("mask_t", [EA, 2, GW])
        h = sb("h", [P, 2, C0, GW])
        ps_h = ps("ps_h", [P, 4, 512])
        ps_y = ps("ps_y", [P, 2, 512])
        ps_t = ps("ps_t", [P, 512])
        ps_m = ps("ps_m", [P, 512])
        s = named_semaphores(nc, c, "l0f", NORM_SEMS + " " + DONE_SEMS + " weights const iota_ready mask_ones logit_psum max_ready logit_ready exp_ready"
                             " chain mask_ready mask_psum mask_t_ready bias_psum bias_added h_psum h_ready y_psum y_added")
        HC = EA * C0
        with nc.Block() as block:
            @block.sync
            def _(e):
                e.dma_start(wr[:, :], a["L0_ffn_Wr"]).then_inc(s["weights"], 16)
                e.dma_start(b1[:, :, :], a["L0_ffn_b1"]).then_inc(s["weights"], 16)
                e.dma_start(b2[0:E0, :], a["L0_ffn_b2p"]).then_inc(s["weights"], 16)
                e.dma_start(b2[E0:EA, :], a["L0_ffn_b2s"].rearrange("(a d) -> a d", a=1)).then_inc(s["weights"], 16)
                e.dma_start(w1[:, 0:E0, :], a["L0_ffn_W1p"].rearrange("e d f -> d e f")).then_inc(s["weights"], 16)
                e.dma_start(w1[:, E0, :], a["L0_ffn_W1s"]).then_inc(s["weights"], 16)
                e.dma_start(w2[:, 0:E0].rearrange("p e c d -> p (e c) d"),
                            a["L0_ffn_W2p"].rearrange("e (c p) d -> p (e c) d", p=P)).then_inc(s["weights"], 16)
                e.dma_start(w2[:, E0], a["L0_ffn_W2s"].rearrange("(c p) d -> p c d", p=P)).then_inc(s["weights"], 16)

            def route(e, g, p):
                n = 5
                at = g * n
                e.wait_ge(s["logit_psum"], g + 1)
                lg = ps_m[:, p * 64:p * 64 + GT * E0].rearrange("p (t e) -> p t e", e=E0)
                e.tensor_reduce(row_max[:, p, :], lg, AX.X, ALU.max).then_inc(s["max_ready"], 1)
                e.wait_ge(s["max_ready"], g + 1)
                e.tensor_tensor(logits[:, p], lg, row_max[:, p, :].unsqueeze(2).broadcast_to([P, GT, E0]),
                                ALU.subtract).then_inc(s["logit_ready"], 1)
                wait_apart(e, w, s["exp_ready"], g + 1)
                for t in range(GT):
                    last = e.max(best[:, p, t, :], expo[:, p, t, :])
                last.then_inc(s["chain"], 1)
                wait_apart(e, w, s["chain"], at + 1)
                for t in range(GT):
                    e.max_index(best_at[:, p, t, :], best[:, p, t, :], expo[:, p, t, :])
                e.tensor_tensor(total[:, p, :], best[:, p, :, 0], best[:, p, :, 1], ALU.add).then_inc(s["chain"], 1)
                e.wait_ge(s["chain"], at + 2)
                e.reciprocal(inv_total[:, p, :], total[:, p, :])
                e.tensor_copy(best_f[:, p], best_at[:, p]).then_inc(s["chain"], 1)
                e.wait_ge(s["chain"], at + 3)
                e.tensor_tensor(weight[:, p], best[:, p, :, 0:2], inv_total[:, p, :].unsqueeze(2).broadcast_to([P, GT, 2]),
                                ALU.mult).then_inc(s["chain"], 1)
                e.wait_ge(s["chain"], at + 4)
                for t in range(GT):
                    for k in range(2):
                        last = e.tensor_scalar(hit[:, p, k, t, :], iota[:, :], best_f[:, p, t, k:k + 1],
                                               weight[:, p, t, k:k + 1], ALU.is_equal, ALU.mult)
                last.then_inc(s["chain"], 1)
                e.wait_ge(s["chain"], at + 5)
                e.tensor_tensor(mask[:, p, :, 0:E0], hit[:, p, 0], hit[:, p, 1], ALU.add).then_inc(s["mask_ready"], 1)

            @block.vector
            def _(e):
                give_credits(e, s["dve_done"])
                e.sem_inc(s["y_added"], 2)
                e.wait_ge(s["const"], 1)

                def stats(g, p):
                    wait_groups_before(e, g, s["pool_done"])
                    norm_stats(e, s, w, g, p)

                def apply(g, p):
                    wait_groups_before(e, g, s["pe_done"])
                    norm_apply(e, s, w, g, p)

                def body(g, p, has_next):
                    e.wait_ge(s["bias_psum"], g + 1)
                    xg = w.x[:, span(g, GW)]
                    e.tensor_tensor(xg, xg, ps_t[:, :], ALU.add).then_inc(s["bias_added"], 1)
                    e.wait_ge(s["mask_ready"], g + 1)
                    e.wait_ge(s["bias_added"], g + 1)
                    for x in range(EA):
                        k = g * EA + x
                        q = (p + x) % 2
                        e.wait_ge(s["y_psum"], k + 3)
                        if x:
                            e.wait_ge(s["y_added"], k + 2)
                        for t in range(GT):
                            xt = w.x[:, span(g, GW, t * D, D)]
                            last = e.scalar_tensor_tensor(xt, ps_y[:, q, t * D:(t + 1) * D], mask[:, p, t, x:x + 1], xt,
                                                          ALU.mult, ALU.add)
                        last.then_inc(s["y_added"], 1)
                        if has_next and x == 0:
                            stats(g + 1, 1 - p)
                        if has_next and x == 1:
                            apply(g + 1, 1 - p)
                        if has_next and x == 4:
                            route(e, g + 1, 1 - p)
                    e.drain().then_inc(s["dve_done"], 1)
                stats(0, 0)
                apply(0, 0)
                route(e, 0, 0)
                over_groups(e, body)

            @block.gpsimd
            def _(e):
                give_credits(e, s["pool_done"])
                e.iota(iota[:, :], pattern=[[1, E0]], base=0, channel_multiplier=0, allow_small_or_imprecise_dtypes=True).then_inc(s["iota_ready"], 1)
                e.memset(mask[:, :, :, :], 1.0).then_inc(s["mask_ones"], 1)
                e.wait_ge(s["iota_ready"], 1)
                e.wait_ge(s["mask_ones"], 1)
                e.sem_inc(s["const"], 1)

                def body(g, p, has_next):
                    if has_next:
                        wait_groups_before(e, g + 1, s["dve_done"])
                        norm_rstd(e, s, w, g + 1, 1 - p)
                    e.drain().then_inc(s["pool_done"], 1)
                norm_rstd(e, s, w, 0, 0)
                over_groups(e, body)

            @block.tensor
            def _(e):
                give_credits(e, s["pe_done"])
                e.sem_inc(s["y_psum"], 2)
                e.wait_ge(s["weights"], 128)

                def transposes(g, p):
                    e.wait_ge(s["bias_added"], g)
                    norm_transpose(e, s, w, g, p, ps_t)

                def logits_of(g, p):
                    e.wait_ge(s["xt_ready"], g + 1)
                    for t in range(GT):
                        last = e.matmul(ps_m[:, p * 64 + t * E0:p * 64 + (t + 1) * E0], w.xt[:, p, t * P:(t + 1) * P], wr[:, :],
                                        start=True, stop=True)
                    last.then_inc(s["logit_psum"], 1)

                def bias_of(g, p):
                    e.wait_ge(s["mask_ready"], g + 1)
                    e.wait_ge(s["xt_ready"], g + 1)
                    for t in range(GT):
                        last = e.transpose(ps_t[0:EA, t * P:(t + 1) * P], mask[:, p, t, :], w.ident[:, :])
                    last.then_inc(s["mask_psum"], 1)
                    e.wait_ge(s["mask_t_ready"], g + 1)
                    for t in range(GT):
                        last = e.matmul(ps_t[:, t * D:(t + 1) * D], mask_t[:, p, t * P:(t + 1) * P], b2[:, :], start=True, stop=True)
                    last.then_inc(s["bias_psum"], 1)

                def hidden(g, p, x):
                    for ch in range(C0):
                        n = g * HC + x * C0 + ch
                        e.wait_ge(s["h_ready"], n + 1)
                        e.matmul(ps_h[:, ch, :], w1[:, x, ch * P:(ch + 1) * P], w.xt[:, p, :],
                                 start=True, stop=True).then_inc(s["h_psum"], 1)

                def output(g, p, x):
                    k = g * EA + x
                    q = (p + x) % 2
                    e.wait_ge(s["y_added"], k + 1)
                    e.wait_ge(s["h_ready"], g * HC + x * C0 + C0 + 4)
                    for t in range(GT):
                        for ch in range(C0):
                            last = e.matmul(ps_y[:, q, t * D:(t + 1) * D], h[:, q, ch, t * P:(t + 1) * P], w2[:, x, ch, :],
                                            start=ch == 0, stop=ch == C0 - 1)
                    last.then_inc(s["y_psum"], 1)

                def body(g, p, has_next):
                    hidden(g, p, 0)
                    bias_of(g, p)
                    for x in range(EA):
                        if x + 1 < EA:
                            hidden(g, p, x + 1)
                        if has_next and x == 2:
                            transposes(g + 1, 1 - p)
                        if has_next and x == 3:
                            logits_of(g + 1, 1 - p)
                        output(g, p, x)
                    e.drain().then_inc(s["pe_done"], 1)
                norm_transpose(e, s, w, 0, 0, ps_t)
                logits_of(0, 0)
                over_groups(e, body)

            @block.scalar
            def _(e):
                give_credits(e, s["act_done"])
                e.sem_inc(s["h_ready"], 4)
                e.wait_ge(s["weights"], 128)

                def copy_xt(g, p):
                    norm_copy(e, s, w, g, p, ps_t[:, :])

                def exps(g, p):
                    e.wait_ge(s["logit_ready"], g + 1)
                    e.activation(expo[:, p], logits[:, p], ACT.Exp).then_inc(s["exp_ready"], 1)

                def body(g, p, has_next):
                    for x in range(EA):
                        q = (p + x) % 2
                        e.wait_ge(s["y_psum"], g * EA + x + 1)
                        for ch in range(C0):
                            e.wait_ge(s["h_psum"], g * HC + x * C0 + ch + 1)
                            e.activation(h[:, q, ch, :], ps_h[:, ch, :], ACT.Gelu, bias=b1[:, x, ch:ch + 1]).then_inc(s["h_ready"], 1)
                        if x == 0:
                            e.wait_ge(s["mask_psum"], g + 1)
                            e.activation(mask_t[:, p, :], ps_t[0:EA, :], ACT.Copy).then_inc(s["mask_t_ready"], 1)
                        if has_next and x == 3:
                            copy_xt(g + 1, 1 - p)
                        if has_next and x == 4:
                            exps(g + 1, 1 - p)
                    e.drain().then_inc(s["act_done"], 1)
                copy_xt(0, 0)
                exps(0, 0)
                over_groups(e, body)


H1 = 8
HD1 = D // H1
HALF = 4
U1 = GT * H1 // HALF


def l1_gnn(nc, w, a):
    with ExitStack() as c:
        sb = lambda n, shape, dt=F32: c.enter_context(nc.sbuf_tensor("l1g_" + n, shape, dt))
        ps = lambda n, shape: c.enter_context(nc.psum_tensor("l1g_" + n, shape, F32))
        wq = sb("wq", [P, D]); wk = sb("wk", [P, D]); wv = sb("wv", [P, D]); wo = sb("wo", [P, D])
        bq = sb("bq", [P, 1]); bk = sb("bk", [P, 1]); bq_scaled = sb("bq_scaled", [P, 1])
        bv = sb("bv", [P, D]); bo = sb("bo", [P, D])
        q_t = sb("q_t", [P, 2, GW])
        k_t = sb("k_t", [P, 2, GW])
        k_diag = sb("k_diag", [P, 2, 2, H1, N])
        v1 = sb("v1", [P, 2, GT, H1, HD1 + 1])
        not_adj = sb("not_adj", [P, 2, GT, N])
        scores = sb("scores", [P, 2, HALF, N])
        row_min = sb("row_min", [P, 2, HALF])
        probs = sb("probs", [P, 2, HALF, N])
        probs_t = sb("probs_t", [P, 2, 2, HALF, P])
        inv_sum = sb("inv_sum", [P, 2, H1])
        o = sb("o", [P, 2, GT, D])
        o_t = sb("o_t", [P, 2, GW])
        xb = sb("xb", [P, 2, GT, D])
        ps_s = ps("ps_s", [P, 2, HALF, N])
        ps_t = ps("ps_t", [P, 2, HALF, P])
        ps_o = ps("ps_o", [P, H1, HD1 + 1])
        ps_m = ps("ps_m", [P, 512])
        s = named_semaphores(nc, c, "l1g", NORM_SEMS + " " + DONE_SEMS + " weights const zeroed bq_scaled q_psum q_ready k_psum k_ready k_diag0 k_diag1"
                             " v_psum v_ready mask_ready s_psum masked exp_ready t_psum t_ready pv_psum inv_ready o_ready"
                             " ot_psum ot_ready y_psum xb_ready")
        k_loaded = [s["k_diag0"], s["k_diag1"]]
        with nc.Block() as block:
            @block.sync
            def _(e):
                for dst, src in ((wq, "Wq"), (wk, "Wk"), (wv, "Wv"), (wo, "Wo")):
                    e.dma_start(dst[:, :], a["L1_gnn_" + src]).then_inc(s["weights"], 16)
                for dst, src in ((bq, "bq"), (bk, "bk")):
                    e.dma_start(dst[:, :], a["L1_gnn_" + src].rearrange("(p a) -> p a", a=1)).then_inc(s["weights"], 16)
                for dst, src in ((bv, "bv"), (bo, "bo")):
                    e.dma_start(dst[:, :], a["L1_gnn_" + src].partition_broadcast(P)).then_inc(s["weights"], 16)
                e.wait_ge(s["zeroed"], 1)

                def diag(g, p):
                    wait_groups_before(e, g, s["pe_done"])
                    e.wait_ge(s["k_ready"], g + 1)
                    for hh in range(H1):
                        r = slice(hh * HD1, (hh + 1) * HD1)
                        e.dma_start(k_diag[r, p, :, hh, :], k_t[r, p, :].rearrange("p (b n) -> p b n", b=2)).then_inc(k_loaded[p], 16)

                def body(g, p, has_next):
                    if has_next:
                        diag(g + 1, 1 - p)
                diag(0, 0)
                over_groups(e, body)

            @block.gpsimd
            def _(e):
                give_credits(e, s["pool_done"])
                e.memset(k_diag[:, :, :, :, :], 0.0).then_inc(s["zeroed"], 1)
                e.memset(v1[:, :, :, :, HD1:HD1 + 1], 1.0).then_inc(s["const"], 1)
                e.wait_ge(s["weights"], 128)

                def body(g, p, has_next):
                    if has_next:
                        wait_groups_before(e, g + 1, s["dve_done"])
                        norm_rstd(e, s, w, g + 1, 1 - p)
                    wait_groups_before(e, g, s["dve_done"])
                    for t in range(GT):
                        last = e.tensor_tensor(xb[:, p, t, :], w.x[:, span(g, GW, t * D, D)], bo[:, :], ALU.add)
                    last.then_inc(s["xb_ready"], 1)
                    e.drain().then_inc(s["pool_done"], 1)
                norm_rstd(e, s, w, 0, 0)
                over_groups(e, body)

            @block.vector
            def _(e):
                give_credits(e, s["dve_done"])
                e.sem_inc(s["masked"], 2)
                e.sem_inc(s["t_ready"], 2)
                e.wait_ge(s["weights"], 128)
                e.wait_ge(s["const"], 1)
                e.tensor_scalar(bq_scaled[:, :], bq[:, :], -0.25, None, ALU.mult).then_inc(s["bq_scaled"], 1)

                def stats(g, p):
                    wait_groups_before(e, g, s["pool_done"])
                    norm_stats(e, s, w, g, p)

                def apply(g, p):
                    wait_groups_before(e, g, s["pe_done"])
                    norm_apply(e, s, w, g, p)

                def edges(g, p):
                    e.tensor_scalar(not_adj[:, p], w.adj[:, span(g, GT * N)].rearrange("p (t n) -> p t n", n=N), 0.0, NEG_MASK,
                                    ALU.is_le, ALU.mult).then_inc(s["mask_ready"], 1)

                def values(g, p):
                    e.wait_ge(s["v_psum"], g + 1)
                    e.tensor_tensor(v1[:, p, :, :, 0:HD1].rearrange("p t h d -> p (t h) d"),
                                    ps_m[:, :].rearrange("p (x d) -> p x d", d=HD1),
                                    bv[:, :].rearrange("p (h d) -> p h d", d=HD1).unsqueeze(1).broadcast_to([P, GT, H1, HD1]),
                                    ALU.add).then_inc(s["v_ready"], 1)

                def mask_unit(g, p, u):
                    n = g * U1 + u
                    q = u % 2
                    if u == 0:
                        e.wait_ge(s["mask_ready"], g + 1)
                    e.wait_ge(s["exp_ready"], n + 1)
                    wait_apart(e, w, s["s_psum"], n + 1)
                    for i in range(HALF):
                        last = e.tensor_tensor_reduce(scores[:, q, i, :], ps_s[:, q, i, :], not_adj[:, p, u // 2, :], 1.0, BIG,
                                                      ALU.add, ALU.min, row_min[:, q, i:i + 1])
                    last.then_inc(s["masked"], 1)

                def copy_t(g, p, u):
                    n = g * U1 + u
                    e.wait_ge(s["pv_psum"], n + 1)
                    for kt in range(2):
                        e.wait_ge(s["t_psum"], 2 * n + kt + 1 + 4)
                        e.tensor_copy(probs_t[:, u % 2, kt], ps_t[:, kt]).then_inc(s["t_ready"], 1)

                def normalise(g, p, v):
                    m = g * GT + v
                    e.wait_ge(s["pv_psum"], g * U1 + 2 * v + 2 + 2)
                    e.reciprocal(inv_sum[:, v % 2, :], ps_o[:, :, HD1]).then_inc(s["inv_ready"], 1)
                    e.wait_ge(s["inv_ready"], m + 1)
                    e.tensor_tensor(o[:, p, v, :].rearrange("p (h d) -> p h d", d=HD1), ps_o[:, :, 0:HD1],
                                    inv_sum[:, v % 2, :].unsqueeze(2).broadcast_to([P, H1, HD1]), ALU.mult).then_inc(s["o_ready"], 1)

                def body(g, p, has_next):
                    for u in range(U1):
                        if u + 1 < U1:
                            mask_unit(g, p, u + 1)
                        copy_t(g, p, u)
                        if u and u % 2 == 0:
                            normalise(g, p, u // 2 - 1)
                        if has_next:
                            if u == 0:
                                stats(g + 1, 1 - p)
                            if u == 1:
                                apply(g + 1, 1 - p)
                            if u == 2:
                                edges(g + 1, 1 - p)
                            if u == 5:
                                values(g + 1, 1 - p)
                    normalise(g, p, GT - 1)
                    if has_next:
                        mask_unit(g + 1, 1 - p, 0)
                    e.wait_ge(s["xb_ready"], g + 1)
                    e.wait_ge(s["y_psum"], g + 1)
                    e.tensor_tensor(w.x[:, span(g, GW)], ps_m[:, :], xb[:, p].rearrange("p t d -> p (t d)"), ALU.add).then_inc(s["dve_done"], 1)
                stats(0, 0)
                apply(0, 0)
                edges(0, 0)
                values(0, 0)
                mask_unit(0, 0, 0)
                over_groups(e, body)

            @block.tensor
            def _(e):
                give_credits(e, s["pe_done"])
                e.sem_inc(s["t_psum"], 4)
                e.sem_inc(s["pv_psum"], 2)
                e.wait_ge(s["weights"], 128)

                def transposes(g, p):
                    e.wait_ge(s["dve_done"], g + 1)
                    norm_transpose(e, s, w, g, p, ps_m)

                def project_q(g, p):
                    e.wait_ge(s["xt_ready"], g + 1)
                    e.matmul(ps_m[:, :], wq[:, :], w.xt[:, p, :], start=True, stop=True).then_inc(s["q_psum"], 1)

                def project_k(g, p):
                    e.wait_ge(s["q_ready"], g + 1)
                    e.matmul(ps_m[:, :], wk[:, :], w.xt[:, p, :], start=True, stop=True).then_inc(s["k_psum"], 1)

                def project_v(g, p):
                    e.wait_ge(s["k_ready"], g + 1)
                    for t in range(GT):
                        last = e.matmul(ps_m[:, t * D:(t + 1) * D], w.xt[:, p, t * P:(t + 1) * P], wv[:, :], start=True, stop=True)
                    last.then_inc(s["v_psum"], 1)

                def score(g, p, u):
                    n = g * U1 + u
                    v, hf = u // 2, u % 2
                    if u == 0:
                        e.wait_ge(k_loaded[p], g * 64 + (128 if p == 0 else 64))
                    e.wait_ge(s["masked"], n + 1)
                    for i in range(0, HALF, 2):
                        last = e.matmul(ps_s[:, u % 2, i:i + 2, :], q_t[:, p, v * P:(v + 1) * P],
                                        k_diag[:, p, v // 2, hf * HALF + i:hf * HALF + i + 2, :], start=True, stop=True)
                    last.then_inc(s["s_psum"], 1)

                def turn(g, p, u):
                    n = g * U1 + u
                    e.wait_ge(s["exp_ready"], n + 1 + 2)
                    for kt in range(2):
                        e.wait_ge(s["t_ready"], 2 * n + kt + 1)
                        for i in range(HALF):
                            last = e.transpose(ps_t[:, kt, i, :], probs[:, u % 2, i, kt * P:(kt + 1) * P], w.ident[:, :])
                        last.then_inc(s["t_psum"], 1)

                def weigh(g, p, u):
                    n = g * U1 + u
                    v, hf = u // 2, u % 2
                    if hf == 0:
                        e.wait_ge(s["o_ready"], g * GT + v + 1)
                    e.wait_ge(s["t_ready"], 2 * n + 2 + 2)
                    for i in range(HALF):
                        hh = hf * HALF + i
                        for kt in range(2):
                            last = e.matmul(ps_o[:, hh, :], probs_t[:, u % 2, kt, i, :], v1[:, p, v // 2 * 2 + kt, hh, :],
                                            start=kt == 0, stop=kt == 1)
                    last.then_inc(s["pv_psum"], 1)

                def body(g, p, has_next):
                    for u in range(U1):
                        if u + 1 < U1:
                            score(g, p, u + 1)
                        turn(g, p, u)
                        if u:
                            weigh(g, p, u - 1)
                        if has_next:
                            if u == 2:
                                transposes(g + 1, 1 - p)
                            if u == 3:
                                project_q(g + 1, 1 - p)
                            if u == 4:
                                project_k(g + 1, 1 - p)
                            if u == 5:
                                project_v(g + 1, 1 - p)
                    weigh(g, p, U1 - 1)
                    if has_next:
                        e.wait_ge(s["v_ready"], g + 2)
                        score(g + 1, 1 - p, 0)
                    e.wait_ge(s["o_ready"], g * GT + GT + 1)
                    for t in range(GT):
                        last = e.transpose(ps_m[:, t * P:(t + 1) * P], o[:, p, t, :], w.ident[:, :])
                    last.then_inc(s["ot_psum"], 1)
                    e.wait_ge(s["ot_ready"], g + 1)
                    for t in range(GT):
                        last = e.matmul(ps_m[:, t * D:(t + 1) * D], o_t[:, p, t * P:(t + 1) * P], wo[:, :], start=True, stop=True)
                    last.then_inc(s["y_psum"], 1)
                    e.drain().then_inc(s["pe_done"], 1)
                e.sem_inc(s["o_ready"], 1)
                transposes(0, 0)
                project_q(0, 0)
                project_k(0, 0)
                project_v(0, 0)
                e.wait_ge(s["v_ready"], 1)
                score(0, 0, 0)
                over_groups(e, body)

            @block.scalar
            def _(e):
                give_credits(e, s["act_done"])
                e.sem_inc(s["exp_ready"], 2)
                e.preload_act_table(ACT.Exp)
                e.wait_ge(s["weights"], 128)
                e.wait_ge(s["bq_scaled"], 1)

                def copy_xt(g, p):
                    norm_copy(e, s, w, g, p, ps_m[:, :])

                def copy_q(g, p):
                    e.wait_ge(s["q_psum"], g + 1)
                    e.activation(q_t[:, p, :], ps_m[:, :], ACT.Identity, bias=bq_scaled[:, 0:1], scale=-0.25).then_inc(s["q_ready"], 1)

                def copy_k(g, p):
                    e.wait_ge(s["k_psum"], g + 1)
                    e.activation(k_t[:, p, :], ps_m[:, :], ACT.Identity, bias=bk[:, 0:1]).then_inc(s["k_ready"], 1)

                def exps(g, p, u):
                    n = g * U1 + u
                    e.wait_ge(s["masked"], n + 1 + 2)
                    e.wait_ge(s["t_psum"], 2 * n + 2)
                    for i in range(HALF):
                        last = e.activation(probs[:, u % 2, i, :], scores[:, u % 2, i, :], ACT.Exp, bias=row_min[:, u % 2, i:i + 1], scale=-1.0)
                    last.then_inc(s["exp_ready"], 1)

                def body(g, p, has_next):
                    for u in range(1, U1 + 1):
                        if u < U1:
                            exps(g, p, u)
                        if has_next:
                            if u == 3:
                                copy_xt(g + 1, 1 - p)
                            if u == 4:
                                copy_q(g + 1, 1 - p)
                            if u == 5:
                                copy_k(g + 1, 1 - p)
                    if has_next:
                        exps(g + 1, 1 - p, 0)
                    e.wait_ge(s["ot_psum"], g + 1)
                    e.activation(o_t[:, p, :], ps_m[:, :], ACT.Copy).then_inc(s["ot_ready"], 1)
                    e.drain().then_inc(s["act_done"], 1)
                copy_xt(0, 0)
                copy_q(0, 0)
                copy_k(0, 0)
                exps(0, 0, 0)
                over_groups(e, body)


E1 = 8
F1 = 256
C1 = F1 // P
CAPACITY = float(-(-B * N * 1.25 // E1))
PACK = F1 + C1 * D + C1


def l1_ffn(nc, w, a):
    with ExitStack() as c:
        sb = lambda n, shape, dt=F32: c.enter_context(nc.sbuf_tensor("l1f_" + n, shape, dt))
        xt_all = sb("xt_all", [P, TILES * D])
        meanvar_all = sb("meanvar_all", [P, TILES, 2])
        rstd_all = sb("rstd_all", [P, TILES])
        sums = sb("sums", [P, B])
        weight_all = sb("weight_all", [P, B * 2])
        at_row = sb("at_row", [1, B * 2], U32)
        scratch_w = nc.dram_tensor("l1f_scratch_w", [B * 2], F32, kind="Internal").ap()
        scratch_at = nc.dram_tensor("l1f_scratch_at", [B * 2], U32, kind="Internal").ap()
        scratch_b = nc.dram_tensor("l1f_scratch_b", [B, D], F32, kind="Internal").ap()
        l1_ffn_normalise(nc, w, xt_all, meanvar_all, rstd_all, sums)
        l1_ffn_route(nc, w, a, sums, scratch_w, scratch_at, scratch_b, weight_all, at_row)
        l1_ffn_experts(nc, w, a, xt_all, meanvar_all, rstd_all, scratch_b, weight_all, at_row)


def l1_ffn_normalise(nc, w, xt_all, meanvar_all, rstd_all, sums):
    with ExitStack() as c:
        ps_t = [c.enter_context(nc.psum_tensor(f"l1n_ps_t{i}", [P, GW], F32)) for i in range(2)]
        s = named_semaphores(nc, c, "l1n", NORM_SEMS + " dve_done pe_done act_done pool_done")
        with nc.Block() as block:
            @block.vector
            def _(e):
                give_credits(e, s["dve_done"])

                def stats(g, p):
                    wait_groups_before(e, g, s["pool_done"])
                    norm_stats(e, s, w, g, p)

                def body(g, p, has_next):
                    if has_next:
                        stats(g + 1, 1 - p)
                    wait_groups_before(e, g, s["pe_done"])
                    norm_apply(e, s, w, g, p)
                    e.wait_ge(s["xt_psum"], g + 1)
                    e.tensor_reduce(sums[:, bass.ds(g * 2, 2)], ps_t[p][:, :].rearrange("p (b n) -> p b n", b=2), AX.X,
                                    ALU.add).then_inc(s["dve_done"], 1)
                stats(0, 0)
                over_groups(e, body)

            @block.gpsimd
            def _(e):
                give_credits(e, s["pool_done"])

                def body(g, p, has_next):
                    wait_groups_before(e, g, s["dve_done"])
                    norm_rstd(e, s, w, g, p)
                    e.tensor_copy(meanvar_all[:, bass.ds(g * GT, GT), :], w.meanvar[:, p])
                    e.wait_ge(s["rstd_ready"], g + 1)
                    e.tensor_copy(rstd_all[:, bass.ds(g * GT, GT)], w.rstd[:, p]).then_inc(s["pool_done"], 1)
                over_groups(e, body)

            @block.tensor
            def _(e):
                give_credits(e, s["pe_done"])

                def body(g, p, has_next):
                    wait_groups_before(e, g, s["dve_done"], s["act_done"])
                    e.wait_ge(s["xn_ready"], g + 1)
                    for t in range(GT):
                        last = e.transpose(ps_t[p][:, t * P:(t + 1) * P], w.xn[:, p, t, :], w.ident[:, :])
                    last.then_inc(s["xt_psum"], 1)
                    e.drain().then_inc(s["pe_done"], 1)
                over_groups(e, body)

            @block.scalar
            def _(e):
                give_credits(e, s["act_done"])

                def body(g, p, has_next):
                    e.wait_ge(s["dve_done"], g + 3)
                    e.activation(xt_all[:, span(g, GW)], ps_t[p][:, :], ACT.Copy).then_inc(s["act_done"], 1)
                over_groups(e, body)


def l1_ffn_route(nc, w, a, sums, scratch_w, scratch_at, scratch_b, weight_all, at_row):
    with ExitStack() as c:
        sb = lambda n, shape, dt=F32: c.enter_context(nc.sbuf_tensor("l1r_" + n, shape, dt))
        ps_l = c.enter_context(nc.psum_tensor("l1r_ps_l", [B, 512], F32))
        ps_load = c.enter_context(nc.psum_tensor("l1r_ps_load", [B, 512], F32))
        ps_d = c.enter_context(nc.psum_tensor("l1r_ps_d", [E1, 512], F32))
        ps_b = c.enter_context(nc.psum_tensor("l1r_ps_b", [B, 512], F32))
        wr = sb("wr", [P, E1]); br = sb("br", [B, E1]); b2 = sb("b2", [E1, D])
        lg = sb("lg", [B, E1]); mx = sb("mx", [B, 1]); ex = sb("ex", [B, E1]); total = sb("total", [B, 1])
        rw = sb("rw", [B, E1]); inv_load = sb("inv_load", [B, E1]); scale = sb("scale", [B, E1])
        lg2 = sb("lg2", [B, E1]); best = sb("best", [B, 8]); at = sb("at", [B, 8], U32); at_f = sb("at_f", [B, 8])
        diff = sb("diff", [B, 2]); ex2 = sb("ex2", [B, 2]); top = sb("top", [B, 2]); iota = sb("iota", [B, E1])
        hit0 = sb("hit0", [B, E1]); dense = sb("dense", [B, E1]); dense_t = sb("dense_t", [E1, B]); bias = sb("bias", [B, D])
        s = named_semaphores(nc, c, "l1r", "weights logit_psum v exps iota load_psum dense_psum dense_t bias_psum bias_ready out")
        with nc.Block() as block:
            @block.sync
            def _(e):
                e.dma_start(wr[:, :], a["L1_ffn_Wr"]).then_inc(s["weights"], 16)
                e.dma_start(br[:, :], a["L1_ffn_br"].partition_broadcast(B)).then_inc(s["weights"], 16)
                e.dma_start(b2[:, :], a["L1_ffn_b2"]).then_inc(s["weights"], 16)
                e.wait_ge(s["bias_ready"], 1)
                e.dma_start(scratch_w.rearrange("(b k) -> b k", k=2), top[:, :]).then_inc(w.scratch_stored, 16)
                e.dma_start(scratch_at.rearrange("(b k) -> b k", k=2), at[:, 0:2]).then_inc(w.scratch_stored, 16)
                e.dma_start(scratch_b, bias[:, :]).then_inc(w.scratch_stored, 16)
                e.wait_ge(w.scratch_stored, 48)
                e.dma_start(weight_all[:, :], scratch_w.partition_broadcast(P)).then_inc(s["out"], 16)
                e.dma_start(at_row[:, :], scratch_at.rearrange("(a k) -> a k", a=1)).then_inc(s["out"], 16)
                e.wait_ge(s["out"], 32)

            @block.gpsimd
            def _(e):
                e.iota(iota[:, :], pattern=[[1, E1]], base=0, channel_multiplier=0,
                       allow_small_or_imprecise_dtypes=True).then_inc(s["iota"], 1)

            @block.tensor
            def _(e):
                e.wait_ge(s["weights"], 48)
                e.matmul(ps_l[:, 0:E1], sums[:, :], wr[:, :], start=True, stop=True).then_inc(s["logit_psum"], 1)
                e.wait_ge(s["v"], 5)
                e.matmul(ps_load[:, 0:E1], w.ones[0:B, 0:B], rw[:, :], start=True, stop=True).then_inc(s["load_psum"], 1)
                e.wait_ge(s["v"], 20)
                e.transpose(ps_d[:, 0:B], dense[:, :], w.ident[0:B, 0:B]).then_inc(s["dense_psum"], 1)
                e.wait_ge(s["dense_t"], 1)
                e.matmul(ps_b[:, 0:D], dense_t[:, :], b2[:, :], start=True, stop=True).then_inc(s["bias_psum"], 1)

            @block.scalar
            def _(e):
                e.wait_ge(s["v"], 3)
                e.activation(ex[:, :], lg2[:, :], ACT.Exp).then_inc(s["exps"], 1)
                e.wait_ge(s["v"], 11)
                e.activation(ex[:, :], lg2[:, :], ACT.Exp).then_inc(s["exps"], 1)
                e.wait_ge(s["v"], 15)
                e.activation(ex2[:, :], diff[:, :], ACT.Exp).then_inc(s["exps"], 1)

            @block.vector
            def _(e):
                done = [0]

                def step(i):
                    i.then_inc(s["v"], 1)
                    done[0] += 1
                    e.wait_ge(s["v"], done[0])
                e.wait_ge(s["weights"], 48)
                e.wait_ge(s["logit_psum"], 1)
                step(e.scalar_tensor_tensor(lg[:, :], ps_l[:, 0:E1], 1.0 / N, br[:, :], ALU.mult, ALU.add))
                step(e.tensor_reduce(mx[:, :], lg[:, :], AX.X, ALU.max))
                step(e.tensor_scalar(lg2[:, :], lg[:, :], mx[:, 0:1], None, ALU.subtract))
                e.wait_ge(s["exps"], 1)
                step(e.tensor_reduce(total[:, :], ex[:, :], AX.X, ALU.add))
                e.reciprocal(mx[:, :], total[:, :]).then_inc(s["iota"], 1)
                e.wait_ge(s["iota"], 2)
                step(e.tensor_scalar(rw[:, :], ex[:, :], mx[:, 0:1], None, ALU.mult))
                e.wait_ge(s["load_psum"], 1)
                step(e.tensor_scalar(scale[:, :], ps_load[:, 0:E1], float(N), None, ALU.mult))
                step(e.reciprocal(inv_load[:, :], scale[:, :]))
                step(e.tensor_scalar(scale[:, :], inv_load[:, :], CAPACITY, 1.0, ALU.mult, ALU.min))
                step(e.tensor_tensor(lg[:, :], rw[:, :], scale[:, :], ALU.mult))
                step(e.tensor_reduce(mx[:, :], lg[:, :], AX.X, ALU.max))
                step(e.tensor_scalar(lg2[:, :], lg[:, :], mx[:, 0:1], None, ALU.subtract))
                e.wait_ge(s["exps"], 2)
                step(e.tensor_reduce(total[:, :], ex[:, :], AX.X, ALU.add))
                e.reciprocal(mx[:, :], total[:, :]).then_inc(s["iota"], 1)
                e.wait_ge(s["iota"], 3)
                step(e.tensor_scalar(rw[:, :], ex[:, :], mx[:, 0:1], None, ALU.mult))
                step(e.max(best[:, :], rw[:, :]))
                step(e.tensor_scalar(diff[:, :], best[:, 0:2], best[:, 0:1], None, ALU.subtract))
                step(e.max_index(at[:, :], best[:, :], rw[:, :]))
                e.wait_ge(s["exps"], 3)
                step(e.tensor_reduce(total[:, :], ex2[:, :], AX.X, ALU.add))
                e.reciprocal(mx[:, :], total[:, :])
                e.tensor_copy(at_f[:, :], at[:, :]).then_inc(s["iota"], 1)
                e.wait_ge(s["iota"], 4)
                step(e.tensor_scalar(top[:, :], ex2[:, :], mx[:, 0:1], None, ALU.mult))
                step(e.tensor_scalar(hit0[:, :], iota[:, :], at_f[:, 0:1], top[:, 0:1], ALU.is_equal, ALU.mult))
                e.tensor_scalar(dense[:, :], iota[:, :], at_f[:, 1:2], top[:, 1:2], ALU.is_equal, ALU.mult).then_inc(s["iota"], 1)
                e.wait_ge(s["iota"], 5)
                step(e.tensor_tensor(dense[:, :], dense[:, :], hit0[:, :], ALU.add))
                e.wait_ge(s["dense_psum"], 1)
                e.tensor_copy(dense_t[:, :], ps_d[:, 0:B]).then_inc(s["dense_t"], 1)
                e.wait_ge(s["bias_psum"], 1)
                e.tensor_copy(bias[:, :], ps_b[:, 0:D]).then_inc(s["bias_ready"], 1)


def l1_ffn_experts(nc, w, a, xt_all, meanvar_all, rstd_all, scratch_b, weight_all, at_row):
    with ExitStack() as c:
        sb = lambda n, shape, dt=F32: c.enter_context(nc.sbuf_tensor("l1f_" + n, shape, dt))
        ps = lambda n, shape: c.enter_context(nc.psum_tensor("l1f_" + n, shape, F32))
        pack = sb("pack", [P, 2, 4, PACK])
        bias = sb("bias", [P, 2, 2, D])
        gamma = sb("gamma", [P, D]); beta = sb("beta", [P, D])
        xn = sb("xn", [P, 2, GT, D]); xnb = sb("xnb", [P, 2, GT, D]); xb = sb("xb", [P, 2, GT, D])
        y0 = sb("y0", [P, 2, GT, D]); y1 = sb("y1", [P, 2, GT, D]); ln = sb("ln", [P, 2, GT, D]); ln_g = sb("ln_g", [P, 2, GT, D])
        h = sb("h", [P, 4, C1, N])
        ps_h = [ps(f"ps_h{i}", [P, C1, N]) for i in range(4)]
        ps_y = [ps(f"ps_y{i}", [P, 2, D]) for i in range(4)]
        s = named_semaphores(nc, c, "l1f", "weights pack0 pack1 xn_ready xnb_ready h_psum h_ready y_psum y0_ready y1_ready stats_done var_ready"
                             " veps_ready rstd_ready ln_ready ln_g_ready xb_ready pe_done act_done dve_done pool_done")
        loaded = [s["pack0"], s["pack1"]]
        with nc.Block() as block:
            @block.sync
            def _(e):
                e.dma_start(gamma[:, :], a["L1_ffn_gamma"].partition_broadcast(P)).then_inc(s["weights"], 16)
                e.dma_start(beta[:, :], a["L1_ffn_beta"].partition_broadcast(P)).then_inc(s["weights"], 16)

                def body(g, p, has_next):
                    wait_groups_before(e, g, s["pe_done"], s["act_done"], s["pool_done"])
                    for k in range(4):
                        x = e.value_load(at_row[0:1, bass.ds(g * 4 + k, 1)], min_val=0, max_val=E1 - 1)
                        e.dma_start(pack[:, p, k, :], a["L1_ffn_pack"][bass.ds(x, 1)].rearrange("a p f -> p (a f)")).then_inc(loaded[p], 16)
                    e.dma_start(bias[:, p].rearrange("p b d -> p (b d)"),
                                scratch_b.rearrange("b d -> (b d)")[bass.ds(g * 2 * D, 2 * D)].partition_broadcast(P)).then_inc(loaded[p], 16)
                over_groups(e, body)

            def wait_loaded(e, g, p):
                e.wait_ge(loaded[p], g * 40 + (80 if p == 0 else 40))

            @block.tensor
            def _(e):
                give_credits(e, s["pe_done"])

                def hidden(g, p, k):
                    e.wait_ge(s["h_ready"], g * 4 + k + 1)
                    for ch in range(C1):
                        last = e.matmul(ps_h[k][:, ch, :], pack[:, p, k, ch * P:(ch + 1) * P], xt_all[:, span(g, GW, k // 2 * N, N)],
                                        start=True, stop=True)
                    last.then_inc(s["h_psum"], 1)

                def output(g, p, k):
                    e.wait_ge(s["h_ready"], g * 4 + k + 1 + 4)
                    for t in range(2):
                        for ch in range(C1):
                            last = e.matmul(ps_y[k][:, t, :], h[:, k, ch, t * P:(t + 1) * P],
                                            pack[:, p, k, F1 + ch * D:F1 + (ch + 1) * D], start=ch == 0, stop=ch == C1 - 1)
                    last.then_inc(s["y_psum"], 1)

                def body(g, p, has_next):
                    wait_loaded(e, g, p)
                    hidden(g, p, 0)
                    for k in range(4):
                        if k + 1 < 4:
                            hidden(g, p, k + 1)
                        if k == 0:
                            e.wait_ge(s["y1_ready"], g + 1)
                        output(g, p, k)
                    e.drain().then_inc(s["pe_done"], 1)
                over_groups(e, body)

            @block.scalar
            def _(e):
                give_credits(e, s["act_done"])
                e.sem_inc(s["h_ready"], 4)
                e.preload_act_table(ACT.Gelu)

                def body(g, p, has_next):
                    wait_loaded(e, g, p)
                    for k in range(4):
                        e.wait_ge(s["h_psum"], g * 4 + k + 1)
                        e.wait_ge(s["y_psum"], g * 4 + k + 1)
                        for ch in range(C1):
                            last = e.activation(h[:, k, ch, :], ps_h[k][:, ch, :], ACT.Gelu, bias=pack[:, p, k, F1 + C1 * D + ch:F1 + C1 * D + ch + 1])
                        last.then_inc(s["h_ready"], 1)
                    e.drain().then_inc(s["act_done"], 1)
                over_groups(e, body)

            @block.vector
            def _(e):
                give_credits(e, s["dve_done"])
                e.sem_inc(s["y_psum"], 4)
                e.sem_inc(s["y1_ready"], 1)

                def apply(g, p):
                    wait_groups_before(e, g, s["pool_done"])
                    for t in range(GT):
                        last = e.tensor_scalar(xn[:, p, t, :], w.x[:, span(g, GW, t * D, D)], meanvar_all[:, bass.ds(g * GT + t, 1), 0],
                                               rstd_all[:, bass.ds(g * GT + t, 1)], ALU.subtract, ALU.mult)
                    last.then_inc(s["xn_ready"], 1)

                def body(g, p, has_next):
                    if has_next:
                        apply(g + 1, 1 - p)
                    e.wait_ge(s["xnb_ready"], g + 1)
                    e.wait_ge(s["y_psum"], g * 4 + 4 + 4)
                    for t in range(GT):
                        last = e.scalar_tensor_tensor(y0[:, p, t, :], ps_y[t // 2 * 2][:, t % 2, :], weight_all[:, bass.ds(g * 4 + t // 2 * 2, 1)],
                                                      xnb[:, p, t, :], ALU.mult, ALU.add)
                    last.then_inc(s["y0_ready"], 1)
                    e.wait_ge(s["y0_ready"], g + 1)
                    for t in range(GT):
                        last = e.scalar_tensor_tensor(y1[:, p, t, :], ps_y[t // 2 * 2 + 1][:, t % 2, :], weight_all[:, bass.ds(g * 4 + t // 2 * 2 + 1, 1)],
                                                      y0[:, p, t, :], ALU.mult, ALU.add)
                    last.then_inc(s["y1_ready"], 1)
                    e.wait_ge(s["y1_ready"], g + 2)
                    for t in range(GT):
                        last = e.bn_stats(w.stats[:, p, t, :], y1[:, p, t, :])
                    last.then_inc(s["stats_done"], 1)
                    wait_apart(e, w, s["stats_done"], g + 1)
                    for t in range(GT):
                        last = e.bn_aggr(w.meanvar[:, p, t, :], w.stats[:, p, t, :])
                    last.then_inc(s["var_ready"], 1)
                    e.wait_ge(s["rstd_ready"], g + 1)
                    for t in range(GT):
                        last = e.tensor_scalar(ln[:, p, t, :], y1[:, p, t, :], w.meanvar[:, p, t, 0:1], w.rstd[:, p, t:t + 1],
                                               ALU.subtract, ALU.mult)
                    last.then_inc(s["ln_ready"], 1)
                    e.wait_ge(s["ln_g_ready"], g + 1)
                    e.tensor_tensor(w.x[:, span(g, GW)], ln_g[:, p].rearrange("p t d -> p (t d)"), xb[:, p].rearrange("p t d -> p (t d)"),
                                    ALU.add).then_inc(s["dve_done"], 1)
                apply(0, 0)
                over_groups(e, body)

            @block.gpsimd
            def _(e):
                give_credits(e, s["pool_done"])
                e.wait_ge(s["weights"], 32)

                def body(g, p, has_next):
                    wait_groups_before(e, g, s["dve_done"])
                    wait_loaded(e, g, p)
                    e.wait_ge(s["xn_ready"], g + 1)
                    for t in range(GT):
                        last = e.tensor_tensor(xnb[:, p, t, :], xn[:, p, t, :], bias[:, p, t // 2, :], ALU.add)
                    last.then_inc(s["xnb_ready"], 1)
                    for t in range(GT):
                        e.tensor_tensor(xb[:, p, t, :], w.x[:, span(g, GW, t * D, D)], beta[:, :], ALU.add)
                    norm_rstd(e, s, w, g, p)
                    e.wait_ge(s["ln_ready"], g + 1)
                    for t in range(GT):
                        last = e.tensor_tensor(ln_g[:, p, t, :], ln[:, p, t, :], gamma[:, :], ALU.mult)
                    last.then_inc(s["ln_g_ready"], 1)
                    e.drain().then_inc(s["pool_done"], 1)
                over_groups(e, body)




def l2_gnn(nc, w, a):
    graph_attention(nc, w, a, "l2g", "L2_gnn_W_a", True)


def graph_attention(nc, w, a, name, weight, cosine):
    with ExitStack() as c:
        sb = lambda n, shape, dt=F32: c.enter_context(nc.sbuf_tensor(name + "_" + n, shape, dt))
        ps = lambda n, shape: c.enter_context(nc.psum_tensor(name + "_" + n, shape, F32))
        wa = sb("wa", [P, D])
        bias = sb("bias", [P, D])
        y_t = sb("y_t", [P, 2, GW])
        square = sb("square", [P, 2, GT, N])
        sum_sq = sb("sum_sq", [P, 2, GT])
        inv_mag = sb("inv_mag", [P, 2, GT])
        neg_inv = sb("neg_inv", [P, 2, GT])
        inv_row = sb("inv_row", [P, 2, 2, N])
        raw = sb("raw", [P, 2, GT, N])
        leaky = sb("leaky", [P, 2, GT, N])
        not_adj = sb("not_adj", [P, 2, GT, N])
        mask_int = sb("mask_int", [P, 2, 2, N], I32)
        scores = sb("scores", [P, 2, GT, N])
        row_min = sb("row_min", [P, 2, GT])
        probs = sb("probs", [P, 2, GT, N])
        row_sum = sb("row_sum", [P, 2, GT])
        inv_sum = sb("inv_sum", [P, 2, GT])
        probs_t = sb("probs_t", [P, 2, 2, 2, 2, P])
        hb = sb("hb", [P, 2, GT, D])
        low = sb("low", [P, 2, GT, D])
        ex = sb("ex", [P, 2, GT, D])
        high = sb("high", [P, 2, GT, D])
        ps_x = ps("ps_x", [P, GW])
        ps_s = [ps(f"ps_s{i}", [P, 2, N]) for i in range(2)]
        ps_b = ps("ps_b", [P, 2, N])
        ps_t = [ps(f"ps_t{i}", [P, 2, 2, P]) for i in range(2)]
        ps_h = ps("ps_h", [P, GT, D])
        s = named_semaphores(nc, c, name, NORM_SEMS + " " + DONE_SEMS + " weights mask_loaded0 mask_loaded1 mask_ready y_psum y_ready s_psum squares"
                             " mag_ready neg_ready b_psum b_ready raw_ready leaky_ready masked exp_ready sum_ready t_psum t_ready h_psum"
                             " hb_ready low_ready high_ready ex_ready")
        mask_loaded = [s["mask_loaded0"], s["mask_loaded1"]]
        with nc.Block() as block:
            @block.sync
            def _(e):
                e.dma_start(wa[:, :], a[weight]).then_inc(s["weights"], 16)
                if cosine:
                    e.dma_start(bias[:, :], a["L2_gnn_bias"].rearrange("a d -> (a d)").partition_broadcast(P)).then_inc(s["weights"], 16)
                else:
                    def body(g, p, has_next):
                        wait_groups_before(e, g, s["dve_done"])
                        e.dma_start(mask_int[:, p].rearrange("p b n -> p (b n)"),
                                    a["nodemask"].rearrange("b n -> (b n)")[bass.ds(g * 2 * N, 2 * N)].partition_broadcast(P)
                                    ).then_inc(mask_loaded[p], 16)
                    over_groups(e, body)

            @block.gpsimd
            def _(e):
                give_credits(e, s["pool_done"])

                def front(g, p):
                    wait_groups_before(e, g, s["dve_done"])
                    norm_rstd(e, s, w, g, p)
                    if cosine:
                        e.wait_ge(s["squares"], g + 1)
                        e.tensor_tensor(inv_mag[:, p, :], sum_sq[:, p, :], w.minus_half[:, 0:GT], ALU.pow).then_inc(s["mag_ready"], 1)

                def body(g, p, has_next):
                    if has_next:
                        front(g + 1, 1 - p)
                    e.drain().then_inc(s["pool_done"], 1)
                front(0, 0)
                over_groups(e, body)

            @block.vector
            def _(e):
                give_credits(e, s["dve_done"])
                e.wait_ge(s["weights"], 32 if cosine else 16)

                def front(g, p):
                    wait_groups_before(e, g, s["pool_done"])
                    norm_stats(e, s, w, g, p)
                    if cosine:
                        e.tensor_scalar(not_adj[:, p], w.adj[:, span(g, GT * N)].rearrange("p (t n) -> p t n", n=N), 0.0, NEG_MASK,
                                        ALU.is_le, ALU.mult).then_inc(s["mask_ready"], 1)
                    else:
                        e.wait_ge(mask_loaded[p], g * 8 + (16 if p == 0 else 8))
                        e.tensor_scalar(not_adj[:, p, 0:2, :], mask_int[:, p], 0.0, KEY_MASK, ALU.is_equal, ALU.mult).then_inc(s["mask_ready"], 1)
                    wait_groups_before(e, g, s["pe_done"])
                    norm_apply(e, s, w, g, p)

                def body(g, p, has_next):
                    if cosine:
                        e.wait_ge(s["mag_ready"], g + 1)
                        e.tensor_scalar(neg_inv[:, p, :], inv_mag[:, p, :], -1.0, None, ALU.mult).then_inc(s["neg_ready"], 1)
                        e.wait_ge(s["neg_ready"], g + 1)
                        e.wait_ge(s["b_ready"], g + 1)
                    e.wait_ge(s["s_psum"], g + 1)
                    for t in range(GT):
                        if cosine:
                            last = e.scalar_tensor_tensor(raw[:, p, t, :], ps_s[t // 2][:, t % 2, :], neg_inv[:, p, t:t + 1],
                                                          inv_row[:, p, t // 2, :], ALU.mult, ALU.mult)
                        else:
                            last = e.scalar_tensor_tensor(raw[:, p, t, :], ps_s[t // 2][:, t % 2, :], -1.0,
                                                          w.adj[:, span(g, GT * N, t * N, N)], ALU.mult, ALU.mult)
                    last.then_inc(s["raw_ready"], 1)
                    e.wait_ge(s["raw_ready"], g + 1)
                    held = raw
                    if cosine:
                        held = leaky
                        e.scalar_tensor_tensor(leaky[:, p], raw[:, p], -0.2, raw[:, p], ALU.mult, ALU.min).then_inc(s["leaky_ready"], 1)
                        e.wait_ge(s["leaky_ready"], g + 1)
                    wait_apart(e, w, s["mask_ready"], g + 1)
                    for t in range(GT):
                        last = e.tensor_tensor_reduce(scores[:, p, t, :], held[:, p, t, :], not_adj[:, p, t if cosine else t // 2, :],
                                                      1.0, BIG, ALU.add, ALU.min, row_min[:, p, t:t + 1])
                    last.then_inc(s["masked"], 1)
                    if has_next:
                        front(g + 1, 1 - p)
                    e.wait_ge(s["exp_ready"], g + 1)
                    e.reciprocal(inv_sum[:, p, :], row_sum[:, p, :]).then_inc(s["sum_ready"], 1)
                    e.wait_ge(s["sum_ready"], g + 1)
                    e.wait_ge(s["h_psum"], g + 1)
                    if not cosine:
                        for t in range(GT):
                            xt = w.x[:, span(g, GW, t * D, D)]
                            last = e.scalar_tensor_tensor(xt, ps_h[:, t, :], inv_sum[:, p, t:t + 1], xt, ALU.mult, ALU.add)
                        last.then_inc(s["dve_done"], 1)
                        return
                    for t in range(GT):
                        last = e.scalar_tensor_tensor(hb[:, p, t, :], ps_h[:, t, :], inv_sum[:, p, t:t + 1], bias[:, :], ALU.mult, ALU.add)
                    last.then_inc(s["hb_ready"], 1)
                    e.wait_ge(s["hb_ready"], g + 1)
                    e.tensor_scalar(low[:, p], hb[:, p], 0.0, None, ALU.min).then_inc(s["low_ready"], 1)
                    xg = w.x[:, span(g, GW)]
                    e.scalar_tensor_tensor(high[:, p].rearrange("p t d -> p (t d)"), hb[:, p].rearrange("p t d -> p (t d)"), 0.0, xg,
                                           ALU.max, ALU.add).then_inc(s["high_ready"], 1)
                    e.wait_ge(s["high_ready"], g + 1)
                    e.wait_ge(s["ex_ready"], g + 1)
                    e.scalar_tensor_tensor(xg, ex[:, p].rearrange("p t d -> p (t d)"), -1.0, high[:, p].rearrange("p t d -> p (t d)"),
                                           ALU.add, ALU.add).then_inc(s["dve_done"], 1)
                front(0, 0)
                over_groups(e, body)

            @block.tensor
            def _(e):
                give_credits(e, s["pe_done"])
                e.wait_ge(s["weights"], 32 if cosine else 16)

                def front(g, p, first=False):
                    norm_transpose(e, s, w, g, p, ps_x)
                    e.wait_ge(s["xt_ready"], g + 1)
                    e.matmul(ps_x[:, :], wa[:, :], w.xt[:, p, :], start=True, stop=True).then_inc(s["y_psum"], 1)
                    e.wait_ge(s["y_ready"], g + 1)
                    if not first:
                        e.wait_ge(s["raw_ready"], g)
                    other = y_t if cosine else w.xt
                    for t in range(GT):
                        last = e.matmul(ps_s[t // 2][:, t % 2, :], y_t[:, p, t * P:(t + 1) * P], other[:, p, t // 2 * N:(t // 2 + 1) * N],
                                        start=True, stop=True)
                    last.then_inc(s["s_psum"], 1)

                def magnitudes(g, p):
                    e.wait_ge(s["mag_ready"], g + 1)
                    for t in range(GT):
                        last = e.matmul(ps_b[:, t // 2, t % 2 * P:(t % 2 + 1) * P], inv_mag[:, p, t:t + 1].broadcast_to([P, P]), w.ident[:, :],
                                        start=True, stop=True)
                    last.then_inc(s["b_psum"], 1)

                def body(g, p, has_next):
                    if cosine:
                        magnitudes(g, p)
                    if has_next:
                        front(g + 1, 1 - p)
                    e.wait_ge(s["exp_ready"], g + 1)
                    for t in range(GT):
                        for m in range(2):
                            last = e.transpose(ps_t[t // 2][:, t % 2, m, :], probs[:, p, t, m * P:(m + 1) * P], w.ident[:, :])
                    last.then_inc(s["t_psum"], 1)
                    e.wait_ge(s["t_ready"], g + 1)
                    for t in range(GT):
                        for m in range(2):
                            last = e.matmul(ps_h[:, t, :], probs_t[:, p, t // 2, t % 2, m, :], w.xn[:, p, t // 2 * 2 + m, :],
                                            start=m == 0, stop=m == 1)
                    last.then_inc(s["h_psum"], 1)
                    e.drain().then_inc(s["pe_done"], 1)
                front(0, 0, True)
                over_groups(e, body)

            @block.scalar
            def _(e):
                give_credits(e, s["act_done"])
                e.preload_act_table(ACT.Exp)

                def front(g, p):
                    norm_copy(e, s, w, g, p, ps_x[:, :])
                    e.wait_ge(s["y_psum"], g + 1)
                    e.activation(y_t[:, p, :], ps_x[:, :], ACT.Copy).then_inc(s["y_ready"], 1)
                    if cosine:
                        e.wait_ge(s["s_psum"], g + 1)
                        for t in range(GT):
                            last = e.activation(square[:, p, t, :], ps_s[t // 2][:, t % 2, :], ACT.Square, accum_out=sum_sq[:, p, t:t + 1])
                        last.then_inc(s["squares"], 1)

                def body(g, p, has_next):
                    if cosine:
                        e.wait_ge(s["b_psum"], g + 1)
                        e.activation(inv_row[:, p], ps_b[:, :, :], ACT.Copy).then_inc(s["b_ready"], 1)
                    e.wait_ge(s["masked"], g + 1)
                    for t in range(GT):
                        last = e.activation(probs[:, p, t, :], scores[:, p, t, :], ACT.Exp, bias=row_min[:, p, t:t + 1], scale=-1.0,
                                            accum_out=row_sum[:, p, t:t + 1])
                    last.then_inc(s["exp_ready"], 1)
                    if has_next:
                        front(g + 1, 1 - p)
                    e.wait_ge(s["t_psum"], g + 1)
                    for b in range(2):
                        last = e.activation(probs_t[:, p, b], ps_t[b][:, :, :, :], ACT.Copy)
                    last.then_inc(s["t_ready"], 1)
                    if cosine:
                        e.wait_ge(s["low_ready"], g + 1)
                        e.activation(ex[:, p], low[:, p], ACT.Exp).then_inc(s["ex_ready"], 1)
                    e.drain().then_inc(s["act_done"], 1)
                front(0, 0)
                over_groups(e, body)


NH = 4
NE = 4
DH = D // NH
BLK = NH * GT
UNITS = NH * GT
CAUSAL = 1e30
HEAD_EPS = 1e-8

SLOTS = [
    [], [("prev", "gate_turn3")], [("prev", "gate_logits3")], [("next", "turn_x")], [("next", "heads")],
    [("next", "heads_turn")], [("own", "gate_turn0"), ("next", "keys")], [("own", "gate_logits0"), ("next", "values")],
    [("next", "query0")], [("prev", "ff_turn"), ("next", "query1")], [("own", "gate_turn1"), ("prev", "ff1")],
    [("own", "gate_logits1"), ("prev", "ff2")], [], [("next", "query2")], [("own", "gate_turn2"), ("prev", "out_turn")],
    [("own", "gate_logits2"), ("next", "query3"), ("prev", "out_logits")],
]
FRONT = ["turn_x", "heads", "heads_turn", "keys", "values", "query0", "query1", "query2", "query3"]
BACK = ["gate_turn3", "gate_logits3", "ff_turn", "ff1", "ff2", "out_turn", "out_logits"]
OWN = 6
PER_GROUP = len(FRONT) + len(BACK) + OWN


def bank_uses(g, has_prev, has_next):
    base = len(FRONT) if not has_prev else PER_GROUP * g + len(FRONT) - len(BACK)
    order = [u for slot in SLOTS for u in slot if (u[0] != "prev" or has_prev) and (u[0] != "next" or has_next)]
    return {u: base + k + 1 for k, u in enumerate(order)}


def gate_count(g, which, has_prev):
    if not has_prev:
        return {"own0": 1, "own1": 2}[which]
    return 5 * g + {"prev2": -2, "prev3": -1, "own0": 0, "own1": 1, "out": 2}[which]


def front_uses():
    return {("next", u): k + 1 for k, u in enumerate(FRONT)}


def tail_uses():
    base = PER_GROUP * GROUPS + len(FRONT) - len(BACK) - len(FRONT)
    return {("prev", u): base + k + 1 for k, u in enumerate(BACK)}


def over_groups_lagged(e, body):
    body(0, 0, False, True)
    with e.Fori(0, GROUPS // 2 - 1) as i:
        body(i * 2 + 1, 1, True, True)
        body(i * 2 + 2, 0, True, True)
    body(GROUPS - 1, 1, True, False)


def l2_ffn(nc, w, a):
    with ExitStack() as c:
        sb = lambda n, shape, dt=F32: c.enter_context(nc.sbuf_tensor("l2f_" + n, shape, dt))
        ps = lambda n, shape: c.enter_context(nc.psum_tensor("l2f_" + n, shape, F32))
        hl = sb("hl", [P, D]); hl_b = sb("hl_b", [P, 1])
        wq = sb("wq", [P, NH, D])
        wk = sb("wk", [P, D]); wv = sb("wv", [P, D]); fc1 = sb("fc1", [P, D]); fc2 = sb("fc2", [P, D])
        gate_w = sb("gate_w", [P, NH, NE]); gate_b = sb("gate_b", [P, NH, NE])
        ln_g = sb("ln_g", [P, DH]); ln_b = sb("ln_b", [P, DH]); fn_g = sb("fn_g", [P, DH]); fn_b = sb("fn_b", [P, DH])
        fc1_b = sb("fc1_b", [P, 1]); fc2_b = sb("fc2_b", [P, DH]); fgate = sb("fgate", [P, NH])
        causal = sb("causal", [P, N])
        head_eps = sb("head_eps", [P, BLK])
        resid = sb("resid", [P, 2, D])
        sx_t = sb("sx_t", [P, GW]); k_t = sb("k_t", [P, GW])
        k_diag = sb("k_diag", [P, NH, NE, GW])
        q_t = sb("q_t", [P, NH, GW])
        v1 = sb("v1", [P, 2, GT, NH, DH + 1])
        not_pad = sb("not_pad", [P, 2, GT, D])
        scores = sb("scores", [P, 2, NE * N]); probs = scores; probs_t = sb("probs_t", [P, 2, 2, NE, P])
        row_min = sb("row_min", [P, 2, NE])
        inv_sum = sb("inv_sum", [P, NE])
        o_raw = sb("o_raw", [P, NE, DH])
        o = sb("o", [P, 2, GT, NE, DH])
        o_t = sb("o_t", [P, GW])
        gl = sb("gl", [P, GT, NE]); gl_max = sb("gl_max", [P, GT]); gl_low = sb("gl_low", [P, GT, NE]); gl_ex = sb("gl_ex", [P, GT, NE])
        gl_sum = sb("gl_sum", [P, GT]); gl_inv = sb("gl_inv", [P, GT]); gate = sb("gate", [P, GT, NE])
        prod = sb("prod", [P, GT, NE, DH])
        mixed = sb("mixed", [P, GT, NH, DH])
        m = sb("m", [P, GT, NH, DH]); hstats = sb("hstats", [P, BLK, 6]); hmv = sb("hmv", [P, BLK, 2]); hve = sb("hve", [P, BLK]); hrstd = sb("hrstd", [P, BLK])
        ln0 = sb("ln0", [P, BLK, DH]); fx = sb("fx", [P, BLK, DH])
        fx_t = sb("fx_t", [P, GW]); r1 = sb("r1", [P, GW]); h1 = r1; t2 = sb("t2", [P, BLK, DH]); t3 = sb("t3", [P, BLK, DH])
        fo_t = fx_t
        ps_s = [ps(f"ps_s{i}", [P, NE * N]) for i in range(2)]
        ps_t = [ps(f"ps_t{i}", [P, NE, P]) for i in range(2)]
        ps_o = ps("ps_o", [P, NE, DH + 1])
        ps_m = ps("ps_m", [P, GW])
        s = named_semaphores(nc, c, "l2f", "stats_done var_ready veps_ready rstd_ready xn_ready weights zeroed const bank_psum bank_read"
                             " s_psum masked exp_ready t_psum t_ready pv_psum inv_ready o_raw_ready o_ready chain gl_ready gl_exp gate_ready prod_ready"
                             " mixed_ready hve_ready hrstd_ready ln0_ready ln1_ready fx_ready h1_ready x_done k_loaded0 k_loaded1 k_loaded2 k_loaded3")
        k_loaded = [s["k_loaded0"], s["k_loaded1"], s["k_loaded2"], s["k_loaded3"]]
        CH = 40
        og_max = sb("og_max", [P, GT]); og_low = sb("og_low", [P, GT, NH]); og_ex = sb("og_ex", [P, GT, NH])
        og_sum = sb("og_sum", [P, GT]); og_inv = sb("og_inv", [P, GT]); og = sb("og", [P, GT, NH])

        with nc.Block() as block:
            @block.sync
            def _(e):
                loads = [(hl[:, :], a["L2_ffn_hl_w_t"]), (hl_b[:, :], a["L2_ffn_hl_b"].rearrange("n (d a) -> (n d) a", a=1)),
                         (gate_w[:, :, :], a["L2_ffn_gate_w_t"]),
                         (gate_b[:, :, :].rearrange("p n e -> p (n e)"), a["L2_ffn_gate_b"].rearrange("n e -> (n e)").partition_broadcast(P)),
                         (fgate[:, :], a["L2_ffn_fgate_t"])]
                for dst, src in ((ln_g, "ln_g"), (ln_b, "ln_b"), (fn_g, "fnorm_g"), (fn_b, "fnorm_b"), (fc2_b, "fc2_b")):
                    loads.append((dst[:, :], a["L2_ffn_" + src].partition_broadcast(P)))
                for n in range(NH):
                    r = slice(n * DH, (n + 1) * DH)
                    loads.append((fc1_b[r, :], a["L2_ffn_fc1_b"].rearrange("(p a) -> p a", a=1)))
                for dst, src in loads:
                    e.dma_start(dst, src).then_inc(s["weights"], 16)
                e.wait_ge(s["zeroed"], 1)
                blocks = []
                for n in range(NH):
                    r = slice(n * DH, (n + 1) * DH)
                    blocks += [(wq[r, n, :], a["L2_ffn_wq_t"][n].rearrange("d e o -> d (e o)")), (wk[r, r], a["L2_ffn_wk_t"][n]),
                               (wv[r, r], a["L2_ffn_wv_t"][n]), (fc1[r, r], a["L2_ffn_fc1_t"]), (fc2[r, r], a["L2_ffn_fc2_t"])]
                for dst, src in blocks:
                    e.dma_start(dst, src).then_inc(s["weights"], 16)
                assert 16 * (len(loads) + len(blocks)) == WEIGHTS

                def keys(g, uses):
                    for n in range(NH):
                        if n == 0:
                            e.wait_ge(s["bank_read"], uses[("next", "keys")])
                        e.wait_ge(s["s_psum"], g * UNITS + 4 * n + 4)
                        for x in range(NE):
                            e.dma_start(k_diag[x * DH:(x + 1) * DH, n, x, :], k_t[n * DH:(n + 1) * DH, :]).then_inc(k_loaded[n], 16)

                def body(g, p, has_prev, has_next):
                    if has_next:
                        keys(g + 1, bank_uses(g, has_prev, has_next))
                keys(0, front_uses())
                over_groups_lagged(e, body)

            @block.gpsimd
            def _(e):
                for z in (wq[:, :, :], wk[:, :], wv[:, :], fc1[:, :], fc2[:, :], k_diag[:, :, :, :]):
                    e.memset(z, 0.0)
                e.memset(causal[:, :], 0.0)
                e.memset(head_eps[:, :], HEAD_EPS)
                e.memset(v1[:, :, :, :, DH:DH + 1], 1.0).then_inc(s["zeroed"], 1)
                e.wait_ge(s["zeroed"], 1)
                e.affine_select(out=causal[:, P:N], in_=causal[:, P:N], compare_op=ALU.is_ge, fill=CAUSAL, base=0,
                                pattern=[[-1, P]], channel_multiplier=1).then_inc(s["const"], 1)

                def head_product(g, n):
                    e.wait_ge(s["gate_ready"], g * NH + n + 1)
                    e.tensor_tensor(prod[:, :, :, :].rearrange("p t e d -> p (t e) d"), o[:, n % 2].rearrange("p t e d -> p (t e) d"),
                                    gate[:, :, :].rearrange("p t e -> p (t e)").unsqueeze(2).broadcast_to([P, GT * NE, DH]), ALU.mult
                                    ).then_inc(s["prod_ready"], 1)

                def head_rstd(k):
                    e.wait_ge(s["mixed_ready"], k + 1)
                    e.tensor_tensor(hve[:, :], hmv[:, :, 1], head_eps[:, :], ALU.add).then_inc(s["hve_ready"], 1)
                    e.wait_ge(s["hve_ready"], k + 1)
                    e.tensor_tensor(hrstd[:, :], hve[:, :], w.minus_half[:, 0:BLK], ALU.pow).then_inc(s["hrstd_ready"], 1)

                def head_affine(k, gain, shift):
                    e.wait_ge(s["ln0_ready"], k + 1)
                    e.tensor_tensor(ln0[:, :, :], ln0[:, :, :], gain[:, :].unsqueeze(1).broadcast_to([P, BLK, DH]), ALU.mult).then_inc(s["ln1_ready"], 1)
                    e.wait_ge(s["ln1_ready"], k + 1)
                    e.tensor_tensor(fx[:, :, :], ln0[:, :, :], shift[:, :].unsqueeze(1).broadcast_to([P, BLK, DH]), ALU.add).then_inc(s["fx_ready"], 1)

                def back_rest(g):
                    head_product(g, 3)
                    head_rstd(2 * g)
                    head_affine(2 * g, ln_g, ln_b)

                def back_last(g):
                    head_rstd(2 * g + 1)

                def body(g, p, has_prev, has_next):
                    if has_next:
                        norm_rstd(e, s, w, g + 1, 1 - p)
                    if has_prev:
                        head_product(g - 1, 2)
                        back_rest(g - 1)
                    head_product(g, 0)
                    if has_prev:
                        back_last(g - 1)
                    head_product(g, 1)
                    if has_prev:
                        head_affine(2 * (g - 1) + 1, fn_g, fn_b)
                e.wait_ge(s["weights"], WEIGHTS)
                norm_rstd(e, s, w, 0, 0)
                over_groups_lagged(e, body)
                head_product(GROUPS - 1, 2)
                back_rest(GROUPS - 1)
                back_last(GROUPS - 1)
                head_affine(2 * GROUPS - 1, fn_g, fn_b)

            def width(t):
                return P * (t % 2 + 1)

            @block.vector
            def _(e):
                e.sem_inc(s["masked"], 2)
                e.wait_ge(s["weights"], WEIGHTS)
                e.wait_ge(s["const"], 1)
                count = [None]

                def start_chain(g, first=0):
                    count[0] = (g, first)

                def step(i):
                    g, k = count[0]
                    i.then_inc(s["chain"], 1)
                    count[0] = (g, k + 1)
                    e.wait_ge(s["chain"], g * CH + k + 1)

                def end_chain():
                    g, k = count[0]
                    assert k <= CH, k
                    if k < CH:
                        e.sem_inc(s["chain"], CH - k)

                def apply(g, p):
                    norm_apply(e, s, w, g, p)

                def take_heads_turn(g, p, use):
                    e.wait_ge(s["bank_psum"], use)
                    i = e.tensor_scalar(not_pad[:, p].rearrange("p t d -> p (t d)"), ps_m[:, :], 0.0, None, ALU.not_equal)
                    if isinstance(g, int) and 2 * g < NH:
                        for b in range(2):
                            n = 2 * g + b
                            for t in range(2):
                                i = e.tensor_copy(resid[:, t, n * DH:(n + 1) * DH], ps_m[:, (2 * b + t) * D + n * DH:(2 * b + t) * D + (n + 1) * DH])
                    i.then_inc(s["bank_read"], 1)

                def take_values(g, p, use):
                    e.wait_ge(s["bank_psum"], use)
                    e.tensor_copy(v1[:, p, :, :, 0:DH].rearrange("p t n d -> p (t n) d"), ps_m[:, :].rearrange("p (x d) -> p x d", d=DH)).then_inc(s["bank_read"], 1)

                def take_gate(n, use):
                    e.wait_ge(s["bank_psum"], use)
                    e.tensor_tensor(gl[:, :, :], ps_m[:, 0:GT * NE].rearrange("p (t e) -> p t e", e=NE),
                                    gate_b[:, n, :].unsqueeze(1).broadcast_to([P, GT, NE]), ALU.add).then_inc(s["bank_read"], 1)
                    e.wait_ge(s["bank_read"], use)
                    step(e.tensor_reduce(gl_max[:, :], gl[:, :, :], AX.X, ALU.max))
                    e.tensor_tensor(gl_low[:, :, :], gl[:, :, :], gl_max[:, :].unsqueeze(2).broadcast_to([P, GT, NE]), ALU.subtract).then_inc(s["gl_ready"], 1)

                def gate_values(exps_done):
                    e.wait_ge(s["gl_exp"], exps_done)
                    step(e.tensor_reduce(gl_sum[:, :], gl_ex[:, :, :], AX.X, ALU.add))
                    step(e.reciprocal(gl_inv[:, :], gl_sum[:, :]))
                    e.tensor_tensor(gate[:, :, :], gl_ex[:, :, :], gl_inv[:, :].unsqueeze(2).broadcast_to([P, GT, NE]), ALU.mult).then_inc(s["gate_ready"], 1)

                def gate_sum(g, n):
                    e.wait_ge(s["prod_ready"], g * NH + n + 1)
                    step(e.tensor_reduce(mixed[:, :, n, :], prod[:, :, :, :].rearrange("p t e d -> p t d e"), AX.X, ALU.add))

                def block_stats(src):
                    for b in range(BLK):
                        i = e.bn_stats(hstats[:, b, :], src[:, b, :])
                    step(i)
                    e.sem_inc(w.passed, 1)
                    for b in range(BLK):
                        i = e.bn_aggr(hmv[:, b, :], hstats[:, b, :])
                    i.then_inc(s["mixed_ready"], 1)

                def block_apply(k, src):
                    e.wait_ge(s["hrstd_ready"], k + 1)
                    for b in range(BLK):
                        i = e.tensor_scalar(ln0[:, b, :], src[:, b, :], hmv[:, b, 0:1], hrstd[:, b:b + 1], ALU.subtract, ALU.mult)
                    i.then_inc(s["ln0_ready"], 1)

                def back1(g):
                    for b in range(2):
                        i = e.tensor_tensor(m[:, 2 * b:2 * b + 2].rearrange("p t n d -> p t (n d)"), mixed[:, 2 * b:2 * b + 2].rearrange("p t n d -> p t (n d)"),
                                            resid[:, :, :], ALU.add)
                    step(i)
                    block_stats(m[:, :, :, :].rearrange("p t n d -> p (t n) d"))

                def back2(g):
                    block_apply(2 * g, m[:, :, :, :].rearrange("p t n d -> p (t n) d"))

                def back_h1(g, use):
                    e.wait_ge(s["bank_read"], use)
                    e.scalar_tensor_tensor(h1[:, :], fx_t[:, :], 0.0, r1[:, :], ALU.not_equal, ALU.mult).then_inc(s["h1_ready"], 1)

                def back_ff2(g, use):
                    e.wait_ge(s["bank_psum"], use)
                    e.tensor_tensor(t2[:, :, :], ps_m[:, :].rearrange("p (x d) -> p x d", d=DH), fc2_b[:, :].unsqueeze(1).broadcast_to([P, BLK, DH]),
                                    ALU.add).then_inc(s["bank_read"], 1)

                def back3(g, use):
                    e.wait_ge(s["bank_read"], use)
                    step(e.scalar_tensor_tensor(t3[:, :, :], fx[:, :, :], 0.0, t2[:, :, :], ALU.not_equal, ALU.mult))
                    step(e.tensor_tensor(t2[:, :, :], t3[:, :, :], fx[:, :, :], ALU.add))
                    block_stats(t2)

                def back4(g):
                    block_apply(2 * g + 1, t2)

                def back_logits(g, use):
                    e.wait_ge(s["bank_psum"], use)
                    step(e.tensor_reduce(og_max[:, :], ps_m[:, 0:GT * NH].rearrange("p (t n) -> p t n", n=NH), AX.X, ALU.max))
                    e.tensor_tensor(og_low[:, :, :], ps_m[:, 0:GT * NH].rearrange("p (t n) -> p t n", n=NH),
                                    og_max[:, :].unsqueeze(2).broadcast_to([P, GT, NH]), ALU.subtract).then_inc(s["bank_read"], 1)

                def back_final(g, exps_done):
                    e.wait_ge(s["gl_exp"], exps_done)
                    step(e.tensor_reduce(og_sum[:, :], og_ex[:, :, :], AX.X, ALU.add))
                    step(e.reciprocal(og_inv[:, :], og_sum[:, :]))
                    step(e.tensor_tensor(og[:, :, :], og_ex[:, :, :], og_inv[:, :].unsqueeze(2).broadcast_to([P, GT, NH]), ALU.mult))
                    step(e.tensor_tensor(t3[:, :, :], fx[:, :, :], og[:, :, :].rearrange("p t n -> p (t n)").unsqueeze(2).broadcast_to([P, BLK, DH]), ALU.mult))
                    xg = w.x[:, span(g, GW)]
                    e.tensor_tensor(xg, xg, t3[:, :, :].rearrange("p x d -> p (x d)"), ALU.add).then_inc(s["x_done"], 1)

                def mask_unit(g, u):
                    k = g * UNITS + u
                    q, t = u % 2, u % GT
                    wd = width(t)
                    e.wait_ge(s["t_psum"], k + 3)
                    wait_apart(e, w, s["s_psum"], k + 1 + UNITS)
                    for x in range(NE):
                        i = e.tensor_tensor_reduce(scores[:, q, x * wd:(x + 1) * wd], ps_s[q][:, x * wd:(x + 1) * wd], causal[:, N - wd:N],
                                                   1.0, BIG, ALU.add, ALU.min, row_min[:, q, x:x + 1])
                    i.then_inc(s["masked"], 1)

                def normalise(g, p, u):
                    k = g * UNITS + u
                    n, t = u // GT, u % GT
                    e.wait_ge(s["pv_psum"], k + 1 + 2)
                    e.reciprocal(inv_sum[:, :], ps_o[:, :, DH]).then_inc(s["inv_ready"], 1)
                    e.wait_ge(s["inv_ready"], k + 1)
                    e.tensor_tensor(o_raw[:, :, :], ps_o[:, :, 0:DH], inv_sum[:, :].unsqueeze(2).broadcast_to([P, NE, DH]), ALU.mult).then_inc(s["o_raw_ready"], 1)
                    e.wait_ge(s["o_raw_ready"], k + 1)
                    e.tensor_tensor(o[:, n % 2, t], o_raw[:, :, :], not_pad[:, p, t, n * DH:(n + 1) * DH].unsqueeze(1).broadcast_to([P, NE, DH]),
                                    ALU.mult).then_inc(s["o_ready"], 1)

                def body(g, p, has_prev, has_next):
                    uses = bank_uses(g, has_prev, has_next)
                    start_chain(g)
                    for u in range(UNITS):
                        if u + 1 < UNITS:
                            mask_unit(g, u + 1)
                        if has_next and u == 0:
                            norm_stats(e, s, w, g + 1, 1 - p)
                        if has_prev and u == 0:
                            gate_values(gate_count(g, "prev2", True))
                        if has_prev and u == 1:
                            gate_sum(g - 1, 2)
                        if has_next and u == 1:
                            apply(g + 1, 1 - p)
                        if has_prev and u == 2:
                            take_gate(3, uses[("prev", "gate_logits3")])
                        if has_prev and u == 4:
                            gate_values(gate_count(g, "prev3", True))
                        if u == 5:
                            if has_prev:
                                gate_sum(g - 1, 3)
                            if has_next:
                                take_heads_turn(g + 1, 1 - p, uses[("next", "heads_turn")])
                        if has_prev and u == 6:
                            back1(g - 1)
                        if u == 7:
                            take_gate(0, uses[("own", "gate_logits0")])
                            if has_next:
                                take_values(g + 1, 1 - p, uses[("next", "values")])
                            if has_prev:
                                back2(g - 1)
                        if u == 8:
                            gate_values(gate_count(g, "own0", has_prev))
                        if u == 9:
                            gate_sum(g, 0)
                        if u == 11:
                            if has_prev:
                                back_h1(g - 1, uses[("prev", "ff1")])
                            take_gate(1, uses[("own", "gate_logits1")])
                            if has_prev:
                                back_ff2(g - 1, uses[("prev", "ff2")])
                        if u == 12:
                            if has_prev:
                                back3(g - 1, uses[("prev", "ff2")])
                            gate_values(gate_count(g, "own1", has_prev))
                        if u == 13:
                            gate_sum(g, 1)
                            if has_prev:
                                back4(g - 1)
                        if u == 15:
                            take_gate(2, uses[("own", "gate_logits2")])
                        if u:
                            normalise(g, p, u - 1)
                    normalise(g, p, UNITS - 1)
                    if has_next:
                        mask_unit(g + 1, 0)
                    if has_prev:
                        back_logits(g - 1, uses[("prev", "out_logits")])
                        back_final(g - 1, gate_count(g, "out", True))
                    end_chain()

                norm_stats(e, s, w, 0, 0)
                apply(0, 0)
                uses = front_uses()
                take_heads_turn(0, 0, uses[("next", "heads_turn")])
                take_values(0, 0, uses[("next", "values")])
                mask_unit(0, 0)
                over_groups_lagged(e, body)
                g, uses = GROUPS - 1, tail_uses()
                start_chain(GROUPS)
                gate_values(gate_count(GROUPS, "prev2", True))
                gate_sum(g, 2)
                take_gate(3, uses[("prev", "gate_logits3")])
                gate_values(gate_count(GROUPS, "prev3", True))
                gate_sum(g, 3)
                back1(g)
                back2(g)
                back_h1(g, uses[("prev", "ff1")])
                back_ff2(g, uses[("prev", "ff2")])
                back3(g, uses[("prev", "ff2")])
                back4(g)
                back_logits(g, uses[("prev", "out_logits")])
                back_final(g, gate_count(GROUPS, "prev3", True) + 1)

            @block.tensor
            def _(e):
                e.sem_inc(s["s_psum"], UNITS)
                e.sem_inc(s["t_psum"], 4)
                e.sem_inc(s["pv_psum"], 2)
                e.sem_inc(s["o_ready"], 1)
                e.wait_ge(s["weights"], WEIGHTS)

                def use(kind, name, count, g, p):
                    if not (isinstance(count, int) and count == 1):
                        e.wait_ge(s["bank_read"], count - 1)
                    if name == "turn_x":
                        e.wait_ge(s["xn_ready"], g + 1)
                        for t in range(GT):
                            i = e.transpose(ps_m[:, t * P:(t + 1) * P], w.xn[:, p, t, :], w.ident[:, :])
                    elif name == "heads":
                        i = e.matmul(ps_m[:, :], hl[:, :], w.xt[:, p, :], start=True, stop=True)
                    elif name == "heads_turn":
                        for t in range(GT):
                            i = e.transpose(ps_m[:, t * P:(t + 1) * P], sx_t[:, t * P:(t + 1) * P], w.ident[:, :])
                    elif name == "keys":
                        i = e.matmul(ps_m[:, :], wk[:, :], sx_t[:, :], start=True, stop=True)
                    elif name == "values":
                        for t in range(GT):
                            i = e.matmul(ps_m[:, t * D:(t + 1) * D], sx_t[:, t * P:(t + 1) * P], wv[:, :], start=True, stop=True)
                    elif name.startswith("query"):
                        i = e.matmul(ps_m[:, :], wq[:, int(name[-1]), :], sx_t[:, :], start=True, stop=True)
                    elif name.startswith("gate_turn"):
                        n = int(name[-1])
                        e.wait_ge(s["o_ready"], g * UNITS + 4 * n + 4 + 1)
                        for t in range(GT):
                            i = e.transpose(ps_m[:, t * P:(t + 1) * P], o[:, n % 2, t].rearrange("p e d -> p (e d)"), w.ident[:, :])
                    elif name.startswith("gate_logits"):
                        n = int(name[-1])
                        for t in range(GT):
                            i = e.matmul(ps_m[:, t * NE:(t + 1) * NE], o_t[:, t * P:(t + 1) * P], gate_w[:, n, :], start=True, stop=True)
                    elif name in ("ff_turn", "out_turn"):
                        e.wait_ge(s["fx_ready"], 2 * g + (1 if name == "ff_turn" else 2))
                        for t in range(GT):
                            i = e.transpose(ps_m[:, t * P:(t + 1) * P], fx[:, t * NH:(t + 1) * NH, :].rearrange("p n d -> p (n d)"), w.ident[:, :])
                    elif name == "ff1":
                        i = e.matmul(ps_m[:, :], fc1[:, :], fx_t[:, :], start=True, stop=True)
                    elif name == "ff2":
                        e.wait_ge(s["h1_ready"], g + 1)
                        for t in range(GT):
                            i = e.matmul(ps_m[:, t * D:(t + 1) * D], h1[:, t * P:(t + 1) * P], fc2[:, :], start=True, stop=True)
                    else:
                        assert name == "out_logits"
                        for t in range(GT):
                            i = e.matmul(ps_m[:, t * NH:(t + 1) * NH], fo_t[:, t * P:(t + 1) * P], fgate[:, :], start=True, stop=True)
                    i.then_inc(s["bank_psum"], 1)

                def score(g, u):
                    k = g * UNITS + u
                    n, t = u // GT, u % GT
                    wd = width(t)
                    if t == 0:
                        e.wait_ge(k_loaded[n], g * 64 + 64)
                    e.wait_ge(s["masked"], k + 1)
                    step = 512 // wd
                    for x in range(0, NE, step):
                        keys = k_diag[:, n, x:x + step, t // 2 * N:t // 2 * N + wd]
                        i = e.matmul(ps_s[u % 2][:, x * wd:(x + step) * wd], q_t[:, n, t * P:(t + 1) * P], keys, start=True, stop=True)
                    i.then_inc(s["s_psum"], 1)

                def turn(g, u):
                    k = g * UNITS + u
                    t = u % GT
                    wd = width(t)
                    e.wait_ge(s["exp_ready"], k + 1 + 2)
                    for kt in range(t % 2 + 1):
                        e.wait_ge(s["t_ready"], k + 1)
                        for x in range(NE):
                            i = e.transpose(ps_t[kt][:, x, :], probs[:, u % 2, x * wd + kt * P:x * wd + (kt + 1) * P], w.ident[:, :])
                    i.then_inc(s["t_psum"], 1)

                def weigh(g, p, u):
                    k = g * UNITS + u
                    n, t = u // GT, u % GT
                    e.wait_ge(s["o_ready"], k + 1)
                    e.wait_ge(s["t_ready"], k + 2)
                    for x in range(NE):
                        for kt in range(t % 2 + 1):
                            i = e.matmul(ps_o[:, x, :], probs_t[:, u % 2, kt, x, :], v1[:, p, t // 2 * 2 + kt, n, :],
                                         start=kt == 0, stop=kt == t % 2)
                    i.then_inc(s["pv_psum"], 1)

                def body(g, p, has_prev, has_next):
                    uses = bank_uses(g, has_prev, has_next)
                    group = {"prev": (g - 1, 1 - p), "own": (g, p), "next": (g + 1, 1 - p)}
                    for u in range(UNITS):
                        if u + 1 < UNITS:
                            score(g, u + 1)
                        mine = [x for x in SLOTS[u] if x in uses and x[1] not in ("out_logits", "query3")]
                        for x in mine[:1]:
                            use(*x, uses[x], *group[x[0]])
                        turn(g, u)
                        for x in mine[1:]:
                            use(*x, uses[x], *group[x[0]])
                        if u:
                            weigh(g, p, u - 1)
                    weigh(g, p, UNITS - 1)
                    if has_next:
                        x = ("next", "query3")
                        use(*x, uses[x], *group["next"])
                        score(g + 1, 0)
                    if has_prev:
                        x = ("prev", "out_logits")
                        use(*x, uses[x], *group["prev"])
                for x, k in front_uses().items():
                    use(*x, k, 0, 0)
                score(0, 0)
                over_groups_lagged(e, body)
                for x, k in tail_uses().items():
                    use(*x, k, GROUPS - 1, 1)

            @block.scalar
            def _(e):
                e.sem_inc(s["exp_ready"], 2)
                e.sem_inc(s["t_ready"], 1)
                e.preload_act_table(ACT.Exp)
                e.wait_ge(s["weights"], WEIGHTS)

                def take(name, count, g, p):
                    if name in ("heads_turn", "values", "ff2", "out_logits") or name.startswith("gate_logits"):
                        return
                    e.wait_ge(s["bank_psum"], count)
                    if name == "turn_x":
                        i = e.activation(w.xt[:, p, :], ps_m[:, :], ACT.Copy)
                    elif name == "heads":
                        i = e.activation(sx_t[:, :], ps_m[:, :], ACT.Identity, bias=hl_b[:, 0:1])
                    elif name == "keys":
                        if not isinstance(g, int) or g:
                            for k in k_loaded:
                                e.wait_ge(k, g * 64)
                        i = e.activation(k_t[:, :], ps_m[:, :], ACT.Copy)
                    elif name.startswith("query"):
                        n = int(name[-1])
                        e.wait_ge(s["s_psum"], g * UNITS + 4 * n + 4)
                        e.activation(q_t[:, n, :], ps_m[:, :], ACT.Copy, scale=-float(DH) ** 0.5).then_inc(s["bank_read"], 1)
                        return
                    elif name.startswith("gate_turn"):
                        i = e.activation(o_t[:, :], ps_m[:, :], ACT.Copy)
                    elif name == "ff_turn":
                        i = e.activation(fx_t[:, :], ps_m[:, :], ACT.Copy)
                    elif name == "ff1":
                        i = e.activation(r1[:, :], ps_m[:, :], ACT.Relu, bias=fc1_b[:, 0:1])
                    else:
                        assert name == "out_turn"
                        i = e.activation(fo_t[:, :], ps_m[:, :], ACT.Copy)
                    i.then_inc(s["bank_read"], 1)

                def exps(g, u):
                    k = g * UNITS + u
                    wd = width(u % GT)
                    e.wait_ge(s["masked"], k + 1 + 2)
                    for x in range(NE):
                        i = e.activation(probs[:, u % 2, x * wd:(x + 1) * wd], scores[:, u % 2, x * wd:(x + 1) * wd], ACT.Exp,
                                         bias=row_min[:, u % 2, x:x + 1], scale=-1.0)
                    i.then_inc(s["exp_ready"], 1)

                def copy_t(g, u):
                    k = g * UNITS + u
                    e.wait_ge(s["t_psum"], k + 1 + 4)
                    e.wait_ge(s["pv_psum"], k + 1)
                    for kt in range(u % GT % 2 + 1):
                        i = e.activation(probs_t[:, u % 2, kt], ps_t[kt][:, :, :], ACT.Copy)
                    i.then_inc(s["t_ready"], 1)

                def head_gate(g, n):
                    e.wait_ge(s["gl_ready"], g * NH + n + 1)
                    e.activation(gl_ex[:, :, :], gl_low[:, :, :], ACT.Exp).then_inc(s["gl_exp"], 1)

                def out_gate(use):
                    e.wait_ge(s["bank_read"], use)
                    e.activation(og_ex[:, :, :], og_low[:, :, :], ACT.Exp).then_inc(s["gl_exp"], 1)

                def body(g, p, has_prev, has_next):
                    uses = bank_uses(g, has_prev, has_next)
                    group = {"prev": (g - 1, 1 - p), "own": (g, p), "next": (g + 1, 1 - p)}
                    for u in range(UNITS):
                        if u + 1 < UNITS:
                            exps(g, u + 1)
                        if has_prev and u == 0:
                            head_gate(g - 1, 2)
                        if has_prev and u == 3:
                            head_gate(g - 1, 3)
                        if u == 8:
                            head_gate(g, 0)
                        if u == 12:
                            head_gate(g, 1)
                        mine = [x for x in SLOTS[u] if x in uses and x[1] not in ("out_logits", "query3")]
                        for x in mine[:1]:
                            take(x[1], uses[x], *group[x[0]])
                        copy_t(g, u)
                        for x in mine[1:]:
                            take(x[1], uses[x], *group[x[0]])
                    if has_next:
                        take("query3", uses[("next", "query3")], g + 1, 1 - p)
                        exps(g + 1, 0)
                    if has_prev:
                        out_gate(uses[("prev", "out_logits")])
                for x, k in front_uses().items():
                    take(x[1], k, 0, 0)
                exps(0, 0)
                over_groups_lagged(e, body)
                g, uses = GROUPS - 1, tail_uses()
                head_gate(g, 2)
                take("gate_turn3", uses[("prev", "gate_turn3")], g, 1)
                head_gate(g, 3)
                for name in ("ff_turn", "ff1", "out_turn"):
                    take(name, uses[("prev", name)], g, 1)
                out_gate(uses[("prev", "out_logits")])


WEIGHTS = 16 * (5 + 5 + 4 + 5 * NH)


def l3_gnn(nc, w, a):
    graph_attention(nc, w, a, "l3g", "L3_gnn_W", False)


E3 = 6
R3 = D // 2
PAD = 8


def l3_ffn(nc, w, a):
    with ExitStack() as c:
        sb = lambda n, shape, dt=F32: c.enter_context(nc.sbuf_tensor("l3f_" + n, shape, dt))
        ps = lambda n, shape: c.enter_context(nc.psum_tensor("l3f_" + n, shape, F32))
        w1 = sb("w1", [P, E3, D]); w2 = sb("w2", [P, E3, D]); w3 = sb("w3", [P, E3, D])
        b1 = sb("b1", [P, E3]); b2 = sb("b2", [P, E3]); b3 = sb("b3", [E3, D])
        rw1 = sb("rw1", [P, R3]); rb1 = sb("rb1", [R3, 1]); rw2 = sb("rw2", [R3, E3]); rb2 = sb("rb2", [P, E3])
        iota = sb("iota", [P, E3])
        r_t = sb("r_t", [R3, 2, GW])
        lg = sb("lg", [P, 2, GT, E3])
        row_max = sb("row_max", [P, 2, GT])
        logits = sb("logits", [P, 2, GT, E3])
        expo = sb("expo", [P, 2, GT, E3])
        total = sb("total", [P, 2, GT])
        inv_total = sb("inv_total", [P, 2, GT])
        prob = sb("prob", [P, 2, GT, PAD])
        best = sb("best", [P, 2, GT, 8])
        best_at = sb("best_at", [P, 2, GT, 8], U32)
        best_f = sb("best_f", [P, 2, GT, 8])
        diff = sb("diff", [P, 2, GT, 2])
        top = sb("top", [P, 2, GT, 2])
        top_total = sb("top_total", [P, 2, GT])
        inv_top = sb("inv_top", [P, 2, GT])
        weight = sb("weight", [P, 2, GT, 2])
        hit = sb("hit", [P, 2, 2, GT, E3])
        mask = sb("mask", [P, 2, GT, E3])
        mask_t = sb("mask_t", [E3, 2, GW])
        h1 = sb("h1", [P, 2, GW]); h2 = sb("h2", [P, 2, GW])
        ps_1 = [ps(f"ps_1{i}", [P, 512]) for i in range(2)]
        ps_2 = [ps(f"ps_2{i}", [P, 512]) for i in range(2)]
        ps_y = [ps(f"ps_y{i}", [P, 512]) for i in range(2)]
        ps_t = ps("ps_t", [P, 512])
        ps_m = ps("ps_m", [P, 512])
        s = named_semaphores(nc, c, "l3f", NORM_SEMS + " " + DONE_SEMS + " weights const pads r_psum r_ready logit_psum lg_ready max_ready logit_ready"
                             " exp_ready chain diff_ready top_ready mask_ready mask_psum mask_t_ready bias_psum bias_added h1_psum h1_ready h2_psum h2_ready"
                             " y_psum y_added")
        LINKS = 8
        with nc.Block() as block:
            @block.sync
            def _(e):
                for dst, src in ((rw1[:, :], a["L3_ffn_router_w1"]), (rb1[:, :], a["L3_ffn_router_b1"].rearrange("(p a) -> p a", a=1)),
                                 (rw2[:, :], a["L3_ffn_router_w2"]), (rb2[:, :], a["L3_ffn_router_b2"].partition_broadcast(P)),
                                 (b1[:, :], a["L3_ffn_b1_t"]), (b2[:, :], a["L3_ffn_b2_t"]), (b3[:, :], a["L3_ffn_expert_b3"]),
                                 (w1[:, :, :], a["L3_ffn_expert_w1"].rearrange("e d h -> d e h")),
                                 (w2[:, :, :], a["L3_ffn_expert_w2"].rearrange("e d h -> d e h")),
                                 (w3[:, :, :], a["L3_ffn_expert_w3"].rearrange("e d h -> d e h"))):
                    e.dma_start(dst, src).then_inc(s["weights"], 16)

            def route(e, g, p):
                at = g * LINKS

                def wide(v, n):
                    return v.unsqueeze(2).broadcast_to([P, GT, n])
                e.wait_ge(s["logit_psum"], g + 1)
                e.tensor_tensor(lg[:, p], ps_m[:, 0:GT * E3].rearrange("p (t e) -> p t e", e=E3),
                                rb2[:, :].unsqueeze(1).broadcast_to([P, GT, E3]), ALU.add).then_inc(s["lg_ready"], 1)
                e.wait_ge(s["lg_ready"], g + 1)
                e.tensor_reduce(row_max[:, p, :], lg[:, p], AX.X, ALU.max).then_inc(s["max_ready"], 1)
                e.wait_ge(s["max_ready"], g + 1)
                e.tensor_tensor(logits[:, p], lg[:, p], wide(row_max[:, p, :], E3), ALU.subtract).then_inc(s["logit_ready"], 1)
                e.wait_ge(s["exp_ready"], g + 1)
                e.tensor_reduce(total[:, p, :], expo[:, p], AX.X, ALU.add).then_inc(s["chain"], 1)
                e.wait_ge(s["chain"], at + 1)
                e.reciprocal(inv_total[:, p, :], total[:, p, :]).then_inc(s["chain"], 1)
                e.wait_ge(s["chain"], at + 2)
                e.tensor_tensor(prob[:, p, :, 0:E3], expo[:, p], wide(inv_total[:, p, :], E3), ALU.mult).then_inc(s["chain"], 1)
                wait_apart(e, w, s["chain"], at + 3)
                for t in range(GT):
                    last = e.max(best[:, p, t, :], prob[:, p, t, :])
                last.then_inc(s["chain"], 1)
                wait_apart(e, w, s["chain"], at + 4)
                e.tensor_tensor(diff[:, p], best[:, p, :, 0:2], wide(best[:, p, :, 0], 2), ALU.subtract).then_inc(s["diff_ready"], 1)
                for t in range(GT):
                    last = e.max_index(best_at[:, p, t, :], best[:, p, t, :], prob[:, p, t, :])
                last.then_inc(s["chain"], 1)
                e.wait_ge(s["chain"], at + 5)
                e.tensor_copy(best_f[:, p], best_at[:, p])
                e.wait_ge(s["top_ready"], g + 1)
                e.tensor_tensor(top_total[:, p, :], top[:, p, :, 0], top[:, p, :, 1], ALU.add).then_inc(s["chain"], 1)
                e.wait_ge(s["chain"], at + 6)
                e.reciprocal(inv_top[:, p, :], top_total[:, p, :]).then_inc(s["chain"], 1)
                e.wait_ge(s["chain"], at + 7)
                e.tensor_tensor(weight[:, p], top[:, p], wide(inv_top[:, p, :], 2), ALU.mult).then_inc(s["chain"], 1)
                e.wait_ge(s["chain"], at + 8)
                for t in range(GT):
                    for k in range(2):
                        last = e.tensor_scalar(hit[:, p, k, t, :], iota[:, :], best_f[:, p, t, k:k + 1],
                                               weight[:, p, t, k:k + 1], ALU.is_equal, ALU.mult)
                last.then_inc(s["pads"], 1)
                e.wait_ge(s["pads"], g + 2)
                e.tensor_tensor(mask[:, p], hit[:, p, 0], hit[:, p, 1], ALU.add).then_inc(s["mask_ready"], 1)

            @block.vector
            def _(e):
                give_credits(e, s["dve_done"])
                e.sem_inc(s["y_added"], 2)
                e.wait_ge(s["const"], 1)
                e.wait_ge(s["pads"], 1)
                e.wait_ge(s["weights"], 160)

                def stats(g, p):
                    wait_groups_before(e, g, s["pool_done"])
                    norm_stats(e, s, w, g, p)

                def apply(g, p):
                    wait_groups_before(e, g, s["pe_done"])
                    norm_apply(e, s, w, g, p)

                def body(g, p, has_next):
                    e.wait_ge(s["bias_psum"], g + 1)
                    xg = w.x[:, span(g, GW)]
                    e.tensor_tensor(xg, xg, ps_t[:, :], ALU.add).then_inc(s["bias_added"], 1)
                    e.wait_ge(s["mask_ready"], g + 1)
                    e.wait_ge(s["bias_added"], g + 1)
                    for x in range(E3):
                        k = g * E3 + x
                        e.wait_ge(s["y_psum"], k + 3)
                        if x:
                            e.wait_ge(s["y_added"], k + 2)
                        for t in range(GT):
                            xt = w.x[:, span(g, GW, t * D, D)]
                            last = e.scalar_tensor_tensor(xt, ps_y[x % 2][:, t * D:(t + 1) * D], mask[:, p, t, x:x + 1], xt,
                                                          ALU.mult, ALU.add)
                        last.then_inc(s["y_added"], 1)
                        if has_next and x == 0:
                            stats(g + 1, 1 - p)
                        if has_next and x == 1:
                            apply(g + 1, 1 - p)
                        if has_next and x == 4:
                            route(e, g + 1, 1 - p)
                    e.drain().then_inc(s["dve_done"], 1)
                stats(0, 0)
                apply(0, 0)
                route(e, 0, 0)
                over_groups(e, body)

            @block.gpsimd
            def _(e):
                give_credits(e, s["pool_done"])
                e.iota(iota[:, :], pattern=[[1, E3]], base=0, channel_multiplier=0, allow_small_or_imprecise_dtypes=True).then_inc(s["const"], 1)
                e.memset(prob[:, :, :, E3:PAD], -1.0).then_inc(s["pads"], 1)

                def body(g, p, has_next):
                    if has_next:
                        wait_groups_before(e, g + 1, s["dve_done"])
                        norm_rstd(e, s, w, g + 1, 1 - p)
                    e.drain().then_inc(s["pool_done"], 1)
                norm_rstd(e, s, w, 0, 0)
                over_groups(e, body)

            @block.tensor
            def _(e):
                give_credits(e, s["pe_done"])
                e.sem_inc(s["y_psum"], 2)
                e.wait_ge(s["weights"], 160)

                def transposes(g, p, first=False):
                    if not first:
                        e.wait_ge(s["bias_added"], g)
                    norm_transpose(e, s, w, g, p, ps_t)

                def router(g, p, first=False):
                    e.wait_ge(s["xt_ready"], g + 1)
                    if not first:
                        e.wait_ge(s["lg_ready"], g)
                    e.matmul(ps_m[0:R3, :], rw1[:, :], w.xt[:, p, :], start=True, stop=True).then_inc(s["r_psum"], 1)

                def router_logits(g, p):
                    e.wait_ge(s["r_ready"], g + 1)
                    for t in range(GT):
                        last = e.matmul(ps_m[:, t * E3:(t + 1) * E3], r_t[:, p, t * P:(t + 1) * P], rw2[:, :], start=True, stop=True)
                    last.then_inc(s["logit_psum"], 1)

                def bias_of(g, p):
                    e.wait_ge(s["mask_ready"], g + 1)
                    e.wait_ge(s["xt_ready"], g + 1)
                    for t in range(GT):
                        last = e.transpose(ps_t[0:E3, t * P:(t + 1) * P], mask[:, p, t, :], w.ident[:, :])
                    last.then_inc(s["mask_psum"], 1)
                    e.wait_ge(s["mask_t_ready"], g + 1)
                    for t in range(GT):
                        last = e.matmul(ps_t[:, t * D:(t + 1) * D], mask_t[:, p, t * P:(t + 1) * P], b3[:, :], start=True, stop=True)
                    last.then_inc(s["bias_psum"], 1)

                def layer1(g, p, x):
                    e.wait_ge(s["h1_ready"], g * E3 + x + 1)
                    e.matmul(ps_1[x % 2][:, :], w1[:, x, :], w.xt[:, p, :], start=True, stop=True).then_inc(s["h1_psum"], 1)

                def layer2(g, p, x):
                    e.wait_ge(s["h2_ready"], g * E3 + x + 1)
                    e.wait_ge(s["h1_ready"], g * E3 + x + 3)
                    e.matmul(ps_2[x % 2][:, :], w2[:, x, :], h1[:, x % 2, :], start=True, stop=True).then_inc(s["h2_psum"], 1)

                def layer3(g, p, x):
                    e.wait_ge(s["y_added"], g * E3 + x + 1)
                    e.wait_ge(s["h2_ready"], g * E3 + x + 3)
                    for t in range(GT):
                        last = e.matmul(ps_y[x % 2][:, t * D:(t + 1) * D], h2[:, x % 2, t * P:(t + 1) * P], w3[:, x, :], start=True, stop=True)
                    last.then_inc(s["y_psum"], 1)

                def body(g, p, has_next):
                    layer1(g, p, 0)
                    bias_of(g, p)
                    for x in range(E3):
                        if x + 1 < E3:
                            layer1(g, p, x + 1)
                        layer2(g, p, x)
                        if has_next and x == 3:
                            transposes(g + 1, 1 - p)
                        if has_next and x == 4:
                            router(g + 1, 1 - p)
                        if has_next and x == 5:
                            router_logits(g + 1, 1 - p)
                        if x:
                            layer3(g, p, x - 1)
                    layer3(g, p, E3 - 1)
                    e.drain().then_inc(s["pe_done"], 1)
                transposes(0, 0, True)
                router(0, 0, True)
                router_logits(0, 0)
                over_groups(e, body)

            @block.scalar
            def _(e):
                give_credits(e, s["act_done"])
                e.sem_inc(s["h1_ready"], 2)
                e.sem_inc(s["h2_ready"], 2)
                e.preload_act_table(ACT.Exp)
                e.wait_ge(s["weights"], 160)

                def copy_xt(g, p):
                    norm_copy(e, s, w, g, p, ps_t[:, :])

                def router(g, p):
                    e.wait_ge(s["r_psum"], g + 1)
                    e.activation(r_t[:, p, :], ps_m[0:R3, :], ACT.Relu, bias=rb1[:, 0:1]).then_inc(s["r_ready"], 1)

                def exps(g, p):
                    e.wait_ge(s["logit_ready"], g + 1)
                    e.activation(expo[:, p], logits[:, p], ACT.Exp).then_inc(s["exp_ready"], 1)
                    e.wait_ge(s["diff_ready"], g + 1)
                    e.activation(top[:, p], diff[:, p], ACT.Exp).then_inc(s["top_ready"], 1)

                def body(g, p, has_next):
                    for x in range(E3):
                        e.wait_ge(s["h1_psum"], g * E3 + x + 1)
                        e.wait_ge(s["h2_psum"], g * E3 + x + 1)
                        e.activation(h1[:, x % 2, :], ps_1[x % 2][:, :], ACT.Relu, bias=b1[:, x:x + 1]).then_inc(s["h1_ready"], 1)
                        if x == 0:
                            e.wait_ge(s["mask_psum"], g + 1)
                            e.activation(mask_t[:, p, :], ps_t[0:E3, :], ACT.Copy).then_inc(s["mask_t_ready"], 1)
                        e.wait_ge(s["h2_psum"], g * E3 + x + 3)
                        e.wait_ge(s["y_psum"], g * E3 + x + 1)
                        e.activation(h2[:, x % 2, :], ps_2[x % 2][:, :], ACT.Relu, bias=b2[:, x:x + 1]).then_inc(s["h2_ready"], 1)
                        if has_next and x == 3:
                            copy_xt(g + 1, 1 - p)
                        if has_next and x == 4:
                            router(g + 1, 1 - p)
                        if has_next and x == 5:
                            exps(g + 1, 1 - p)
                    e.drain().then_inc(s["act_done"], 1)
                e.sem_inc(s["h2_psum"], 2)
                copy_xt(0, 0)
                router(0, 0)
                exps(0, 0)
                over_groups(e, body)


def store(nc, w, out):
    with nc.Block() as block:
        @block.sync
        def _(e):
            e.dma_start(out.rearrange("b (h p) d -> p (b h) d", p=P),
                        w.x[:, :].rearrange("p (t d) -> p t d", d=D)).then_inc(w.stored, 16)
            e.wait_ge(w.stored, 16)


def four_layers(nc, a, out):
    with ExitStack() as c:
        w = Resident(nc, c)
        constants(nc, w)
        l0_gnn(nc, w, a)
        l0_ffn(nc, w, a)
        l1_gnn(nc, w, a)
        l1_ffn(nc, w, a)
        l2_gnn(nc, w, a)
        l2_ffn(nc, w, a)
        l3_gnn(nc, w, a)
        l3_ffn(nc, w, a)
        store(nc, w, out)


def laid_out(i):
    o = {k: np.asarray(v) for k, v in i.items()}
    o["adj_t"] = o["adj"].transpose(0, 2, 1)
    o["L0_gnn_Wt"] = o["L0_gnn_W"].T
    o["L0_ffn_b1"] = np.concatenate([o["L0_ffn_b1p"], o["L0_ffn_b1s"][None]]).reshape(EA, C0, P).transpose(2, 0, 1)
    o["L1_ffn_pack"] = np.concatenate([o["L1_ffn_W1"], o["L1_ffn_W2"].reshape(E1, C1, P, D).transpose(0, 2, 1, 3).reshape(E1, P, C1 * D),
                                       o["L1_ffn_b1"].reshape(E1, C1, P).transpose(0, 2, 1)], axis=2)
    o["L2_ffn_hl_w_t"] = o["L2_ffn_hl_w"].reshape(D, D).T
    o["L2_ffn_wq_t"] = o["L2_ffn_wq"].transpose(0, 3, 1, 2)
    o["L2_ffn_wk_t"] = o["L2_ffn_wk"].transpose(0, 2, 1)
    o["L2_ffn_wv_t"] = o["L2_ffn_wv"].transpose(0, 2, 1)
    o["L2_ffn_gate_w_t"] = o["L2_ffn_gate_w"].transpose(2, 0, 1)
    o["L2_ffn_fc1_t"] = o["L2_ffn_fc1_w"].T
    o["L2_ffn_fc2_t"] = o["L2_ffn_fc2_w"].T
    o["L2_ffn_fgate_t"] = o["L2_ffn_fgate_w"].T
    o["L3_ffn_b1_t"] = o["L3_ffn_expert_b1"].T
    o["L3_ffn_b2_t"] = o["L3_ffn_expert_b2"].T
    return {k: np.ascontiguousarray(v) for k, v in o.items() if k not in LAID_OUT_ONLY}


LAID_OUT_ONLY = ("L0_gnn_W", "L0_ffn_b1p", "L0_ffn_b1s", "L1_ffn_W1", "L1_ffn_W2", "L1_ffn_b1", "L2_ffn_hl_w", "L2_ffn_wq", "L2_ffn_wk",
                 "L2_ffn_wv", "L2_ffn_gate_w", "L2_ffn_fc1_w", "L2_ffn_fc2_w", "L2_ffn_fgate_w", "L3_ffn_expert_b1", "L3_ffn_expert_b2")


def kernel(**inputs):
    import concourse.bacc as bacc
    from concourse.bass_utils import run_bass_kernel_spmd

    nc = bacc.Bacc("TRN2", target_bir_lowering=False, num_devices=1)
    arrays, a = {}, {}
    for name, array in laid_out(inputs).items():
        arrays[f"in_{name}"] = array
        a[name] = nc.dram_tensor(f"in_{name}", array.shape, mybir.dt.from_np(array.dtype), kind="ExternalInput").ap()
    out = nc.dram_tensor("out", (B, N, D), F32, kind="ExternalOutput").ap()
    four_layers(nc, a, out)
    r = run_bass_kernel_spmd(nc, [arrays], core_ids=[0])
    return r.results[0]["out"]
```

```python
from contextlib import ExitStack

import numpy as np
import concourse.bass as bass
from concourse import mybir

F32 = mybir.dt.float32
I32 = mybir.dt.int32
U32 = mybir.dt.uint32
ALU = mybir.AluOpType
ACT = mybir.ActivationFunctionType
AX = mybir.AxisListType
P = 128
D = 128
B, N = 32, 256
TILES = B * N // P
GT = 4
GROUPS = TILES // GT
GW = GT * D
LN_EPS = 1e-5


def span(g, width, start=0, size=None):
    return bass.ds(g * width + start, width if size is None else size)


def named_semaphores(nc, stack, phase, names):
    handles = {n: stack.enter_context(nc.semaphore(f"{phase}_{n}")) for n in names.split()}
    stack.callback(zero_semaphores, nc, list(handles.values()))
    return handles


def zero_semaphores(nc, handles):
    with nc.Block() as block:
        @block.gpsimd
        def _(e):
            for h in handles:
                e.sem_clear(h)


NORM_SEMS = "stats_done var_ready veps_ready rstd_ready xn_ready xt_psum xt_ready"
DONE_SEMS = "pe_done act_done dve_done pool_done"


def give_credits(e, done):
    e.sem_inc(done, 2)


def wait_groups_before(e, g, *dones):
    for d in dones:
        e.wait_ge(d, g + 1)


def wait_apart(e, w, semaphore, value):
    e.wait_ge(semaphore, value)
    e.sem_inc(w.passed, 1)


class Resident:

    def __init__(self, nc, c):
        def sb(n, shape):
            return c.enter_context(nc.sbuf_tensor(n, shape, F32))
        self.passed = c.enter_context(nc.semaphore("passed"))
        self.stored = c.enter_context(nc.semaphore("stored"))
        self.scratch_stored = c.enter_context(nc.semaphore("scratch_stored"))
        self.x = sb("x", [P, TILES * D])
        self.adj = sb("adj", [P, TILES * N])
        self.xn = sb("xn", [P, 2, GT, D])
        self.xt = sb("xt", [P, 2, GW])
        self.stats = sb("stats", [P, 2, GT, 6])
        self.meanvar = sb("meanvar", [P, 2, GT, 2])
        self.veps = sb("veps", [P, 2, GT])
        self.rstd = sb("rstd", [P, 2, GT])
        self.ident = sb("ident", [P, P])
        self.ones = sb("ones", [P, P])
        self.minus_half = sb("minus_half", [P, 64])
        self.ln_eps = sb("ln_eps", [P, 16])


def norm_stats(e, s, w, g, p):
    for t in range(GT):
        last = e.bn_stats(w.stats[:, p, t, :], w.x[:, span(g, GW, t * D, D)])
    last.then_inc(s["stats_done"], 1)
    wait_apart(e, w, s["stats_done"], g + 1)
    for t in range(GT):
        last = e.bn_aggr(w.meanvar[:, p, t, :], w.stats[:, p, t, :])
    last.then_inc(s["var_ready"], 1)


def norm_rstd(e, s, w, g, p):
    e.wait_ge(s["var_ready"], g + 1)
    e.tensor_tensor(w.veps[:, p, :], w.meanvar[:, p, :, 1], w.ln_eps[:, 0:GT], ALU.add).then_inc(s["veps_ready"], 1)
    e.wait_ge(s["veps_ready"], g + 1)
    e.tensor_tensor(w.rstd[:, p, :], w.veps[:, p, :], w.minus_half[:, 0:GT], ALU.pow).then_inc(s["rstd_ready"], 1)


def norm_apply(e, s, w, g, p):
    e.wait_ge(s["rstd_ready"], g + 1)
    for t in range(GT):
        last = e.tensor_scalar(w.xn[:, p, t, :], w.x[:, span(g, GW, t * D, D)], w.meanvar[:, p, t, 0:1],
                               w.rstd[:, p, t:t + 1], ALU.subtract, ALU.mult)
    last.then_inc(s["xn_ready"], 1)


def norm_transpose(e, s, w, g, p, out):
    e.wait_ge(s["xn_ready"], g + 1)
    for t in range(GT):
        last = e.transpose(out[:, t * P:(t + 1) * P], w.xn[:, p, t, :], w.ident[:, :])
    last.then_inc(s["xt_psum"], 1)


def norm_copy(e, s, w, g, p, src):
    e.wait_ge(s["xt_psum"], g + 1)
    e.activation(w.xt[:, p, :], src, ACT.Copy).then_inc(s["xt_ready"], 1)


def over_groups(e, body):
    with e.Fori(0, GROUPS - 2, 2) as i:
        body(i, 0, True)
        body(i + 1, 1, True)
    body(GROUPS - 2, 0, True)
    body(GROUPS - 1, 1, False)


def over_groups_lagged(e, body):
    body(0, 0, False, True)
    with e.Fori(0, GROUPS // 2 - 1) as i:
        body(i * 2 + 1, 1, True, True)
        body(i * 2 + 2, 0, True, True)
    body(GROUPS - 1, 1, True, False)


def over_groups_ahead(e, body):
    body(0, 0, False, True, True)
    with e.Fori(0, GROUPS // 2 - 2) as i:
        body(i * 2 + 1, 1, True, True, True)
        body(i * 2 + 2, 0, True, True, True)
    body(GROUPS - 3, 1, True, True, True)
    body(GROUPS - 2, 0, True, True, False)
    body(GROUPS - 1, 1, True, False, False)
NEG_MASK = 9e15
KEY_MASK = 1e30
BIG = 3e38


def constants(nc, w):
    with ExitStack() as c:
        s = named_semaphores(nc, c, "const", "ones zero ident")
        with nc.Block() as block:
            @block.gpsimd
            def _(e):
                e.memset(w.ident[:, :], 0.0).then_inc(s["zero"], 1)
                e.memset(w.ones[:, :], 1.0).then_inc(s["ones"], 1)
                e.memset(w.minus_half[:, :], -0.5).then_inc(s["ones"], 1)
                e.memset(w.ln_eps[:, :], LN_EPS).then_inc(s["ones"], 1)
                e.wait_ge(s["zero"], 1)
                e.affine_select(out=w.ident[:, :], in_=w.ident[:, :], compare_op=ALU.not_equal, fill=1.0,
                                base=0, pattern=[[-1, P]], channel_multiplier=1).then_inc(s["ident"], 1)
                e.wait_ge(s["ident"], 1)
                e.wait_ge(s["ones"], 3)

def l0_gnn(nc, w, a):
    with ExitStack() as c:
        sb = lambda n, shape: c.enter_context(nc.sbuf_tensor("l0g_" + n, shape, F32))
        ps = lambda n, shape: c.enter_context(nc.psum_tensor("l0g_" + n, shape, F32))
        adj_t = sb("adj_t", [P, 2, 2, 2, N])
        deg_is0 = sb("deg_is0", [P, 2, GT])
        deg = sb("deg", [P, 2, GT])
        dinv = sb("dinv", [P, 2, GT])
        alpha_deg = sb("alpha_deg", [P, 2, GT])
        alpha = sb("alpha", [P, 1])
        alpha_eff = sb("alpha_eff", [P, 1])
        w_t = sb("w_t", [D, D])
        bias = sb("bias", [P, D])
        xd = sb("xd", [P, 2, GT, D])
        xb = sb("xb", [P, 2, GT, D])
        h_t = sb("h_t", [P, 2, GW])
        ps_t = ps("ps_t", [P, 2, 512])
        ps_deg = ps("ps_deg", [P, 2, 512])
        ps_h = ps("ps_h", [P, 2, 512])
        ps_y = ps("ps_y", [P, 2, 512])
        s = named_semaphores(nc, c, "l0g", NORM_SEMS + " weights alpha x_loaded0 x_loaded1 adj_loaded0 adj_loaded1 deg_psum is0 deg_ready"
                             " dinv_ready alpha_deg_ready xd_ready xb_ready h_psum h_ready y_psum x_done")
        x_loaded = [s["x_loaded0"], s["x_loaded1"]]
        adj_loaded = [s["adj_loaded0"], s["adj_loaded1"]]
        x_dram = a["x"].rearrange("b (h p) d -> p (b h) d", p=P)
        adj_dram = a["adj"].rearrange("b (h p) m -> p (b h) m", p=P)
        adj_t_dram = a["adj_t"].rearrange("b (h p) n -> p b h n", p=P)

        def wait_x(e, g, p):
            e.wait_ge(x_loaded[p], g * 8 + (16 if p == 0 else 8))

        def wait_adj(e, g, p):
            e.wait_ge(adj_loaded[p], g * 16 + (32 if p == 0 else 16))

        with nc.Block() as block:
            @block.sync
            def _(e):
                def load_x(g, p):
                    if not isinstance(g, int) or g >= 2:
                        e.wait_ge(s["var_ready"], g - 1)
                        e.wait_ge(s["xb_ready"], g - 1)
                    e.dma_start(w.x[:, span(g, GW)].rearrange("p (t d) -> p t d", d=D),
                                x_dram[:, bass.ds(g * GT, GT), :]).then_inc(x_loaded[p], 16)

                def load_adj(g, p):
                    if not isinstance(g, int) or g >= 2:
                        e.wait_ge(s["h_psum"], g - 1)
                    e.dma_start(adj_t[:, p], adj_t_dram[:, bass.ds(g * 2, 2)]).then_inc(adj_loaded[p], 16)
                    e.dma_start(w.adj[:, span(g, GT * N)].rearrange("p (t m) -> p t m", m=N),
                                adj_dram[:, bass.ds(g * GT, GT), :]).then_inc(adj_loaded[p], 16)

                def body(g, p, has_prev, has_next, has_second):
                    if has_next:
                        load_adj(g + 1, 1 - p)
                    if has_second:
                        load_x(g + 2, p)
                load_x(0, 0)
                load_adj(0, 0)
                load_x(1, 1)
                e.dma_start(w_t[:, :], a["L0_gnn_Wt"]).then_inc(s["weights"], 16)
                e.dma_start(bias[:, :], a["L0_gnn_b"].partition_broadcast(P)).then_inc(s["weights"], 16)
                e.dma_start(alpha[:, :], a["L0_gnn_alpha"].partition_broadcast(P)).then_inc(s["weights"], 16)
                over_groups_ahead(e, body)

            @block.vector
            def _(e):
                def stats(g, p):
                    wait_x(e, g, p)
                    norm_stats(e, s, w, g, p)

                def degrees(g, p):
                    e.wait_ge(s["deg_psum"], g + 1)
                    e.tensor_scalar(deg_is0[:, p, :], ps_deg[:, p, 0:GT], 0.0, None, ALU.is_equal).then_inc(s["is0"], 1)
                    e.wait_ge(s["is0"], g + 1)
                    e.tensor_tensor(deg[:, p, :], ps_deg[:, p, 0:GT], deg_is0[:, p, :], ALU.add).then_inc(s["deg_ready"], 1)
                    e.wait_ge(s["deg_ready"], g + 1)
                    e.tensor_scalar(alpha_deg[:, p, :], deg[:, p, :], alpha_eff[:, 0:1], None, ALU.mult).then_inc(s["alpha_deg_ready"], 1)
                    e.wait_ge(s["alpha_deg_ready"], g + 1)
                    for t in range(GT):
                        diag = adj_t[:, p, t // 2, t % 2, (t % 2) * P:(t % 2 + 1) * P]
                        e.scalar_tensor_tensor(diag, w.ident[:, :], alpha_deg[:, p, t:t + 1], diag, ALU.mult, ALU.add)

                def scale(g, p):
                    e.wait_ge(s["dinv_ready"], g + 1)
                    if not isinstance(g, int) or g >= 2:
                        e.wait_ge(s["h_psum"], g - 1)
                    for t in range(GT):
                        last = e.tensor_scalar(xd[:, p, t, :], w.xn[:, p, t, :], dinv[:, p, t:t + 1], None, ALU.mult)
                    last.then_inc(s["xd_ready"], 1)

                def finish(g, p):
                    e.wait_ge(s["xb_ready"], g + 1)
                    e.wait_ge(s["y_psum"], g + 1)
                    for t in range(GT):
                        last = e.scalar_tensor_tensor(w.x[:, span(g, GW, t * D, D)], ps_y[:, p, t * D:(t + 1) * D],
                                                      dinv[:, p, t:t + 1], xb[:, p, t, :], ALU.mult, ALU.add)
                    last.then_inc(s["x_done"], 1)

                def front(g, p):
                    norm_apply(e, s, w, g, p)
                    degrees(g, p)
                    e.wait_ge(s["xn_ready"], g + 1)
                    scale(g, p)

                def body(g, p, has_prev, has_next, has_second):
                    if has_second:
                        stats(g + 2, p)
                    if has_next:
                        front(g + 1, 1 - p)
                    finish(g, p)
                stats(0, 0)
                stats(1, 1)
                e.wait_ge(s["weights"], 48)
                e.tensor_scalar(alpha_eff[:, :], alpha[:, :], 1e-10, None, ALU.max).then_inc(s["alpha"], 1)
                e.wait_ge(s["alpha"], 1)
                front(0, 0)
                over_groups_ahead(e, body)

            @block.gpsimd
            def _(e):
                def front(g, p):
                    e.wait_ge(s["deg_ready"], g + 1)
                    e.tensor_tensor(dinv[:, p, :], deg[:, p, :], w.minus_half[:, 0:GT], ALU.pow).then_inc(s["dinv_ready"], 1)
                    wait_x(e, g, p)
                    for t in range(GT):
                        last = e.tensor_tensor(xb[:, p, t, :], w.x[:, span(g, GW, t * D, D)], bias[:, :], ALU.add)
                    last.then_inc(s["xb_ready"], 1)

                def body(g, p, has_prev, has_next, has_second):
                    if has_second:
                        norm_rstd(e, s, w, g + 2, p)
                    if has_next:
                        front(g + 1, 1 - p)
                e.wait_ge(s["weights"], 48)
                norm_rstd(e, s, w, 0, 0)
                norm_rstd(e, s, w, 1, 1)
                front(0, 0)
                over_groups_ahead(e, body)

            @block.tensor
            def _(e):
                def degrees(g, p):
                    if not isinstance(g, int) or g >= 2:
                        e.wait_ge(s["deg_ready"], g - 1)
                    wait_adj(e, g, p)
                    for t in range(GT):
                        for m in range(2):
                            last = e.matmul(ps_deg[:, p, t:t + 1], adj_t[:, p, t // 2, m, (t % 2) * P:(t % 2 + 1) * P],
                                            w.ones[:, 0:1], start=m == 0, stop=m == 1)
                    last.then_inc(s["deg_psum"], 1)

                def body(g, p, has_prev, has_next):
                    if not isinstance(g, int) or g >= 2:
                        e.wait_ge(s["h_ready"], g - 1)
                    e.wait_ge(s["xd_ready"], g + 1)
                    for b in range(2):
                        for m in range(2):
                            last = e.matmul(ps_h[:, p, b * N:(b + 1) * N], xd[:, p, 2 * b + m, :], adj_t[:, p, b, m, :],
                                            start=m == 0, stop=m == 1)
                    last.then_inc(s["h_psum"], 1)
                    if has_next:
                        degrees(g + 1, 1 - p)
                    if not isinstance(g, int) or g >= 2:
                        e.wait_ge(s["x_done"], g - 1)
                    e.wait_ge(s["h_ready"], g + 1)
                    for t in range(GT):
                        last = e.matmul(ps_y[:, p, t * D:(t + 1) * D], h_t[:, p, t * P:(t + 1) * P], w_t[:, :],
                                        start=True, stop=True)
                    last.then_inc(s["y_psum"], 1)
                degrees(0, 0)
                e.wait_ge(s["weights"], 48)
                over_groups_lagged(e, body)

            @block.scalar
            def _(e):
                def body(g, p, has_next):
                    e.wait_ge(s["h_psum"], g + 1)
                    e.activation(h_t[:, p, :], ps_h[:, p, :], ACT.Copy).then_inc(s["h_ready"], 1)
                over_groups(e, body)


E0 = 8
EA = E0 + 1
F0 = 512
C0 = F0 // P


def l0_ffn(nc, w, a):
    with ExitStack() as c:
        sb = lambda n, shape, dt=F32: c.enter_context(nc.sbuf_tensor("l0f_" + n, shape, dt))
        ps = lambda n, shape: c.enter_context(nc.psum_tensor("l0f_" + n, shape, F32))
        w1 = sb("w1", [P, EA, F0])
        w2 = sb("w2", [P, EA, C0, D])
        b1 = sb("b1", [P, EA, C0])
        b2 = sb("b2", [EA, D])
        wr = sb("wr", [P, E0])
        iota = sb("iota", [P, E0])
        logits = sb("logits", [P, 2, GT, E0])
        row_max = sb("row_max", [P, 2, GT])
        expo = sb("expo", [P, 2, GT, E0])
        best = sb("best", [P, 2, GT, 8])
        best_at = sb("best_at", [P, 2, GT, 8], U32)
        best_f = sb("best_f", [P, 2, GT, 8])
        total = sb("total", [P, 2, GT])
        inv_total = sb("inv_total", [P, 2, GT])
        weight = sb("weight", [P, 2, GT, 2])
        hit = sb("hit", [P, 2, 2, GT, E0])
        mask = sb("mask", [P, 2, GT, EA])
        mask_t = sb("mask_t", [EA, 2, GW])
        h = sb("h", [P, 2, C0, GW])
        ps_h = ps("ps_h", [P, 4, 512])
        ps_y = ps("ps_y", [P, 2, 512])
        ps_t = ps("ps_t", [P, 512])
        ps_m = ps("ps_m", [P, 512])
        s = named_semaphores(nc, c, "l0f", NORM_SEMS + " " + DONE_SEMS + " router experts const iota_ready mask_ones logit_psum max_ready logit_ready exp_ready"
                             " chain mask_ready mask_psum mask_t_ready bias_psum bias_added h_psum h_ready y_psum y_added")
        HC = EA * C0
        with nc.Block() as block:
            @block.sync
            def _(e):
                e.dma_start(wr[:, :], a["L0_ffn_Wr"]).then_inc(s["router"], 16)
                e.dma_start(b1[:, :, :], a["L0_ffn_b1"]).then_inc(s["router"], 16)
                e.dma_start(b2[0:E0, :], a["L0_ffn_b2p"]).then_inc(s["router"], 16)
                e.dma_start(b2[E0:EA, :], a["L0_ffn_b2s"].rearrange("(a d) -> a d", a=1)).then_inc(s["router"], 16)
                e.dma_start(w1[:, 0:E0, :], a["L0_ffn_W1p"].rearrange("e d f -> d e f")).then_inc(s["experts"], 16)
                e.dma_start(w1[:, E0, :], a["L0_ffn_W1s"]).then_inc(s["experts"], 16)
                e.dma_start(w2[:, 0:E0].rearrange("p e c d -> p (e c) d"),
                            a["L0_ffn_W2p"].rearrange("e (c p) d -> p (e c) d", p=P)).then_inc(s["experts"], 16)
                e.dma_start(w2[:, E0], a["L0_ffn_W2s"].rearrange("(c p) d -> p c d", p=P)).then_inc(s["experts"], 16)

            def route(e, g, p):
                n = 5
                at = g * n
                e.wait_ge(s["logit_psum"], g + 1)
                lg = ps_m[:, p * 64:p * 64 + GT * E0].rearrange("p (t e) -> p t e", e=E0)
                e.tensor_reduce(row_max[:, p, :], lg, AX.X, ALU.max).then_inc(s["max_ready"], 1)
                e.wait_ge(s["max_ready"], g + 1)
                e.tensor_tensor(logits[:, p], lg, row_max[:, p, :].unsqueeze(2).broadcast_to([P, GT, E0]),
                                ALU.subtract).then_inc(s["logit_ready"], 1)
                wait_apart(e, w, s["exp_ready"], g + 1)
                for t in range(GT):
                    last = e.max(best[:, p, t, :], expo[:, p, t, :])
                last.then_inc(s["chain"], 1)
                wait_apart(e, w, s["chain"], at + 1)
                for t in range(GT):
                    e.max_index(best_at[:, p, t, :], best[:, p, t, :], expo[:, p, t, :])
                e.tensor_tensor(total[:, p, :], best[:, p, :, 0], best[:, p, :, 1], ALU.add).then_inc(s["chain"], 1)
                e.wait_ge(s["chain"], at + 2)
                e.reciprocal(inv_total[:, p, :], total[:, p, :])
                e.tensor_copy(best_f[:, p], best_at[:, p]).then_inc(s["chain"], 1)
                e.wait_ge(s["chain"], at + 3)
                e.tensor_tensor(weight[:, p], best[:, p, :, 0:2], inv_total[:, p, :].unsqueeze(2).broadcast_to([P, GT, 2]),
                                ALU.mult).then_inc(s["chain"], 1)
                e.wait_ge(s["chain"], at + 4)
                for t in range(GT):
                    for k in range(2):
                        last = e.tensor_scalar(hit[:, p, k, t, :], iota[:, :], best_f[:, p, t, k:k + 1],
                                               weight[:, p, t, k:k + 1], ALU.is_equal, ALU.mult)
                last.then_inc(s["chain"], 1)
                e.wait_ge(s["chain"], at + 5)
                e.tensor_tensor(mask[:, p, :, 0:E0], hit[:, p, 0], hit[:, p, 1], ALU.add).then_inc(s["mask_ready"], 1)

            @block.vector
            def _(e):
                give_credits(e, s["dve_done"])
                e.sem_inc(s["y_added"], 2)
                e.wait_ge(s["const"], 1)

                def stats(g, p):
                    wait_groups_before(e, g, s["pool_done"])
                    norm_stats(e, s, w, g, p)

                def apply(g, p):
                    wait_groups_before(e, g, s["pe_done"])
                    norm_apply(e, s, w, g, p)

                def body(g, p, has_next):
                    e.wait_ge(s["bias_psum"], g + 1)
                    xg = w.x[:, span(g, GW)]
                    e.tensor_tensor(xg, xg, ps_t[:, :], ALU.add).then_inc(s["bias_added"], 1)
                    e.wait_ge(s["mask_ready"], g + 1)
                    e.wait_ge(s["bias_added"], g + 1)
                    for x in range(EA):
                        k = g * EA + x
                        q = (p + x) % 2
                        e.wait_ge(s["y_psum"], k + 3)
                        if x:
                            e.wait_ge(s["y_added"], k + 2)
                        for t in range(GT):
                            xt = w.x[:, span(g, GW, t * D, D)]
                            last = e.scalar_tensor_tensor(xt, ps_y[:, q, t * D:(t + 1) * D], mask[:, p, t, x:x + 1], xt,
                                                          ALU.mult, ALU.add)
                        last.then_inc(s["y_added"], 1)
                        if has_next and x == 0:
                            stats(g + 1, 1 - p)
                        if has_next and x == 1:
                            apply(g + 1, 1 - p)
                        if has_next and x == 4:
                            route(e, g + 1, 1 - p)
                    e.drain().then_inc(s["dve_done"], 1)
                stats(0, 0)
                apply(0, 0)
                route(e, 0, 0)
                over_groups(e, body)

            @block.gpsimd
            def _(e):
                give_credits(e, s["pool_done"])
                e.iota(iota[:, :], pattern=[[1, E0]], base=0, channel_multiplier=0, allow_small_or_imprecise_dtypes=True).then_inc(s["iota_ready"], 1)
                e.memset(mask[:, :, :, :], 1.0).then_inc(s["mask_ones"], 1)
                e.wait_ge(s["iota_ready"], 1)
                e.wait_ge(s["mask_ones"], 1)
                e.sem_inc(s["const"], 1)

                def body(g, p, has_next):
                    if has_next:
                        wait_groups_before(e, g + 1, s["dve_done"])
                        norm_rstd(e, s, w, g + 1, 1 - p)
                    e.drain().then_inc(s["pool_done"], 1)
                norm_rstd(e, s, w, 0, 0)
                over_groups(e, body)

            @block.tensor
            def _(e):
                give_credits(e, s["pe_done"])
                e.sem_inc(s["y_psum"], 2)
                e.wait_ge(s["router"], 64)

                def transposes(g, p):
                    e.wait_ge(s["bias_added"], g)
                    norm_transpose(e, s, w, g, p, ps_t)

                def logits_of(g, p):
                    e.wait_ge(s["xt_ready"], g + 1)
                    for t in range(GT):
                        last = e.matmul(ps_m[:, p * 64 + t * E0:p * 64 + (t + 1) * E0], w.xt[:, p, t * P:(t + 1) * P], wr[:, :],
                                        start=True, stop=True)
                    last.then_inc(s["logit_psum"], 1)

                def bias_of(g, p):
                    e.wait_ge(s["mask_ready"], g + 1)
                    e.wait_ge(s["xt_ready"], g + 1)
                    for t in range(GT):
                        last = e.transpose(ps_t[0:EA, t * P:(t + 1) * P], mask[:, p, t, :], w.ident[:, :])
                    last.then_inc(s["mask_psum"], 1)
                    e.wait_ge(s["mask_t_ready"], g + 1)
                    for t in range(GT):
                        last = e.matmul(ps_t[:, t * D:(t + 1) * D], mask_t[:, p, t * P:(t + 1) * P], b2[:, :], start=True, stop=True)
                    last.then_inc(s["bias_psum"], 1)

                def hidden(g, p, x):
                    for ch in range(C0):
                        n = g * HC + x * C0 + ch
                        e.wait_ge(s["h_ready"], n + 1)
                        e.matmul(ps_h[:, ch, :], w1[:, x, ch * P:(ch + 1) * P], w.xt[:, p, :],
                                 start=True, stop=True).then_inc(s["h_psum"], 1)

                def output(g, p, x):
                    k = g * EA + x
                    q = (p + x) % 2
                    e.wait_ge(s["y_added"], k + 1)
                    e.wait_ge(s["h_ready"], g * HC + x * C0 + C0 + 4)
                    for t in range(GT):
                        for ch in range(C0):
                            last = e.matmul(ps_y[:, q, t * D:(t + 1) * D], h[:, q, ch, t * P:(t + 1) * P], w2[:, x, ch, :],
                                            start=ch == 0, stop=ch == C0 - 1)
                    last.then_inc(s["y_psum"], 1)

                def body(g, p, has_next):
                    hidden(g, p, 0)
                    bias_of(g, p)
                    for x in range(EA):
                        if x + 1 < EA:
                            hidden(g, p, x + 1)
                        if has_next and x == 2:
                            transposes(g + 1, 1 - p)
                        if has_next and x == 3:
                            logits_of(g + 1, 1 - p)
                        output(g, p, x)
                    e.drain().then_inc(s["pe_done"], 1)
                norm_transpose(e, s, w, 0, 0, ps_t)
                logits_of(0, 0)
                e.wait_ge(s["experts"], 64)
                over_groups(e, body)

            @block.scalar
            def _(e):
                give_credits(e, s["act_done"])
                e.sem_inc(s["h_ready"], 4)
                e.wait_ge(s["router"], 64)

                def copy_xt(g, p):
                    norm_copy(e, s, w, g, p, ps_t[:, :])

                def exps(g, p):
                    e.wait_ge(s["logit_ready"], g + 1)
                    e.activation(expo[:, p], logits[:, p], ACT.Exp).then_inc(s["exp_ready"], 1)

                def body(g, p, has_next):
                    for x in range(EA):
                        q = (p + x) % 2
                        e.wait_ge(s["y_psum"], g * EA + x + 1)
                        for ch in range(C0):
                            e.wait_ge(s["h_psum"], g * HC + x * C0 + ch + 1)
                            e.activation(h[:, q, ch, :], ps_h[:, ch, :], ACT.Gelu, bias=b1[:, x, ch:ch + 1]).then_inc(s["h_ready"], 1)
                        if x == 0:
                            e.wait_ge(s["mask_psum"], g + 1)
                            e.activation(mask_t[:, p, :], ps_t[0:EA, :], ACT.Copy).then_inc(s["mask_t_ready"], 1)
                        if has_next and x == 3:
                            copy_xt(g + 1, 1 - p)
                        if has_next and x == 5:
                            exps(g + 1, 1 - p)
                    e.drain().then_inc(s["act_done"], 1)
                copy_xt(0, 0)
                exps(0, 0)
                over_groups(e, body)


H1 = 8
HD1 = D // H1
HALF = 4
U1 = GT * H1 // HALF
VW = 32


def l1_gnn(nc, w, a):
    with ExitStack() as c:
        sb = lambda n, shape, dt=F32: c.enter_context(nc.sbuf_tensor("l1g_" + n, shape, dt))
        ps = lambda n, shape: c.enter_context(nc.psum_tensor("l1g_" + n, shape, F32))
        wq = sb("wq", [P, D]); wk = sb("wk", [P, D]); wv = sb("wv", [P, D]); wo = sb("wo", [P, D])
        bq = sb("bq", [P, 1]); bk = sb("bk", [P, 1]); bq_scaled = sb("bq_scaled", [P, 1])
        bv = sb("bv", [P, D]); bo = sb("bo", [P, D])
        q_t = sb("q_t", [P, 2, GW])
        k_t = sb("k_t", [P, 2, GW])
        k_diag = sb("k_diag", [P, 2, 2, H1, N])
        v1 = sb("v1", [P, 2, GT, H1, VW])
        not_adj = sb("not_adj", [P, 2, GT, N])
        scores = sb("scores", [P, 2, HALF, N])
        row_min = sb("row_min", [P, 2, HALF])
        probs = sb("probs", [P, 2, HALF, N])
        probs_t = sb("probs_t", [P, 2, 2, HALF, P])
        raw_t = sb("raw_t", [P, P])
        inv_sum = sb("inv_sum", [P, HALF])
        o = sb("o", [P, 2, GT, D])
        o_t = sb("o_t", [P, 2, GW])
        xb = sb("xb", [P, 2, GT, D])
        ps_s = ps("ps_s", [P, 2, HALF, N])
        ps_t = ps("ps_t", [P, 2, HALF, P])
        ps_o = ps("ps_o", [P, 2, 2 * P])
        ps_m = ps("ps_m", [P, 512])
        s = named_semaphores(nc, c, "l1g", NORM_SEMS + " " + DONE_SEMS + " weights const zeroed bq_scaled q_psum q_ready k_psum k_ready k_diag0 k_diag1"
                             " v_psum v_ready mask_ready s_psum masked exp_ready t_psum t0_ready t1_ready pv_psum raw_copied raw_turned inv_ready o_ready"
                             " ot_psum ot_ready y_psum xb_ready")
        k_loaded = [s["k_diag0"], s["k_diag1"]]
        with nc.Block() as block:
            @block.sync
            def _(e):
                for dst, src in ((wq, "Wq"), (wk, "Wk"), (wv, "Wv"), (wo, "Wo")):
                    e.dma_start(dst[:, :], a["L1_gnn_" + src]).then_inc(s["weights"], 16)
                for dst, src in ((bq, "bq"), (bk, "bk")):
                    e.dma_start(dst[:, :], a["L1_gnn_" + src].rearrange("(p a) -> p a", a=1)).then_inc(s["weights"], 16)
                for dst, src in ((bv, "bv"), (bo, "bo")):
                    e.dma_start(dst[:, :], a["L1_gnn_" + src].partition_broadcast(P)).then_inc(s["weights"], 16)
                e.wait_ge(s["zeroed"], 1)

                def diag(g, p):
                    wait_groups_before(e, g, s["pe_done"])
                    e.wait_ge(s["k_ready"], g + 1)
                    for hh in range(H1):
                        r = slice(hh * HD1, (hh + 1) * HD1)
                        e.dma_start(k_diag[r, p, :, hh, :], k_t[r, p, :].rearrange("p (b n) -> p b n", b=2)).then_inc(k_loaded[p], 16)

                def body(g, p, has_next):
                    if has_next:
                        diag(g + 1, 1 - p)
                diag(0, 0)
                over_groups(e, body)

            @block.gpsimd
            def _(e):
                give_credits(e, s["pool_done"])
                e.memset(k_diag[:, :, :, :, :], 0.0).then_inc(s["zeroed"], 1)
                e.memset(v1[:, :, :, :, HD1 + 1:VW], 0.0)
                e.memset(v1[:, :, :, :, HD1:HD1 + 1], 1.0).then_inc(s["const"], 1)
                e.wait_ge(s["weights"], 128)

                def body(g, p, has_next):
                    if has_next:
                        wait_groups_before(e, g, s["dve_done"])
                        norm_rstd(e, s, w, g + 1, 1 - p)
                    wait_groups_before(e, g, s["dve_done"])
                    for t in range(GT):
                        last = e.tensor_tensor(xb[:, p, t, :], w.x[:, span(g, GW, t * D, D)], bo[:, :], ALU.add)
                    last.then_inc(s["xb_ready"], 1)
                    e.drain().then_inc(s["pool_done"], 1)
                norm_rstd(e, s, w, 0, 0)
                over_groups(e, body)

            @block.vector
            def _(e):
                give_credits(e, s["dve_done"])
                e.sem_inc(s["masked"], 2)
                e.sem_inc(s["t0_ready"], 1)
                e.wait_ge(s["weights"], 128)
                e.wait_ge(s["const"], 1)
                e.tensor_scalar(bq_scaled[:, :], bq[:, :], -0.25, None, ALU.mult).then_inc(s["bq_scaled"], 1)

                def stats(g, p):
                    wait_groups_before(e, g, s["pool_done"])
                    norm_stats(e, s, w, g, p)

                def apply(g, p):
                    wait_groups_before(e, g, s["pe_done"])
                    norm_apply(e, s, w, g, p)

                def edges(g, p):
                    e.tensor_scalar(not_adj[:, p], w.adj[:, span(g, GT * N)].rearrange("p (t n) -> p t n", n=N), 0.0, NEG_MASK,
                                    ALU.is_le, ALU.mult).then_inc(s["mask_ready"], 1)

                def values(g, p):
                    e.wait_ge(s["v_psum"], g + 1)
                    e.tensor_tensor(v1[:, p, :, :, 0:HD1].rearrange("p t h d -> p (t h) d"),
                                    ps_m[:, :].rearrange("p (x d) -> p x d", d=HD1),
                                    bv[:, :].rearrange("p (h d) -> p h d", d=HD1).unsqueeze(1).broadcast_to([P, GT, H1, HD1]),
                                    ALU.add).then_inc(s["v_ready"], 1)

                def mask_unit(g, p, u):
                    n = g * U1 + u
                    q = u % 2
                    if u == 0:
                        e.wait_ge(s["mask_ready"], g + 1)
                    e.wait_ge(s["exp_ready"], n + 1)
                    wait_apart(e, w, s["s_psum"], n + 1)
                    for i in range(HALF):
                        last = e.tensor_tensor_reduce(scores[:, q, i, :], ps_s[:, q, i, :], not_adj[:, p, u // 2, :], 1.0, BIG,
                                                      ALU.add, ALU.min, row_min[:, q, i:i + 1])
                    last.then_inc(s["masked"], 1)

                def copy_t(g, p, u):
                    n = g * U1 + u
                    e.wait_ge(s["pv_psum"], n + 1)
                    e.wait_ge(s["t_psum"], 2 * n + 1 + 4)
                    e.tensor_copy(probs_t[:, u % 2, 0], ps_t[:, 0]).then_inc(s["t0_ready"], 1)

                def normalise(g, p, u):
                    n = g * U1 + u
                    turned = ps_o[:, 1, 0:P].rearrange("p (h d) -> p h d", d=VW)
                    e.wait_ge(s["raw_turned"], n + 1)
                    e.reciprocal(inv_sum[:, :], turned[:, :, HD1]).then_inc(s["inv_ready"], 1)
                    e.wait_ge(s["inv_ready"], n + 1)
                    e.tensor_tensor(o[:, p, u // 2, u % 2 * D // 2:(u % 2 + 1) * D // 2].rearrange("p (h d) -> p h d", d=HD1), turned[:, :, 0:HD1],
                                    inv_sum[:, :].unsqueeze(2).broadcast_to([P, HALF, HD1]), ALU.mult).then_inc(s["o_ready"], 1)

                def add_output(g, p):
                    e.wait_ge(s["xb_ready"], g + 1)
                    e.wait_ge(s["y_psum"], g + 1)
                    e.tensor_tensor(w.x[:, span(g, GW)], ps_m[:, :], xb[:, p].rearrange("p t d -> p (t d)"), ALU.add).then_inc(s["dve_done"], 1)

                def body(g, p, has_prev, has_next):
                    for u in range(U1):
                        if u + 1 < U1:
                            mask_unit(g, p, u + 1)
                        elif has_next:
                            mask_unit(g + 1, 1 - p, 0)
                        copy_t(g, p, u)
                        if u:
                            normalise(g, p, u - 1)
                        elif has_prev:
                            normalise(g - 1, 1 - p, U1 - 1)
                        if has_next and u == 0:
                            stats(g + 1, 1 - p)
                        if has_prev and u == 2:
                            add_output(g - 1, 1 - p)
                        if has_next and u == 2:
                            apply(g + 1, 1 - p)
                        if has_next and u == 3:
                            edges(g + 1, 1 - p)
                        if has_next and u == 6:
                            values(g + 1, 1 - p)
                stats(0, 0)
                apply(0, 0)
                edges(0, 0)
                values(0, 0)
                mask_unit(0, 0, 0)
                over_groups_lagged(e, body)
                normalise(GROUPS - 1, 1, U1 - 1)
                add_output(GROUPS - 1, 1)

            @block.tensor
            def _(e):
                give_credits(e, s["pe_done"])
                e.sem_inc(s["t_psum"], 4)
                e.sem_inc(s["pv_psum"], 2)
                e.wait_ge(s["weights"], 128)

                def transposes(g, p):
                    e.wait_ge(s["dve_done"], g + 1)
                    norm_transpose(e, s, w, g, p, ps_m)

                def project_q(g, p):
                    e.wait_ge(s["k_ready"], g + 1)
                    e.matmul(ps_m[:, :], wq[:, :], w.xt[:, p, :], start=True, stop=True).then_inc(s["q_psum"], 1)

                def project_k(g, p):
                    e.wait_ge(s["xt_ready"], g + 1)
                    e.matmul(ps_m[:, :], wk[:, :], w.xt[:, p, :], start=True, stop=True).then_inc(s["k_psum"], 1)

                def project_v(g, p):
                    e.wait_ge(s["q_ready"], g + 1)
                    for t in range(GT):
                        last = e.matmul(ps_m[:, t * D:(t + 1) * D], w.xt[:, p, t * P:(t + 1) * P], wv[:, :], start=True, stop=True)
                    last.then_inc(s["v_psum"], 1)

                def score(g, p, u):
                    n = g * U1 + u
                    v, hf = u // 2, u % 2
                    if u == 0:
                        e.wait_ge(k_loaded[p], g * 64 + (128 if p == 0 else 64))
                    e.wait_ge(s["masked"], n + 1)
                    for i in range(0, HALF, 2):
                        last = e.matmul(ps_s[:, u % 2, i:i + 2, :], q_t[:, p, v * P:(v + 1) * P],
                                        k_diag[:, p, v // 2, hf * HALF + i:hf * HALF + i + 2, :], start=True, stop=True)
                    last.then_inc(s["s_psum"], 1)

                def turn(g, p, u):
                    n = g * U1 + u
                    e.wait_ge(s["exp_ready"], n + 1 + 2)
                    for kt in range(2):
                        e.wait_ge(s[("t0_ready", "t1_ready")[kt]], n + 1)
                        for i in range(HALF):
                            last = e.transpose(ps_t[:, kt, i, :], probs[:, u % 2, i, kt * P:(kt + 1) * P], w.ident[:, :])
                        last.then_inc(s["t_psum"], 1)

                def weigh(g, p, u):
                    n = g * U1 + u
                    v, hf = u // 2, u % 2
                    e.wait_ge(s["o_ready"], n + 1)
                    e.wait_ge(s["t0_ready"], n + 2)
                    e.wait_ge(s["t1_ready"], n + 2)
                    for i in range(HALF):
                        for kt in range(2):
                            last = e.matmul(ps_o[i * VW:(i + 1) * VW, 0, 0:P], v1[:, p, v // 2 * 2 + kt, hf * HALF + i, :], probs_t[:, u % 2, kt, i, :],
                                            start=kt == 0, stop=kt == 1)
                    last.then_inc(s["pv_psum"], 1)

                def turn_back(g, u):
                    e.wait_ge(s["raw_copied"], g * U1 + u + 1)
                    e.transpose(ps_o[:, 1, 0:P], raw_t[:, :], w.ident[:, :]).then_inc(s["raw_turned"], 1)

                def turn_output(g, p):
                    e.wait_ge(s["v_ready"], min(g + 2, GROUPS) if isinstance(g, int) else g + 2)
                    e.wait_ge(s["o_ready"], g * U1 + U1 + 1)
                    for t in range(GT):
                        last = e.transpose(ps_m[:, t * P:(t + 1) * P], o[:, p, t, :], w.ident[:, :])
                    last.then_inc(s["ot_psum"], 1)

                def project_output(g, p):
                    e.wait_ge(s["ot_ready"], g + 1)
                    for t in range(GT):
                        last = e.matmul(ps_m[:, t * D:(t + 1) * D], o_t[:, p, t * P:(t + 1) * P], wo[:, :], start=True, stop=True)
                    last.then_inc(s["y_psum"], 1)

                def body(g, p, has_prev, has_next):
                    for u in range(U1):
                        if u + 1 < U1:
                            score(g, p, u + 1)
                        elif has_next:
                            score(g + 1, 1 - p, 0)
                        if u:
                            weigh(g, p, u - 1)
                        elif has_prev:
                            weigh(g - 1, 1 - p, U1 - 1)
                        if has_prev and u == 1:
                            turn_output(g - 1, 1 - p)
                        if has_prev and u == 2:
                            project_output(g - 1, 1 - p)
                        if has_next:
                            if u == 3:
                                transposes(g + 1, 1 - p)
                            if u == 4:
                                project_k(g + 1, 1 - p)
                            if u == 5:
                                project_q(g + 1, 1 - p)
                            if u == 6:
                                project_v(g + 1, 1 - p)
                        turn(g, p, u)
                        if u:
                            turn_back(g, u - 1)
                        elif has_prev:
                            turn_back(g - 1, U1 - 1)
                    e.drain().then_inc(s["pe_done"], 1)
                e.sem_inc(s["o_ready"], 1)
                transposes(0, 0)
                project_k(0, 0)
                project_q(0, 0)
                project_v(0, 0)
                e.wait_ge(s["v_ready"], 1)
                score(0, 0, 0)
                over_groups_lagged(e, body)
                weigh(GROUPS - 1, 1, U1 - 1)
                turn_back(GROUPS - 1, U1 - 1)
                turn_output(GROUPS - 1, 1)
                project_output(GROUPS - 1, 1)

            @block.scalar
            def _(e):
                give_credits(e, s["act_done"])
                e.sem_inc(s["exp_ready"], 2)
                e.sem_inc(s["t1_ready"], 1)
                e.preload_act_table(ACT.Exp)
                e.wait_ge(s["weights"], 128)
                e.wait_ge(s["bq_scaled"], 1)

                def copy_xt(g, p):
                    norm_copy(e, s, w, g, p, ps_m[:, :])

                def copy_q(g, p):
                    e.wait_ge(s["q_psum"], g + 1)
                    e.activation(q_t[:, p, :], ps_m[:, :], ACT.Identity, bias=bq_scaled[:, 0:1], scale=-0.25).then_inc(s["q_ready"], 1)

                def copy_k(g, p):
                    e.wait_ge(s["k_psum"], g + 1)
                    e.activation(k_t[:, p, :], ps_m[:, :], ACT.Identity, bias=bk[:, 0:1]).then_inc(s["k_ready"], 1)

                def exps(g, p, u):
                    n = g * U1 + u
                    e.wait_ge(s["masked"], n + 1 + 2)
                    e.wait_ge(s["t_psum"], 2 * n + 2)
                    for i in range(HALF):
                        last = e.activation(probs[:, u % 2, i, :], scores[:, u % 2, i, :], ACT.Exp, bias=row_min[:, u % 2, i:i + 1], scale=-1.0)
                    last.then_inc(s["exp_ready"], 1)

                def copy_t(g, p, u):
                    n = g * U1 + u
                    e.wait_ge(s["pv_psum"], n + 1)
                    e.wait_ge(s["t_psum"], 2 * n + 2 + 4)
                    e.activation(probs_t[:, u % 2, 1], ps_t[:, 1], ACT.Copy).then_inc(s["t1_ready"], 1)

                def copy_raw(g, u):
                    e.wait_ge(s["pv_psum"], g * U1 + u + 1 + 2)
                    e.activation(raw_t[:, :], ps_o[:, 0, 0:P], ACT.Copy).then_inc(s["raw_copied"], 1)

                def copy_output(g, p):
                    e.wait_ge(s["ot_psum"], g + 1)
                    e.activation(o_t[:, p, :], ps_m[:, :], ACT.Copy).then_inc(s["ot_ready"], 1)

                def body(g, p, has_prev, has_next):
                    for u in range(U1):
                        if u:
                            copy_raw(g, u - 1)
                        elif has_prev:
                            copy_raw(g - 1, U1 - 1)
                        if has_prev and u == 1:
                            copy_output(g - 1, 1 - p)
                        if has_next:
                            if u == 3:
                                copy_xt(g + 1, 1 - p)
                            if u == 4:
                                copy_k(g + 1, 1 - p)
                            if u == 5:
                                copy_q(g + 1, 1 - p)
                        copy_t(g, p, u)
                        if u + 1 < U1:
                            exps(g, p, u + 1)
                        elif has_next:
                            exps(g + 1, 1 - p, 0)
                    e.drain().then_inc(s["act_done"], 1)
                copy_xt(0, 0)
                copy_k(0, 0)
                copy_q(0, 0)
                exps(0, 0, 0)
                over_groups_lagged(e, body)
                copy_raw(GROUPS - 1, U1 - 1)
                copy_output(GROUPS - 1, 1)


E1 = 8
F1 = 256
C1 = F1 // P
CAPACITY = float(-(-B * N * 1.25 // E1))
PACK = F1 + C1 * D + C1


def l1_ffn(nc, w, a):
    with ExitStack() as c:
        sb = lambda n, shape, dt=F32: c.enter_context(nc.sbuf_tensor("l1f_" + n, shape, dt))
        xt_all = sb("xt_all", [P, TILES * D])
        meanvar_all = sb("meanvar_all", [P, TILES, 2])
        rstd_all = sb("rstd_all", [P, TILES])
        sums = sb("sums", [P, B])
        weight_all = sb("weight_all", [P, B * 2])
        at_row = sb("at_row", [1, B * 2], U32)
        scratch_w = nc.dram_tensor("l1f_scratch_w", [B * 2], F32, kind="Internal").ap()
        scratch_at = nc.dram_tensor("l1f_scratch_at", [B * 2], U32, kind="Internal").ap()
        scratch_b = nc.dram_tensor("l1f_scratch_b", [B, D], F32, kind="Internal").ap()
        l1_ffn_normalise(nc, w, xt_all, meanvar_all, rstd_all, sums)
        l1_ffn_route(nc, w, a, sums, scratch_w, scratch_at, scratch_b, weight_all, at_row)
        l1_ffn_experts(nc, w, a, xt_all, meanvar_all, rstd_all, scratch_b, weight_all, at_row)


def l1_ffn_normalise(nc, w, xt_all, meanvar_all, rstd_all, sums):
    with ExitStack() as c:
        ps_t = [c.enter_context(nc.psum_tensor(f"l1n_ps_t{i}", [P, GW], F32)) for i in range(2)]
        s = named_semaphores(nc, c, "l1n", NORM_SEMS + " summed kept xt_copied")
        with nc.Block() as block:
            @block.vector
            def _(e):
                def apply(g, p, first=False):
                    if not first:
                        e.wait_ge(s["xt_psum"], g - 1)
                    norm_apply(e, s, w, g, p)

                def body(g, p, has_prev, has_next, has_second):
                    if has_second:
                        e.wait_ge(s["kept"], g + 1)
                        norm_stats(e, s, w, g + 2, p)
                    if has_next:
                        apply(g + 1, 1 - p, not has_prev)
                    e.wait_ge(s["xt_psum"], g + 1)
                    e.tensor_reduce(sums[:, bass.ds(g * 2, 2)], ps_t[p][:, :].rearrange("p (b n) -> p b n", b=2), AX.X,
                                    ALU.add).then_inc(s["summed"], 1)
                norm_stats(e, s, w, 0, 0)
                norm_stats(e, s, w, 1, 1)
                apply(0, 0, True)
                over_groups_ahead(e, body)

            @block.gpsimd
            def _(e):
                def front(g, p):
                    norm_rstd(e, s, w, g, p)
                    e.tensor_copy(meanvar_all[:, bass.ds(g * GT, GT), :], w.meanvar[:, p])
                    e.wait_ge(s["rstd_ready"], g + 1)
                    e.tensor_copy(rstd_all[:, bass.ds(g * GT, GT)], w.rstd[:, p]).then_inc(s["kept"], 1)

                def body(g, p, has_prev, has_next, has_second):
                    if has_second:
                        front(g + 2, p)
                front(0, 0)
                front(1, 1)
                over_groups_ahead(e, body)

            @block.tensor
            def _(e):
                e.sem_inc(s["xt_copied"], 2)

                def body(g, p, has_next):
                    e.wait_ge(s["xt_copied"], g + 1)
                    e.wait_ge(s["xn_ready"], g + 1)
                    for t in range(GT):
                        last = e.transpose(ps_t[p][:, t * P:(t + 1) * P], w.xn[:, p, t, :], w.ident[:, :])
                    last.then_inc(s["xt_psum"], 1)
                over_groups(e, body)

            @block.scalar
            def _(e):
                def body(g, p, has_next):
                    e.wait_ge(s["summed"], g + 1)
                    e.activation(xt_all[:, span(g, GW)], ps_t[p][:, :], ACT.Copy).then_inc(s["xt_copied"], 1)
                over_groups(e, body)


def l1_ffn_route(nc, w, a, sums, scratch_w, scratch_at, scratch_b, weight_all, at_row):
    with ExitStack() as c:
        sb = lambda n, shape, dt=F32: c.enter_context(nc.sbuf_tensor("l1r_" + n, shape, dt))
        ps_l = c.enter_context(nc.psum_tensor("l1r_ps_l", [B, 512], F32))
        ps_load = c.enter_context(nc.psum_tensor("l1r_ps_load", [B, 512], F32))
        ps_d = c.enter_context(nc.psum_tensor("l1r_ps_d", [E1, 512], F32))
        ps_b = c.enter_context(nc.psum_tensor("l1r_ps_b", [B, 512], F32))
        wr = sb("wr", [P, E1]); br = sb("br", [B, E1]); b2 = sb("b2", [E1, D])
        lg = sb("lg", [B, E1]); mx = sb("mx", [B, 1]); ex = sb("ex", [B, E1]); total = sb("total", [B, 1])
        rw = sb("rw", [B, E1]); inv_load = sb("inv_load", [B, E1]); scale = sb("scale", [B, E1])
        lg2 = sb("lg2", [B, E1]); best = sb("best", [B, 8]); at = sb("at", [B, 8], U32); at_f = sb("at_f", [B, 8])
        diff = sb("diff", [B, 2]); ex2 = sb("ex2", [B, 2]); top = sb("top", [B, 2]); iota = sb("iota", [B, E1])
        hit0 = sb("hit0", [B, E1]); dense = sb("dense", [B, E1]); dense_t = sb("dense_t", [E1, B]); bias = sb("bias", [B, D])
        s = named_semaphores(nc, c, "l1r", "weights logit_psum v exps iota load_psum dense_psum dense_t bias_psum bias_ready out")
        with nc.Block() as block:
            @block.sync
            def _(e):
                e.dma_start(wr[:, :], a["L1_ffn_Wr"]).then_inc(s["weights"], 16)
                e.dma_start(br[:, :], a["L1_ffn_br"].partition_broadcast(B)).then_inc(s["weights"], 16)
                e.dma_start(b2[:, :], a["L1_ffn_b2"]).then_inc(s["weights"], 16)
                e.wait_ge(s["bias_ready"], 1)
                e.dma_start(scratch_w.rearrange("(b k) -> b k", k=2), top[:, :]).then_inc(w.scratch_stored, 16)
                e.dma_start(scratch_at.rearrange("(b k) -> b k", k=2), at[:, 0:2]).then_inc(w.scratch_stored, 16)
                e.dma_start(scratch_b, bias[:, :]).then_inc(w.scratch_stored, 16)
                e.wait_ge(w.scratch_stored, 48)
                e.dma_start(weight_all[:, :], scratch_w.partition_broadcast(P)).then_inc(s["out"], 16)
                e.dma_start(at_row[:, :], scratch_at.rearrange("(a k) -> a k", a=1)).then_inc(s["out"], 16)
                e.wait_ge(s["out"], 32)

            @block.gpsimd
            def _(e):
                e.iota(iota[:, :], pattern=[[1, E1]], base=0, channel_multiplier=0,
                       allow_small_or_imprecise_dtypes=True).then_inc(s["iota"], 1)

            @block.tensor
            def _(e):
                e.wait_ge(s["weights"], 48)
                e.matmul(ps_l[:, 0:E1], sums[:, :], wr[:, :], start=True, stop=True).then_inc(s["logit_psum"], 1)
                e.wait_ge(s["v"], 5)
                e.matmul(ps_load[:, 0:E1], w.ones[0:B, 0:B], rw[:, :], start=True, stop=True).then_inc(s["load_psum"], 1)
                e.wait_ge(s["v"], 20)
                e.transpose(ps_d[:, 0:B], dense[:, :], w.ident[0:B, 0:B]).then_inc(s["dense_psum"], 1)
                e.wait_ge(s["dense_t"], 1)
                e.matmul(ps_b[:, 0:D], dense_t[:, :], b2[:, :], start=True, stop=True).then_inc(s["bias_psum"], 1)

            @block.scalar
            def _(e):
                e.wait_ge(s["v"], 3)
                e.activation(ex[:, :], lg2[:, :], ACT.Exp).then_inc(s["exps"], 1)
                e.wait_ge(s["v"], 11)
                e.activation(ex[:, :], lg2[:, :], ACT.Exp).then_inc(s["exps"], 1)
                e.wait_ge(s["v"], 15)
                e.activation(ex2[:, :], diff[:, :], ACT.Exp).then_inc(s["exps"], 1)

            @block.vector
            def _(e):
                done = [0]

                def step(i):
                    i.then_inc(s["v"], 1)
                    done[0] += 1
                    e.wait_ge(s["v"], done[0])
                e.wait_ge(s["weights"], 48)
                e.wait_ge(s["logit_psum"], 1)
                step(e.scalar_tensor_tensor(lg[:, :], ps_l[:, 0:E1], 1.0 / N, br[:, :], ALU.mult, ALU.add))
                step(e.tensor_reduce(mx[:, :], lg[:, :], AX.X, ALU.max))
                step(e.tensor_scalar(lg2[:, :], lg[:, :], mx[:, 0:1], None, ALU.subtract))
                e.wait_ge(s["exps"], 1)
                step(e.tensor_reduce(total[:, :], ex[:, :], AX.X, ALU.add))
                e.reciprocal(mx[:, :], total[:, :]).then_inc(s["iota"], 1)
                e.wait_ge(s["iota"], 2)
                step(e.tensor_scalar(rw[:, :], ex[:, :], mx[:, 0:1], None, ALU.mult))
                e.wait_ge(s["load_psum"], 1)
                step(e.tensor_scalar(scale[:, :], ps_load[:, 0:E1], float(N), None, ALU.mult))
                step(e.reciprocal(inv_load[:, :], scale[:, :]))
                step(e.tensor_scalar(scale[:, :], inv_load[:, :], CAPACITY, 1.0, ALU.mult, ALU.min))
                step(e.tensor_tensor(lg[:, :], rw[:, :], scale[:, :], ALU.mult))
                step(e.tensor_reduce(mx[:, :], lg[:, :], AX.X, ALU.max))
                step(e.tensor_scalar(lg2[:, :], lg[:, :], mx[:, 0:1], None, ALU.subtract))
                e.wait_ge(s["exps"], 2)
                step(e.tensor_reduce(total[:, :], ex[:, :], AX.X, ALU.add))
                e.reciprocal(mx[:, :], total[:, :]).then_inc(s["iota"], 1)
                e.wait_ge(s["iota"], 3)
                step(e.tensor_scalar(rw[:, :], ex[:, :], mx[:, 0:1], None, ALU.mult))
                step(e.max(best[:, :], rw[:, :]))
                step(e.tensor_scalar(diff[:, :], best[:, 0:2], best[:, 0:1], None, ALU.subtract))
                step(e.max_index(at[:, :], best[:, :], rw[:, :]))
                e.wait_ge(s["exps"], 3)
                step(e.tensor_reduce(total[:, :], ex2[:, :], AX.X, ALU.add))
                e.reciprocal(mx[:, :], total[:, :])
                e.tensor_copy(at_f[:, :], at[:, :]).then_inc(s["iota"], 1)
                e.wait_ge(s["iota"], 4)
                step(e.tensor_scalar(top[:, :], ex2[:, :], mx[:, 0:1], None, ALU.mult))
                step(e.tensor_scalar(hit0[:, :], iota[:, :], at_f[:, 0:1], top[:, 0:1], ALU.is_equal, ALU.mult))
                e.tensor_scalar(dense[:, :], iota[:, :], at_f[:, 1:2], top[:, 1:2], ALU.is_equal, ALU.mult).then_inc(s["iota"], 1)
                e.wait_ge(s["iota"], 5)
                step(e.tensor_tensor(dense[:, :], dense[:, :], hit0[:, :], ALU.add))
                e.wait_ge(s["dense_psum"], 1)
                e.tensor_copy(dense_t[:, :], ps_d[:, 0:B]).then_inc(s["dense_t"], 1)
                e.wait_ge(s["bias_psum"], 1)
                e.tensor_copy(bias[:, :], ps_b[:, 0:D]).then_inc(s["bias_ready"], 1)


def l1_ffn_experts(nc, w, a, xt_all, meanvar_all, rstd_all, scratch_b, weight_all, at_row):
    with ExitStack() as c:
        sb = lambda n, shape, dt=F32: c.enter_context(nc.sbuf_tensor("l1f_" + n, shape, dt))
        ps = lambda n, shape: c.enter_context(nc.psum_tensor("l1f_" + n, shape, F32))
        pack = sb("pack", [P, 2, 4, PACK])
        bias = sb("bias", [P, 2, 2, D])
        gamma = sb("gamma", [P, D]); beta = sb("beta", [P, D])
        xn = sb("xn", [P, 2, GT, D]); xnb = sb("xnb", [P, 2, GT, D]); xb = sb("xb", [P, 2, GT, D])
        y0 = sb("y0", [P, 2, GT, D]); y1 = sb("y1", [P, 2, GT, D]); ln = sb("ln", [P, 2, GT, D]); ln_g = sb("ln_g", [P, 2, GT, D])
        h = sb("h", [P, 4, C1, N])
        ps_h = [ps(f"ps_h{i}", [P, C1, N]) for i in range(4)]
        ps_y = [ps(f"ps_y{i}", [P, 2, D]) for i in range(4)]
        s = named_semaphores(nc, c, "l1f", "weights pack0 pack1 xn_ready xnb_ready h_psum h_ready y_psum y0_ready y1_ready stats_done var_ready"
                             " veps_ready rstd_ready ln_ready ln_g_ready xb_ready pe_done act_done dve_done")
        loaded = [s["pack0"], s["pack1"]]
        with nc.Block() as block:
            @block.sync
            def _(e):
                e.dma_start(gamma[:, :], a["L1_ffn_gamma"].partition_broadcast(P)).then_inc(s["weights"], 16)
                e.dma_start(beta[:, :], a["L1_ffn_beta"].partition_broadcast(P)).then_inc(s["weights"], 16)

                def body(g, p, has_next):
                    wait_groups_before(e, g, s["pe_done"], s["act_done"], s["xnb_ready"])
                    for k in range(4):
                        x = e.value_load(at_row[0:1, bass.ds(g * 4 + k, 1)], min_val=0, max_val=E1 - 1)
                        e.dma_start(pack[:, p, k, :], a["L1_ffn_pack"][bass.ds(x, 1)].rearrange("a p f -> p (a f)")).then_inc(loaded[p], 16)
                    e.dma_start(bias[:, p].rearrange("p b d -> p (b d)"),
                                scratch_b.rearrange("b d -> (b d)")[bass.ds(g * 2 * D, 2 * D)].partition_broadcast(P)).then_inc(loaded[p], 16)
                over_groups(e, body)

            def wait_loaded(e, g, p):
                e.wait_ge(loaded[p], g * 40 + (80 if p == 0 else 40))

            @block.tensor
            def _(e):
                give_credits(e, s["pe_done"])

                def hidden(g, p, k):
                    e.wait_ge(s["h_ready"], g * 4 + k + 1)
                    for ch in range(C1):
                        last = e.matmul(ps_h[k][:, ch, :], pack[:, p, k, ch * P:(ch + 1) * P], xt_all[:, span(g, GW, k // 2 * N, N)],
                                        start=True, stop=True)
                    last.then_inc(s["h_psum"], 1)

                def output(g, p, k):
                    e.wait_ge(s["h_ready"], g * 4 + k + 1 + 4)
                    for t in range(2):
                        for ch in range(C1):
                            last = e.matmul(ps_y[k][:, t, :], h[:, k, ch, t * P:(t + 1) * P],
                                            pack[:, p, k, F1 + ch * D:F1 + (ch + 1) * D], start=ch == 0, stop=ch == C1 - 1)
                    last.then_inc(s["y_psum"], 1)

                def body(g, p, has_next):
                    wait_loaded(e, g, p)
                    hidden(g, p, 0)
                    for k in range(4):
                        if k + 1 < 4:
                            hidden(g, p, k + 1)
                        if k == 0:
                            e.wait_ge(s["y1_ready"], g + 1)
                        output(g, p, k)
                    e.drain().then_inc(s["pe_done"], 1)
                over_groups(e, body)

            @block.scalar
            def _(e):
                give_credits(e, s["act_done"])
                e.sem_inc(s["h_ready"], 4)
                e.preload_act_table(ACT.Gelu)

                def body(g, p, has_next):
                    wait_loaded(e, g, p)
                    for k in range(4):
                        e.wait_ge(s["h_psum"], g * 4 + k + 1)
                        e.wait_ge(s["y_psum"], g * 4 + k + 1)
                        for ch in range(C1):
                            last = e.activation(h[:, k, ch, :], ps_h[k][:, ch, :], ACT.Gelu, bias=pack[:, p, k, F1 + C1 * D + ch:F1 + C1 * D + ch + 1])
                        last.then_inc(s["h_ready"], 1)
                    e.drain().then_inc(s["act_done"], 1)
                over_groups(e, body)

            @block.vector
            def _(e):
                give_credits(e, s["dve_done"])
                e.sem_inc(s["y_psum"], 4)
                e.sem_inc(s["y1_ready"], 1)

                def apply(g, p):
                    e.wait_ge(s["xnb_ready"], g + 1)
                    for t in range(GT):
                        last = e.tensor_scalar(xn[:, p, t, :], w.x[:, span(g, GW, t * D, D)], meanvar_all[:, bass.ds(g * GT + t, 1), 0],
                                               rstd_all[:, bass.ds(g * GT + t, 1)], ALU.subtract, ALU.mult)
                    last.then_inc(s["xn_ready"], 1)

                def add(g, p):
                    e.wait_ge(s["ln_g_ready"], g + 1)
                    e.tensor_tensor(w.x[:, span(g, GW)], ln_g[:, p].rearrange("p t d -> p (t d)"), xb[:, p].rearrange("p t d -> p (t d)"),
                                    ALU.add).then_inc(s["dve_done"], 1)

                def body(g, p, has_prev, has_next):
                    if has_next:
                        apply(g + 1, 1 - p)
                    e.wait_ge(s["xnb_ready"], g + 3)
                    e.wait_ge(s["y_psum"], g * 4 + 4 + 4)
                    for t in range(GT):
                        last = e.scalar_tensor_tensor(y0[:, p, t, :], ps_y[t // 2 * 2][:, t % 2, :], weight_all[:, bass.ds(g * 4 + t // 2 * 2, 1)],
                                                      xnb[:, p, t, :], ALU.mult, ALU.add)
                    last.then_inc(s["y0_ready"], 1)
                    e.wait_ge(s["y0_ready"], g + 1)
                    for t in range(GT):
                        last = e.scalar_tensor_tensor(y1[:, p, t, :], ps_y[t // 2 * 2 + 1][:, t % 2, :], weight_all[:, bass.ds(g * 4 + t // 2 * 2 + 1, 1)],
                                                      y0[:, p, t, :], ALU.mult, ALU.add)
                    last.then_inc(s["y1_ready"], 1)
                    e.wait_ge(s["y1_ready"], g + 2)
                    for t in range(GT):
                        last = e.bn_stats(w.stats[:, p, t, :], y1[:, p, t, :])
                    last.then_inc(s["stats_done"], 1)
                    wait_apart(e, w, s["stats_done"], g + 1)
                    for t in range(GT):
                        last = e.bn_aggr(w.meanvar[:, p, t, :], w.stats[:, p, t, :])
                    last.then_inc(s["var_ready"], 1)
                    e.wait_ge(s["rstd_ready"], g + 1)
                    for t in range(GT):
                        last = e.tensor_scalar(ln[:, p, t, :], y1[:, p, t, :], w.meanvar[:, p, t, 0:1], w.rstd[:, p, t:t + 1],
                                               ALU.subtract, ALU.mult)
                    last.then_inc(s["ln_ready"], 1)
                    if has_prev:
                        add(g - 1, 1 - p)
                apply(0, 0)
                over_groups_lagged(e, body)
                add(GROUPS - 1, 1)

            @block.gpsimd
            def _(e):
                give_credits(e, s["xnb_ready"])
                e.wait_ge(s["weights"], 32)

                def add_bias(g, p):
                    wait_loaded(e, g, p)
                    e.wait_ge(s["xn_ready"], g + 1)
                    for t in range(GT):
                        last = e.tensor_tensor(xnb[:, p, t, :], xn[:, p, t, :], bias[:, p, t // 2, :], ALU.add)
                    last.then_inc(s["xnb_ready"], 1)

                def body(g, p, has_next):
                    if has_next:
                        add_bias(g + 1, 1 - p)
                    wait_groups_before(e, g, s["dve_done"])
                    for t in range(GT):
                        e.tensor_tensor(xb[:, p, t, :], w.x[:, span(g, GW, t * D, D)], beta[:, :], ALU.add)
                    norm_rstd(e, s, w, g, p)
                    e.wait_ge(s["ln_ready"], g + 1)
                    for t in range(GT):
                        last = e.tensor_tensor(ln_g[:, p, t, :], ln[:, p, t, :], gamma[:, :], ALU.mult)
                    last.then_inc(s["ln_g_ready"], 1)
                add_bias(0, 0)
                over_groups(e, body)




def l2_gnn(nc, w, a):
    graph_attention(nc, w, a, "l2g", "L2_gnn_W_a", True)


def graph_attention(nc, w, a, name, weight, cosine):
    with ExitStack() as c:
        sb = lambda n, shape, dt=F32: c.enter_context(nc.sbuf_tensor(name + "_" + n, shape, dt))
        ps = lambda n, shape: c.enter_context(nc.psum_tensor(name + "_" + n, shape, F32))
        wa = sb("wa", [P, D])
        bias = sb("bias", [P, D])
        y_t = sb("y_t", [P, 2, GW])
        square = sb("square", [P, 2, GT, N])
        sum_sq = sb("sum_sq", [P, 2, GT])
        inv_mag = sb("inv_mag", [P, 2, GT])
        neg_inv = sb("neg_inv", [P, 2, GT])
        inv_row = sb("inv_row", [P, 2, 2, N])
        raw = sb("raw", [P, 2, GT, N])
        leaky = sb("leaky", [P, 2, GT, N])
        not_adj = sb("not_adj", [P, 2, GT, N])
        mask_int = sb("mask_int", [P, 2, 2, N], I32)
        scores = sb("scores", [P, 2, GT, N])
        row_min = sb("row_min", [P, 2, GT])
        probs = sb("probs", [P, 2, GT, N])
        row_sum = sb("row_sum", [P, 2, GT])
        inv_sum = sb("inv_sum", [P, 2, GT])
        probs_t = sb("probs_t", [P, 2, 2, 2, 2, P])
        xn_kept = sb("xn_kept", [P, 2, GT, D])
        hb = sb("hb", [P, 2, GT, D])
        low = sb("low", [P, 2, GT, D])
        ex = sb("ex", [P, 2, GT, D])
        high = sb("high", [P, 2, GT, D])
        ps_x = ps("ps_x", [P, GW])
        ps_s = [ps(f"ps_s{i}", [P, 2, N]) for i in range(2)]
        ps_b = ps("ps_b", [P, 2, N])
        ps_t = [ps(f"ps_t{i}", [P, 2, 2, P]) for i in range(2)]
        ps_h = ps("ps_h", [P, GT, D])
        s = named_semaphores(nc, c, name, NORM_SEMS + " weights mask_loaded0 mask_loaded1 mask_ready y_psum y_ready s_psum squares"
                             " mag_ready neg_ready b_psum b_ready raw_ready leaky_ready masked exp_ready sum_ready t_psum t_ready h_psum"
                             " hb_ready low_ready high_ready ex_ready x_done kept_ready")
        mask_loaded = [s["mask_loaded0"], s["mask_loaded1"]]
        with nc.Block() as block:
            @block.sync
            def _(e):
                e.dma_start(wa[:, :], a[weight]).then_inc(s["weights"], 16)
                if cosine:
                    e.dma_start(bias[:, :], a["L2_gnn_bias"].rearrange("a d -> (a d)").partition_broadcast(P)).then_inc(s["weights"], 16)
                else:
                    def body(g, p, has_next):
                        wait_groups_before(e, g, s["mask_ready"])
                        e.dma_start(mask_int[:, p].rearrange("p b n -> p (b n)"),
                                    a["nodemask"].rearrange("b n -> (b n)")[bass.ds(g * 2 * N, 2 * N)].partition_broadcast(P)
                                    ).then_inc(mask_loaded[p], 16)
                    over_groups(e, body)

            @block.gpsimd
            def _(e):
                def magnitudes(g, p):
                    if cosine:
                        e.wait_ge(s["squares"], g + 1)
                        e.tensor_tensor(inv_mag[:, p, :], sum_sq[:, p, :], w.minus_half[:, 0:GT], ALU.pow).then_inc(s["mag_ready"], 1)

                def keep(g, p, first):
                    if not first:
                        e.wait_ge(s["h_psum"], g - 1)
                    wait_apart(e, w, s["xn_ready"], g + 1)
                    e.tensor_copy(xn_kept[:, p], w.xn[:, p]).then_inc(s["kept_ready"], 1)

                def body(g, p, has_prev, has_next, has_second):
                    if has_second:
                        norm_rstd(e, s, w, g + 2, p)
                    if has_next:
                        keep(g + 1, 1 - p, not has_prev)
                        magnitudes(g + 1, 1 - p)
                norm_rstd(e, s, w, 0, 0)
                norm_rstd(e, s, w, 1, 1)
                keep(0, 0, True)
                magnitudes(0, 0)
                over_groups_ahead(e, body)

            @block.vector
            def _(e):
                give_credits(e, s["mask_ready"])
                e.wait_ge(s["weights"], 32 if cosine else 16)

                def edges(g, p):
                    if cosine:
                        e.tensor_scalar(not_adj[:, p], w.adj[:, span(g, GT * N)].rearrange("p (t n) -> p t n", n=N), 0.0, NEG_MASK,
                                        ALU.is_le, ALU.mult).then_inc(s["mask_ready"], 1)
                    else:
                        e.wait_ge(mask_loaded[p], g * 8 + (16 if p == 0 else 8))
                        e.tensor_scalar(not_adj[:, p, 0:2, :], mask_int[:, p], 0.0, KEY_MASK, ALU.is_equal, ALU.mult).then_inc(s["mask_ready"], 1)

                def raw_scores(g, p):
                    if cosine:
                        e.wait_ge(s["mag_ready"], g + 1)
                        e.tensor_scalar(neg_inv[:, p, :], inv_mag[:, p, :], -1.0, None, ALU.mult).then_inc(s["neg_ready"], 1)
                        e.wait_ge(s["neg_ready"], g + 1)
                        e.wait_ge(s["b_ready"], g + 1)
                    e.wait_ge(s["s_psum"], g + 1)
                    for t in range(GT):
                        if cosine:
                            last = e.scalar_tensor_tensor(raw[:, p, t, :], ps_s[t // 2][:, t % 2, :], neg_inv[:, p, t:t + 1],
                                                          inv_row[:, p, t // 2, :], ALU.mult, ALU.mult)
                        else:
                            last = e.scalar_tensor_tensor(raw[:, p, t, :], ps_s[t // 2][:, t % 2, :], -1.0,
                                                          w.adj[:, span(g, GT * N, t * N, N)], ALU.mult, ALU.mult)
                    last.then_inc(s["raw_ready"], 1)
                    e.wait_ge(s["raw_ready"], g + 1)
                    if cosine:
                        e.scalar_tensor_tensor(leaky[:, p], raw[:, p], -0.2, raw[:, p], ALU.mult, ALU.min).then_inc(s["leaky_ready"], 1)

                def apply(g, p, first=False):
                    if not first:
                        e.wait_ge(s["xt_psum"], g - 1)
                        e.wait_ge(s["kept_ready"], g - 1)
                    norm_apply(e, s, w, g, p)

                def mask(g, p):
                    if cosine:
                        e.wait_ge(s["leaky_ready"], g + 1)
                    held = leaky if cosine else raw
                    wait_apart(e, w, s["mask_ready"], g + 3)
                    for t in range(GT):
                        last = e.tensor_tensor_reduce(scores[:, p, t, :], held[:, p, t, :], not_adj[:, p, t if cosine else t // 2, :],
                                                      1.0, BIG, ALU.add, ALU.min, row_min[:, p, t:t + 1])
                    last.then_inc(s["masked"], 1)

                def back(g, p):
                    e.wait_ge(s["exp_ready"], g + 1)
                    e.reciprocal(inv_sum[:, p, :], row_sum[:, p, :]).then_inc(s["sum_ready"], 1)
                    e.wait_ge(s["sum_ready"], g + 1)
                    e.wait_ge(s["h_psum"], g + 1)
                    if not cosine:
                        for t in range(GT):
                            xt = w.x[:, span(g, GW, t * D, D)]
                            last = e.scalar_tensor_tensor(xt, ps_h[:, t, :], inv_sum[:, p, t:t + 1], xt, ALU.mult, ALU.add)
                        last.then_inc(s["hb_ready"], 1)
                        return
                    for t in range(GT):
                        last = e.scalar_tensor_tensor(hb[:, p, t, :], ps_h[:, t, :], inv_sum[:, p, t:t + 1], bias[:, :], ALU.mult, ALU.add)
                    last.then_inc(s["hb_ready"], 1)
                    e.wait_ge(s["hb_ready"], g + 2)
                    e.tensor_scalar(low[:, p], hb[:, p], 0.0, None, ALU.min).then_inc(s["low_ready"], 1)
                    e.scalar_tensor_tensor(high[:, p].rearrange("p t d -> p (t d)"), hb[:, p].rearrange("p t d -> p (t d)"), 0.0,
                                           w.x[:, span(g, GW)], ALU.max, ALU.add).then_inc(s["high_ready"], 1)

                def back_sum(g, p):
                    e.wait_ge(s["high_ready"], g + 1)
                    e.wait_ge(s["ex_ready"], g + 1)
                    e.scalar_tensor_tensor(w.x[:, span(g, GW)], ex[:, p].rearrange("p t d -> p (t d)"), -1.0,
                                           high[:, p].rearrange("p t d -> p (t d)"), ALU.add, ALU.add).then_inc(s["x_done"], 1)

                def body(g, p, has_prev, has_next, has_second):
                    if has_second:
                        norm_stats(e, s, w, g + 2, p)
                    raw_scores(g, p)
                    mask(g, p)
                    if has_second:
                        apply(g + 2, p)
                    if has_prev:
                        back(g - 1, 1 - p)
                    if has_next:
                        edges(g + 1, 1 - p)
                    if has_prev and cosine:
                        back_sum(g - 1, 1 - p)
                norm_stats(e, s, w, 0, 0)
                norm_stats(e, s, w, 1, 1)
                apply(0, 0, True)
                apply(1, 1, True)
                edges(0, 0)
                over_groups_ahead(e, body)
                back(GROUPS - 1, 1)
                if cosine:
                    back_sum(GROUPS - 1, 1)

            @block.tensor
            def _(e):
                e.wait_ge(s["weights"], 32 if cosine else 16)

                def front(g, p, first=False):
                    if not first:
                        e.wait_ge(s["y_ready"], g)
                    norm_transpose(e, s, w, g, p, ps_x)

                def project(g, p):
                    e.wait_ge(s["xt_ready"], g + 1)
                    e.matmul(ps_x[:, :], wa[:, :], w.xt[:, p, :], start=True, stop=True).then_inc(s["y_psum"], 1)

                def raw_scores(g, p, first=False):
                    e.wait_ge(s["y_ready"], g + 1)
                    if not first:
                        e.wait_ge(s["raw_ready"], g)
                    other = y_t if cosine else w.xt
                    for t in range(GT):
                        last = e.matmul(ps_s[t // 2][:, t % 2, :], y_t[:, p, t * P:(t + 1) * P], other[:, p, t // 2 * N:(t // 2 + 1) * N],
                                        start=True, stop=True)
                    last.then_inc(s["s_psum"], 1)

                def magnitudes(g, p, first):
                    e.wait_ge(s["mag_ready"], g + 1)
                    if not first:
                        e.wait_ge(s["b_ready"], g)
                    for t in range(GT):
                        last = e.matmul(ps_b[:, t // 2, t % 2 * P:(t % 2 + 1) * P], inv_mag[:, p, t:t + 1].broadcast_to([P, P]), w.ident[:, :],
                                        start=True, stop=True)
                    last.then_inc(s["b_psum"], 1)

                def turn(g, p):
                    e.wait_ge(s["exp_ready"], g + 1)
                    e.wait_ge(s["t_ready"], g + 1)
                    for t in range(GT):
                        for m in range(2):
                            last = e.transpose(ps_t[t // 2][:, t % 2, m, :], probs[:, p, t, m * P:(m + 1) * P], w.ident[:, :])
                    last.then_inc(s["t_psum"], 1)

                def weigh(g, p):
                    e.wait_ge(s["t_ready"], g + 2)
                    e.wait_ge(s["hb_ready"], g + 1)
                    e.wait_ge(s["kept_ready"], g + 1)
                    for t in range(GT):
                        for m in range(2):
                            last = e.matmul(ps_h[:, t, :], probs_t[:, p, t // 2, t % 2, m, :], xn_kept[:, p, t // 2 * 2 + m, :],
                                            start=m == 0, stop=m == 1)
                    last.then_inc(s["h_psum"], 1)

                def body(g, p, has_prev, has_next):
                    if has_prev:
                        turn(g - 1, 1 - p)
                    if has_next:
                        front(g + 1, 1 - p)
                    if cosine:
                        magnitudes(g, p, not has_prev)
                    if has_prev:
                        weigh(g - 1, 1 - p)
                    if has_next:
                        project(g + 1, 1 - p)
                        raw_scores(g + 1, 1 - p)
                e.sem_inc(s["t_ready"], 1)
                front(0, 0, True)
                project(0, 0)
                raw_scores(0, 0, True)
                over_groups_lagged(e, body)
                turn(GROUPS - 1, 1)
                weigh(GROUPS - 1, 1)

            @block.scalar
            def _(e):
                e.sem_inc(s["hb_ready"], 1)
                e.preload_act_table(ACT.Exp)

                def project(g, p):
                    e.wait_ge(s["y_psum"], g + 1)
                    e.activation(y_t[:, p, :], ps_x[:, :], ACT.Copy).then_inc(s["y_ready"], 1)

                def squares(g, p):
                    e.wait_ge(s["s_psum"], g + 1)
                    for t in range(GT):
                        last = e.activation(square[:, p, t, :], ps_s[t // 2][:, t % 2, :], ACT.Square, accum_out=sum_sq[:, p, t:t + 1])
                    last.then_inc(s["squares"], 1)

                def row_magnitudes(g, p):
                    e.wait_ge(s["b_psum"], g + 1)
                    e.activation(inv_row[:, p], ps_b[:, :, :], ACT.Copy).then_inc(s["b_ready"], 1)

                def exps(g, p):
                    e.wait_ge(s["masked"], g + 1)
                    for t in range(GT):
                        last = e.activation(probs[:, p, t, :], scores[:, p, t, :], ACT.Exp, bias=row_min[:, p, t:t + 1], scale=-1.0,
                                            accum_out=row_sum[:, p, t:t + 1])
                    last.then_inc(s["exp_ready"], 1)

                def copy_turned(g, p):
                    e.wait_ge(s["t_psum"], g + 1)
                    for b in range(2):
                        last = e.activation(probs_t[:, p, b], ps_t[b][:, :, :, :], ACT.Copy)
                    last.then_inc(s["t_ready"], 1)

                def low_exp(g, p):
                    e.wait_ge(s["low_ready"], g + 1)
                    e.activation(ex[:, p], low[:, p], ACT.Exp).then_inc(s["ex_ready"], 1)

                def body(g, p, has_prev, has_next):
                    if has_prev:
                        copy_turned(g - 1, 1 - p)
                    if has_next:
                        norm_copy(e, s, w, g + 1, 1 - p, ps_x[:, :])
                    if cosine:
                        row_magnitudes(g, p)
                    if has_next:
                        project(g + 1, 1 - p)
                    exps(g, p)
                    if has_next and cosine:
                        squares(g + 1, 1 - p)
                    if has_prev and cosine:
                        low_exp(g - 1, 1 - p)
                norm_copy(e, s, w, 0, 0, ps_x[:, :])
                project(0, 0)
                if cosine:
                    squares(0, 0)
                over_groups_lagged(e, body)
                copy_turned(GROUPS - 1, 1)
                if cosine:
                    low_exp(GROUPS - 1, 1)


NH = 4
NE = 4
DH = D // NH
BLK = NH * GT
UNITS = NH * GT
CAUSAL = 1e30
HEAD_EPS = 1e-8

SLOTS = [
    [], [("prev", "gate_turn3")], [("prev", "gate_logits3")], [("next", "turn_x")], [("next", "heads")],
    [("next", "heads_turn")], [("own", "gate_turn0"), ("next", "keys")], [("own", "gate_logits0")],
    [("prev", "ff_turn"), ("next", "values")], [("prev", "ff1"), ("next", "query0")], [("own", "gate_turn1"), ("prev", "ff2")],
    [("own", "gate_logits1")], [("next", "query1")], [("next", "query2")], [("own", "gate_turn2"), ("prev", "out_turn")],
    [("own", "gate_logits2"), ("next", "query3"), ("prev", "out_logits")],
]
FRONT = ["turn_x", "heads", "heads_turn", "keys", "values", "query0", "query1", "query2", "query3"]
BACK = ["gate_turn3", "gate_logits3", "ff_turn", "ff1", "ff2", "out_turn", "out_logits"]
OWN = 6
PER_GROUP = len(FRONT) + len(BACK) + OWN


def bank_uses(g, has_prev, has_next):
    base = len(FRONT) if not has_prev else PER_GROUP * g + len(FRONT) - len(BACK)
    order = [u for slot in SLOTS for u in slot if (u[0] != "prev" or has_prev) and (u[0] != "next" or has_next)]
    return {u: base + k + 1 for k, u in enumerate(order)}


def gate_count(g, which, has_prev):
    if not has_prev:
        return {"own0": 1, "own1": 2}[which]
    return 5 * g + {"prev2": -2, "prev3": -1, "own0": 0, "own1": 1, "out": 2}[which]


def front_uses():
    return {("next", u): k + 1 for k, u in enumerate(FRONT)}


def tail_uses():
    base = PER_GROUP * GROUPS + len(FRONT) - len(BACK) - len(FRONT)
    return {("prev", u): base + k + 1 for k, u in enumerate(BACK)}


def l2_ffn(nc, w, a):
    with ExitStack() as c:
        sb = lambda n, shape, dt=F32: c.enter_context(nc.sbuf_tensor("l2f_" + n, shape, dt))
        ps = lambda n, shape: c.enter_context(nc.psum_tensor("l2f_" + n, shape, F32))
        hl = sb("hl", [P, D]); hl_b = sb("hl_b", [P, 1])
        wq = sb("wq", [P, NH, D])
        wk = sb("wk", [P, D]); wv = sb("wv", [P, D]); fc1 = sb("fc1", [P, D]); fc2 = sb("fc2", [P, D])
        gate_w = sb("gate_w", [P, NH, NE]); gate_b = sb("gate_b", [P, NH, NE])
        ln_g = sb("ln_g", [P, DH]); ln_b = sb("ln_b", [P, DH]); fn_g = sb("fn_g", [P, DH]); fn_b = sb("fn_b", [P, DH])
        fc1_b = sb("fc1_b", [P, 1]); fc2_b = sb("fc2_b", [P, DH]); fgate = sb("fgate", [P, NH])
        causal = sb("causal", [P, N])
        head_eps = sb("head_eps", [P, BLK])
        resid = sb("resid", [P, 2, D])
        sx_t = sb("sx_t", [P, GW]); k_t = sb("k_t", [P, GW])
        k_diag = sb("k_diag", [P, NH, NE, GW])
        q_t = sb("q_t", [P, NH, GW])
        v = sb("v", [P, 2, GT, NH, DH])
        not_pad = sb("not_pad", [P, 2, GT, D])
        scores = sb("scores", [P, 2, NE * N]); probs = scores; probs_t = sb("probs_t", [P, 2, 2, NE, P])
        row_min = sb("row_min", [P, 2, NE])
        row_sum = sb("row_sum", [P, 4, NE])
        inv_sum = sb("inv_sum", [P, NE])
        raw_t = sb("raw_t", [P, P])
        o_raw = sb("o_raw", [P, NE, DH])
        o = sb("o", [P, 2, GT, NE, DH])
        o_t = sb("o_t", [P, GW])
        gl = sb("gl", [P, GT, NE]); gl_max = sb("gl_max", [P, GT]); gl_low = sb("gl_low", [P, GT, NE]); gl_ex = sb("gl_ex", [P, GT, NE])
        gl_sum = sb("gl_sum", [P, GT]); gl_inv = sb("gl_inv", [P, GT]); gate = sb("gate", [P, GT, NE])
        prod = sb("prod", [P, GT, NE, DH])
        mixed = sb("mixed", [P, GT, NH, DH])
        m = sb("m", [P, GT, NH, DH]); hstats = sb("hstats", [P, BLK, 6]); hmv = sb("hmv", [P, BLK, 2]); hve = sb("hve", [P, BLK]); hrstd = sb("hrstd", [P, BLK])
        ln0 = sb("ln0", [P, BLK, DH]); fx = sb("fx", [P, BLK, DH])
        fx_t = sb("fx_t", [P, GW]); r1 = sb("r1", [P, GW]); h1 = r1; t2 = sb("t2", [P, BLK, DH]); t3 = sb("t3", [P, BLK, DH])
        fo_t = fx_t
        ps_s = [ps("ps_s0", [P, NE * P]), ps("ps_s1", [P, NE * N])]
        ps_t = [ps(f"ps_t{i}", [P, NE, P]) for i in range(2)]
        ps_o = ps("ps_o", [P, 512])
        ps_r = ps("ps_r", [P, 512])
        ps_m = ps("ps_m", [P, GW])
        s = named_semaphores(nc, c, "l2f", "stats_done var_ready veps_ready rstd_ready xn_ready weights zeroed const bank_psum bank_read"
                             " s_psum masked exp_ready t_psum t_ready pv_psum raw_copied raw_turned inv_ready o_raw_ready o_ready chain gl_ready gl_exp gate_ready prod_ready"
                             " mixed_ready hve_ready hrstd_ready ln0_ready ln1_ready fx_ready h1_ready x_done k_loaded0 k_loaded1 k_loaded2 k_loaded3")
        k_loaded = [s["k_loaded0"], s["k_loaded1"], s["k_loaded2"], s["k_loaded3"]]
        CH = 40
        og_max = sb("og_max", [P, GT]); og_low = sb("og_low", [P, GT, NH]); og_ex = sb("og_ex", [P, GT, NH])
        og_sum = sb("og_sum", [P, GT]); og_inv = sb("og_inv", [P, GT]); og = sb("og", [P, GT, NH])

        with nc.Block() as block:
            @block.sync
            def _(e):
                loads = [(hl[:, :], a["L2_ffn_hl_w_t"]), (hl_b[:, :], a["L2_ffn_hl_b"].rearrange("n (d a) -> (n d) a", a=1)),
                         (gate_w[:, :, :], a["L2_ffn_gate_w_t"]),
                         (gate_b[:, :, :].rearrange("p n e -> p (n e)"), a["L2_ffn_gate_b"].rearrange("n e -> (n e)").partition_broadcast(P)),
                         (fgate[:, :], a["L2_ffn_fgate_t"])]
                for dst, src in ((ln_g, "ln_g"), (ln_b, "ln_b"), (fn_g, "fnorm_g"), (fn_b, "fnorm_b"), (fc2_b, "fc2_b")):
                    loads.append((dst[:, :], a["L2_ffn_" + src].partition_broadcast(P)))
                for n in range(NH):
                    r = slice(n * DH, (n + 1) * DH)
                    loads.append((fc1_b[r, :], a["L2_ffn_fc1_b"].rearrange("(p a) -> p a", a=1)))
                for dst, src in loads:
                    e.dma_start(dst, src).then_inc(s["weights"], 16)
                e.wait_ge(s["zeroed"], 1)
                blocks = []
                for n in range(NH):
                    r = slice(n * DH, (n + 1) * DH)
                    blocks += [(wq[r, n, :], a["L2_ffn_wq_t"][n].rearrange("d e o -> d (e o)")), (wk[r, r], a["L2_ffn_wk_t"][n]),
                               (wv[r, r], a["L2_ffn_wv_t"][n]), (fc1[r, r], a["L2_ffn_fc1_t"]), (fc2[r, r], a["L2_ffn_fc2_t"])]
                for dst, src in blocks:
                    e.dma_start(dst, src).then_inc(s["weights"], 16)
                assert 16 * (len(loads) + len(blocks)) == WEIGHTS

                def keys(g, uses):
                    for n in range(NH):
                        if n == 0:
                            e.wait_ge(s["bank_read"], uses[("next", "keys")])
                        e.wait_ge(s["s_psum"], g * UNITS + 4 * n + 4)
                        for x in range(NE):
                            e.dma_start(k_diag[x * DH:(x + 1) * DH, n, x, :], k_t[n * DH:(n + 1) * DH, :]).then_inc(k_loaded[n], 16)

                def body(g, p, has_prev, has_next):
                    if has_next:
                        keys(g + 1, bank_uses(g, has_prev, has_next))
                e.wait_ge(s["zeroed"], 2)
                keys(0, front_uses())
                over_groups_lagged(e, body)

            @block.gpsimd
            def _(e):
                for z in (wq[:, :, :], wk[:, :], wv[:, :], fc1[:, :], fc2[:, :]):
                    last = e.memset(z, 0.0)
                last.then_inc(s["zeroed"], 1)
                e.memset(causal[:, :], 0.0)
                e.memset(head_eps[:, :], HEAD_EPS)
                e.memset(k_diag[:, :, :, :], 0.0).then_inc(s["zeroed"], 1)
                e.wait_ge(s["zeroed"], 2)
                e.affine_select(out=causal[:, P:N], in_=causal[:, P:N], compare_op=ALU.is_ge, fill=CAUSAL, base=0,
                                pattern=[[-1, P]], channel_multiplier=1).then_inc(s["const"], 1)

                def head_product(g, n):
                    e.wait_ge(s["gate_ready"], g * NH + n + 1)
                    e.tensor_tensor(prod[:, :, :, :].rearrange("p t e d -> p (t e) d"), o[:, n % 2].rearrange("p t e d -> p (t e) d"),
                                    gate[:, :, :].rearrange("p t e -> p (t e)").unsqueeze(2).broadcast_to([P, GT * NE, DH]), ALU.mult
                                    ).then_inc(s["prod_ready"], 1)

                def head_rstd(k):
                    e.wait_ge(s["mixed_ready"], k + 1)
                    e.tensor_tensor(hve[:, :], hmv[:, :, 1], head_eps[:, :], ALU.add).then_inc(s["hve_ready"], 1)
                    e.wait_ge(s["hve_ready"], k + 1)
                    e.tensor_tensor(hrstd[:, :], hve[:, :], w.minus_half[:, 0:BLK], ALU.pow).then_inc(s["hrstd_ready"], 1)

                def head_affine(k, gain, shift):
                    e.wait_ge(s["ln0_ready"], k + 1)
                    e.tensor_tensor(ln0[:, :, :], ln0[:, :, :], gain[:, :].unsqueeze(1).broadcast_to([P, BLK, DH]), ALU.mult).then_inc(s["ln1_ready"], 1)
                    e.wait_ge(s["ln1_ready"], k + 1)
                    e.tensor_tensor(fx[:, :, :], ln0[:, :, :], shift[:, :].unsqueeze(1).broadcast_to([P, BLK, DH]), ALU.add).then_inc(s["fx_ready"], 1)

                def back_rest(g):
                    head_product(g, 3)
                    head_rstd(2 * g)
                    head_affine(2 * g, ln_g, ln_b)

                def back_last(g):
                    head_rstd(2 * g + 1)

                def body(g, p, has_prev, has_next):
                    if has_next:
                        norm_rstd(e, s, w, g + 1, 1 - p)
                    if has_prev:
                        head_product(g - 1, 2)
                        back_rest(g - 1)
                    head_product(g, 0)
                    if has_prev:
                        back_last(g - 1)
                    head_product(g, 1)
                    if has_prev:
                        head_affine(2 * (g - 1) + 1, fn_g, fn_b)
                e.wait_ge(s["weights"], WEIGHTS)
                norm_rstd(e, s, w, 0, 0)
                over_groups_lagged(e, body)
                head_product(GROUPS - 1, 2)
                back_rest(GROUPS - 1)
                back_last(GROUPS - 1)
                head_affine(2 * GROUPS - 1, fn_g, fn_b)

            def width(t):
                return P * (t % 2 + 1)

            @block.vector
            def _(e):
                e.sem_inc(s["masked"], 2)
                e.wait_ge(s["weights"], WEIGHTS)
                e.wait_ge(s["const"], 1)
                count = [None]

                def start_chain(g, first=0):
                    count[0] = (g, first)

                def step(i):
                    g, k = count[0]
                    i.then_inc(s["chain"], 1)
                    count[0] = (g, k + 1)
                    e.wait_ge(s["chain"], g * CH + k + 1)

                def end_chain():
                    g, k = count[0]
                    assert k <= CH, k
                    if k < CH:
                        e.sem_inc(s["chain"], CH - k)

                def apply(g, p):
                    norm_apply(e, s, w, g, p)

                def take_heads_turn(g, p, use):
                    e.wait_ge(s["bank_psum"], use)
                    i = e.tensor_scalar(not_pad[:, p].rearrange("p t d -> p (t d)"), ps_m[:, :], 0.0, None, ALU.not_equal)
                    if isinstance(g, int) and 2 * g < NH:
                        for b in range(2):
                            n = 2 * g + b
                            for t in range(2):
                                i = e.tensor_copy(resid[:, t, n * DH:(n + 1) * DH], ps_m[:, (2 * b + t) * D + n * DH:(2 * b + t) * D + (n + 1) * DH])
                    i.then_inc(s["bank_read"], 1)

                def take_values(g, p, use):
                    e.wait_ge(s["bank_psum"], use)
                    e.tensor_copy(v[:, p, :, :, 0:DH].rearrange("p t n d -> p (t n) d"), ps_m[:, :].rearrange("p (x d) -> p x d", d=DH)).then_inc(s["bank_read"], 1)

                def take_gate(n, use):
                    e.wait_ge(s["bank_psum"], use)
                    e.tensor_tensor(gl[:, :, :], ps_m[:, 0:GT * NE].rearrange("p (t e) -> p t e", e=NE),
                                    gate_b[:, n, :].unsqueeze(1).broadcast_to([P, GT, NE]), ALU.add).then_inc(s["bank_read"], 1)
                    e.wait_ge(s["bank_read"], use)
                    step(e.tensor_reduce(gl_max[:, :], gl[:, :, :], AX.X, ALU.max))
                    e.tensor_tensor(gl_low[:, :, :], gl[:, :, :], gl_max[:, :].unsqueeze(2).broadcast_to([P, GT, NE]), ALU.subtract).then_inc(s["gl_ready"], 1)

                def gate_values(exps_done):
                    e.wait_ge(s["gl_exp"], exps_done)
                    step(e.tensor_reduce(gl_sum[:, :], gl_ex[:, :, :], AX.X, ALU.add))
                    step(e.reciprocal(gl_inv[:, :], gl_sum[:, :]))
                    e.tensor_tensor(gate[:, :, :], gl_ex[:, :, :], gl_inv[:, :].unsqueeze(2).broadcast_to([P, GT, NE]), ALU.mult).then_inc(s["gate_ready"], 1)

                def gate_sum(g, n):
                    e.wait_ge(s["prod_ready"], g * NH + n + 1)
                    step(e.tensor_reduce(mixed[:, :, n, :], prod[:, :, :, :].rearrange("p t e d -> p t d e"), AX.X, ALU.add))

                def block_stats(src):
                    for b in range(BLK):
                        i = e.bn_stats(hstats[:, b, :], src[:, b, :])
                    step(i)
                    e.sem_inc(w.passed, 1)
                    for b in range(BLK):
                        i = e.bn_aggr(hmv[:, b, :], hstats[:, b, :])
                    i.then_inc(s["mixed_ready"], 1)

                def block_apply(k, src):
                    wide = lambda v: v.unsqueeze(2).broadcast_to([P, BLK, DH])
                    e.wait_ge(s["hrstd_ready"], k + 1)
                    step(e.tensor_tensor(ln0[:, :, :], src, wide(hmv[:, :, 0]), ALU.subtract))
                    e.tensor_tensor(ln0[:, :, :], ln0[:, :, :], wide(hrstd[:, :]), ALU.mult).then_inc(s["ln0_ready"], 1)

                def back1(g):
                    for b in range(2):
                        i = e.tensor_tensor(m[:, 2 * b:2 * b + 2].rearrange("p t n d -> p t (n d)"), mixed[:, 2 * b:2 * b + 2].rearrange("p t n d -> p t (n d)"),
                                            resid[:, :, :], ALU.add)
                    step(i)
                    block_stats(m[:, :, :, :].rearrange("p t n d -> p (t n) d"))

                def back2(g):
                    block_apply(2 * g, m[:, :, :, :].rearrange("p t n d -> p (t n) d"))

                def back_h1(g, use):
                    e.wait_ge(s["bank_read"], use)
                    e.scalar_tensor_tensor(h1[:, :], fx_t[:, :], 0.0, r1[:, :], ALU.not_equal, ALU.mult).then_inc(s["h1_ready"], 1)

                def back_ff2(g, use):
                    e.wait_ge(s["bank_psum"], use)
                    e.tensor_tensor(t2[:, :, :], ps_m[:, :].rearrange("p (x d) -> p x d", d=DH), fc2_b[:, :].unsqueeze(1).broadcast_to([P, BLK, DH]),
                                    ALU.add).then_inc(s["bank_read"], 1)

                def back3(g, use):
                    e.wait_ge(s["bank_read"], use)
                    step(e.scalar_tensor_tensor(t3[:, :, :], fx[:, :, :], 0.0, t2[:, :, :], ALU.not_equal, ALU.mult))
                    step(e.tensor_tensor(t2[:, :, :], t3[:, :, :], fx[:, :, :], ALU.add))
                    block_stats(t2)

                def back4(g):
                    block_apply(2 * g + 1, t2[:, :, :])

                def back_logits(g, use):
                    e.wait_ge(s["bank_psum"], use)
                    step(e.tensor_reduce(og_max[:, :], ps_m[:, 0:GT * NH].rearrange("p (t n) -> p t n", n=NH), AX.X, ALU.max))
                    e.tensor_tensor(og_low[:, :, :], ps_m[:, 0:GT * NH].rearrange("p (t n) -> p t n", n=NH),
                                    og_max[:, :].unsqueeze(2).broadcast_to([P, GT, NH]), ALU.subtract).then_inc(s["bank_read"], 1)

                def back_final(g, exps_done):
                    e.wait_ge(s["gl_exp"], exps_done)
                    step(e.tensor_reduce(og_sum[:, :], og_ex[:, :, :], AX.X, ALU.add))
                    step(e.reciprocal(og_inv[:, :], og_sum[:, :]))
                    step(e.tensor_tensor(og[:, :, :], og_ex[:, :, :], og_inv[:, :].unsqueeze(2).broadcast_to([P, GT, NH]), ALU.mult))
                    step(e.tensor_tensor(t3[:, :, :], fx[:, :, :], og[:, :, :].rearrange("p t n -> p (t n)").unsqueeze(2).broadcast_to([P, BLK, DH]), ALU.mult))
                    xg = w.x[:, span(g, GW)]
                    e.tensor_tensor(xg, xg, t3[:, :, :].rearrange("p x d -> p (x d)"), ALU.add).then_inc(s["x_done"], 1)

                def mask_unit(g, u):
                    k = g * UNITS + u
                    q, t = u % 2, u % GT
                    wd = width(t)
                    e.wait_ge(s["t_psum"], k + 3)
                    wait_apart(e, w, s["s_psum"], k + 1 + UNITS)
                    for x in range(NE):
                        i = e.tensor_tensor_reduce(scores[:, q, x * wd:(x + 1) * wd], ps_s[q][:, x * wd:(x + 1) * wd], causal[:, N - wd:N],
                                                   1.0, BIG, ALU.add, ALU.min, row_min[:, q, x:x + 1])
                    i.then_inc(s["masked"], 1)

                def normalise(g, p, u):
                    k = g * UNITS + u
                    n, t = u // GT, u % GT
                    e.wait_ge(s["exp_ready"], k + 1 + 2)
                    e.reciprocal(inv_sum[:, :], row_sum[:, u % 4, :]).then_inc(s["inv_ready"], 1)
                    e.wait_ge(s["inv_ready"], k + 1)
                    e.wait_ge(s["raw_turned"], k + 1)
                    e.tensor_tensor(o_raw[:, :, :], ps_r[:, 0:P].rearrange("p (x d) -> p x d", d=DH), inv_sum[:, :].unsqueeze(2).broadcast_to([P, NE, DH]), ALU.mult).then_inc(s["o_raw_ready"], 1)
                    if t == 0 and not (isinstance(g, int) and g * NH + n < 2):
                        e.wait_ge(s["prod_ready"], g * NH + n - 1)
                    e.wait_ge(s["o_raw_ready"], k + 2)
                    e.tensor_tensor(o[:, n % 2, t], o_raw[:, :, :], not_pad[:, p, t, n * DH:(n + 1) * DH].unsqueeze(1).broadcast_to([P, NE, DH]),
                                    ALU.mult).then_inc(s["o_ready"], 1)

                def body(g, p, has_prev, has_next):
                    uses = bank_uses(g, has_prev, has_next)
                    start_chain(g)
                    for u in range(UNITS):
                        if u + 1 < UNITS:
                            mask_unit(g, u + 1)
                        if u >= 2:
                            normalise(g, p, u - 2)
                        elif has_prev and u == 0:
                            normalise(g - 1, 1 - p, UNITS - 1)
                        if has_next and u == 0:
                            norm_stats(e, s, w, g + 1, 1 - p)
                        if has_prev and u == 0:
                            gate_values(gate_count(g, "prev2", True))
                        if has_prev and u == 1:
                            gate_sum(g - 1, 2)
                        if has_next and u == 1:
                            apply(g + 1, 1 - p)
                        if has_prev and u == 2:
                            take_gate(3, uses[("prev", "gate_logits3")])
                        if has_prev and u == 3:
                            gate_values(gate_count(g, "prev3", True))
                        if has_prev and u == 4:
                            gate_sum(g - 1, 3)
                        if has_next and u == 5:
                            take_heads_turn(g + 1, 1 - p, uses[("next", "heads_turn")])
                        if has_prev and u == 5:
                            back1(g - 1)
                        if has_prev and u == 6:
                            back2(g - 1)
                        if u == 7:
                            take_gate(0, uses[("own", "gate_logits0")])
                        if u == 8:
                            gate_values(gate_count(g, "own0", has_prev))
                            if has_next:
                                take_values(g + 1, 1 - p, uses[("next", "values")])
                        if u == 9:
                            gate_sum(g, 0)
                            if has_prev:
                                back_h1(g - 1, uses[("prev", "ff1")])
                        if has_prev and u == 10:
                            back_ff2(g - 1, uses[("prev", "ff2")])
                        if u == 11:
                            take_gate(1, uses[("own", "gate_logits1")])
                            if has_prev:
                                back3(g - 1, uses[("prev", "ff2")])
                        if u == 12:
                            gate_values(gate_count(g, "own1", has_prev))
                        if u == 13:
                            gate_sum(g, 1)
                            if has_prev:
                                back4(g - 1)
                        if u == 15:
                            take_gate(2, uses[("own", "gate_logits2")])
                    if has_next:
                        mask_unit(g + 1, 0)
                    normalise(g, p, UNITS - 2)
                    if has_prev:
                        back_logits(g - 1, uses[("prev", "out_logits")])
                        back_final(g - 1, gate_count(g, "out", True))
                    end_chain()

                norm_stats(e, s, w, 0, 0)
                apply(0, 0)
                uses = front_uses()
                take_heads_turn(0, 0, uses[("next", "heads_turn")])
                take_values(0, 0, uses[("next", "values")])
                mask_unit(0, 0)
                over_groups_lagged(e, body)
                g, uses = GROUPS - 1, tail_uses()
                start_chain(GROUPS)
                normalise(g, 1, UNITS - 1)
                gate_values(gate_count(GROUPS, "prev2", True))
                gate_sum(g, 2)
                take_gate(3, uses[("prev", "gate_logits3")])
                gate_values(gate_count(GROUPS, "prev3", True))
                gate_sum(g, 3)
                back1(g)
                back2(g)
                back_h1(g, uses[("prev", "ff1")])
                back_ff2(g, uses[("prev", "ff2")])
                back3(g, uses[("prev", "ff2")])
                back4(g)
                back_logits(g, uses[("prev", "out_logits")])
                back_final(g, gate_count(GROUPS, "prev3", True) + 1)

            @block.tensor
            def _(e):
                e.sem_inc(s["s_psum"], UNITS)
                e.sem_inc(s["t_psum"], 4)
                e.sem_inc(s["pv_psum"], 2)
                e.sem_inc(s["o_raw_ready"], 1)
                e.wait_ge(s["weights"], WEIGHTS)

                def use(kind, name, count, g, p):
                    if not (isinstance(count, int) and count == 1):
                        e.wait_ge(s["bank_read"], count - 1)
                    if name == "turn_x":
                        e.wait_ge(s["xn_ready"], g + 1)
                        for t in range(GT):
                            i = e.transpose(ps_m[:, t * P:(t + 1) * P], w.xn[:, p, t, :], w.ident[:, :])
                    elif name == "heads":
                        i = e.matmul(ps_m[:, :], hl[:, :], w.xt[:, p, :], start=True, stop=True)
                    elif name == "heads_turn":
                        for t in range(GT):
                            i = e.transpose(ps_m[:, t * P:(t + 1) * P], sx_t[:, t * P:(t + 1) * P], w.ident[:, :])
                    elif name == "keys":
                        i = e.matmul(ps_m[:, :], wk[:, :], sx_t[:, :], start=True, stop=True)
                    elif name == "values":
                        for t in range(GT):
                            i = e.matmul(ps_m[:, t * D:(t + 1) * D], sx_t[:, t * P:(t + 1) * P], wv[:, :], start=True, stop=True)
                    elif name.startswith("query"):
                        i = e.matmul(ps_m[:, :], wq[:, int(name[-1]), :], sx_t[:, :], start=True, stop=True)
                    elif name.startswith("gate_turn"):
                        n = int(name[-1])
                        e.wait_ge(s["o_ready"], g * UNITS + 4 * n + 4)
                        for t in range(GT):
                            i = e.transpose(ps_m[:, t * P:(t + 1) * P], o[:, n % 2, t].rearrange("p e d -> p (e d)"), w.ident[:, :])
                    elif name.startswith("gate_logits"):
                        n = int(name[-1])
                        for t in range(GT):
                            i = e.matmul(ps_m[:, t * NE:(t + 1) * NE], o_t[:, t * P:(t + 1) * P], gate_w[:, n, :], start=True, stop=True)
                    elif name in ("ff_turn", "out_turn"):
                        e.wait_ge(s["fx_ready"], 2 * g + (1 if name == "ff_turn" else 2))
                        for t in range(GT):
                            i = e.transpose(ps_m[:, t * P:(t + 1) * P], fx[:, t * NH:(t + 1) * NH, :].rearrange("p n d -> p (n d)"), w.ident[:, :])
                    elif name == "ff1":
                        i = e.matmul(ps_m[:, :], fc1[:, :], fx_t[:, :], start=True, stop=True)
                    elif name == "ff2":
                        e.wait_ge(s["h1_ready"], g + 1)
                        for t in range(GT):
                            i = e.matmul(ps_m[:, t * D:(t + 1) * D], h1[:, t * P:(t + 1) * P], fc2[:, :], start=True, stop=True)
                    else:
                        assert name == "out_logits"
                        for t in range(GT):
                            i = e.matmul(ps_m[:, t * NH:(t + 1) * NH], fo_t[:, t * P:(t + 1) * P], fgate[:, :], start=True, stop=True)
                    i.then_inc(s["bank_psum"], 1)

                def score(g, u):
                    k = g * UNITS + u
                    n, t = u // GT, u % GT
                    wd = width(t)
                    if t == 0:
                        e.wait_ge(k_loaded[n], g * 64 + 64)
                    e.wait_ge(s["masked"], k + 1)
                    step = 512 // wd
                    for x in range(0, NE, step):
                        keys = k_diag[:, n, x:x + step, t // 2 * N:t // 2 * N + wd]
                        i = e.matmul(ps_s[u % 2][:, x * wd:(x + step) * wd], q_t[:, n, t * P:(t + 1) * P], keys, start=True, stop=True)
                    i.then_inc(s["s_psum"], 1)

                def turn(g, u):
                    k = g * UNITS + u
                    t = u % GT
                    wd = width(t)
                    e.wait_ge(s["exp_ready"], k + 1 + 2)
                    for kt in range(t % 2 + 1):
                        e.wait_ge(s["t_ready"], k + 1)
                        for x in range(NE):
                            i = e.transpose(ps_t[kt][:, x, :], probs[:, u % 2, x * wd + kt * P:x * wd + (kt + 1) * P], w.ident[:, :])
                    i.then_inc(s["t_psum"], 1)

                def weigh(g, p, u):
                    k = g * UNITS + u
                    n, t = u // GT, u % GT
                    e.wait_ge(s["t_ready"], k + 2)
                    for x in range(NE):
                        for kt in range(t % 2 + 1):
                            i = e.matmul(ps_o[x * DH:(x + 1) * DH, 0:P], v[:, p, t // 2 * 2 + kt, n, :], probs_t[:, u % 2, kt, x, :],
                                         start=kt == 0, stop=kt == t % 2)
                    i.then_inc(s["pv_psum"], 1)

                def turn_back(g, u):
                    e.wait_ge(s["raw_copied"], g * UNITS + u + 1)
                    e.wait_ge(s["o_raw_ready"], g * UNITS + u + 1)
                    e.transpose(ps_r[:, 0:P], raw_t[:, :], w.ident[:, :]).then_inc(s["raw_turned"], 1)

                def body(g, p, has_prev, has_next):
                    uses = bank_uses(g, has_prev, has_next)
                    group = {"prev": (g - 1, 1 - p), "own": (g, p), "next": (g + 1, 1 - p)}
                    for u in range(UNITS):
                        if u + 1 < UNITS:
                            score(g, u + 1)
                        if u >= 2:
                            turn_back(g, u - 2)
                        elif has_prev and u == 0:
                            turn_back(g - 1, UNITS - 1)
                        if u:
                            weigh(g, p, u - 1)
                        mine = [x for x in SLOTS[u] if x in uses and x[1] not in ("out_logits", "query3")]
                        for x in mine[:1]:
                            use(*x, uses[x], *group[x[0]])
                        turn(g, u)
                        for x in mine[1:]:
                            use(*x, uses[x], *group[x[0]])
                    if has_next:
                        x = ("next", "query3")
                        use(*x, uses[x], *group["next"])
                        score(g + 1, 0)
                    turn_back(g, UNITS - 2)
                    weigh(g, p, UNITS - 1)
                    if has_prev:
                        x = ("prev", "out_logits")
                        use(*x, uses[x], *group["prev"])
                for x, k in front_uses().items():
                    use(*x, k, 0, 0)
                score(0, 0)
                over_groups_lagged(e, body)
                turn_back(GROUPS - 1, UNITS - 1)
                for x, k in tail_uses().items():
                    use(*x, k, GROUPS - 1, 1)

            @block.scalar
            def _(e):
                e.sem_inc(s["exp_ready"], 2)
                e.sem_inc(s["t_ready"], 1)
                e.preload_act_table(ACT.Exp)
                e.wait_ge(s["weights"], WEIGHTS)

                def take(name, count, g, p):
                    if name in ("heads_turn", "values", "ff2", "out_logits") or name.startswith("gate_logits"):
                        return
                    e.wait_ge(s["bank_psum"], count)
                    if name == "turn_x":
                        i = e.activation(w.xt[:, p, :], ps_m[:, :], ACT.Copy)
                    elif name == "heads":
                        i = e.activation(sx_t[:, :], ps_m[:, :], ACT.Identity, bias=hl_b[:, 0:1])
                    elif name == "keys":
                        if not isinstance(g, int) or g:
                            for k in k_loaded:
                                e.wait_ge(k, g * 64)
                        i = e.activation(k_t[:, :], ps_m[:, :], ACT.Copy)
                    elif name.startswith("query"):
                        n = int(name[-1])
                        e.wait_ge(s["s_psum"], g * UNITS + 4 * n + 4)
                        e.activation(q_t[:, n, :], ps_m[:, :], ACT.Copy, scale=-float(DH) ** 0.5).then_inc(s["bank_read"], 1)
                        return
                    elif name.startswith("gate_turn"):
                        i = e.activation(o_t[:, :], ps_m[:, :], ACT.Copy)
                    elif name == "ff_turn":
                        i = e.activation(fx_t[:, :], ps_m[:, :], ACT.Copy)
                    elif name == "ff1":
                        i = e.activation(r1[:, :], ps_m[:, :], ACT.Relu, bias=fc1_b[:, 0:1])
                    else:
                        assert name == "out_turn"
                        i = e.activation(fo_t[:, :], ps_m[:, :], ACT.Copy)
                    i.then_inc(s["bank_read"], 1)

                def exps(g, u):
                    k = g * UNITS + u
                    wd = width(u % GT)
                    e.wait_ge(s["masked"], k + 1 + 2)
                    for x in range(NE):
                        i = e.activation(probs[:, u % 2, x * wd:(x + 1) * wd], scores[:, u % 2, x * wd:(x + 1) * wd], ACT.Exp,
                                         bias=row_min[:, u % 2, x:x + 1], scale=-1.0, accum_out=row_sum[:, u % 4, x:x + 1])
                    i.then_inc(s["exp_ready"], 1)

                def copy_raw(g, u):
                    k = g * UNITS + u
                    e.wait_ge(s["pv_psum"], k + 1 + 2)
                    e.activation(raw_t[:, :], ps_o[:, 0:P], ACT.Copy).then_inc(s["raw_copied"], 1)

                def copy_t(g, u):
                    k = g * UNITS + u
                    e.wait_ge(s["t_psum"], k + 1 + 4)
                    e.wait_ge(s["pv_psum"], k + 1)
                    for kt in range(u % GT % 2 + 1):
                        i = e.activation(probs_t[:, u % 2, kt], ps_t[kt][:, :, :], ACT.Copy)
                    i.then_inc(s["t_ready"], 1)

                def head_gate(g, n):
                    e.wait_ge(s["gl_ready"], g * NH + n + 1)
                    e.activation(gl_ex[:, :, :], gl_low[:, :, :], ACT.Exp).then_inc(s["gl_exp"], 1)

                def out_gate(use):
                    e.wait_ge(s["bank_read"], use)
                    e.activation(og_ex[:, :, :], og_low[:, :, :], ACT.Exp).then_inc(s["gl_exp"], 1)

                def body(g, p, has_prev, has_next):
                    uses = bank_uses(g, has_prev, has_next)
                    group = {"prev": (g - 1, 1 - p), "own": (g, p), "next": (g + 1, 1 - p)}
                    for u in range(UNITS):
                        if has_prev and u == 0:
                            head_gate(g - 1, 2)
                        if has_prev and u == 3:
                            head_gate(g - 1, 3)
                        if u == 8:
                            head_gate(g, 0)
                        if u == 12:
                            head_gate(g, 1)
                        mine = [x for x in SLOTS[u] if x in uses and x[1] not in ("out_logits", "query3")]
                        if u:
                            copy_raw(g, u - 1)
                        for x in mine[:1]:
                            take(x[1], uses[x], *group[x[0]])
                        copy_t(g, u)
                        for x in mine[1:2]:
                            take(x[1], uses[x], *group[x[0]])
                        if u + 1 < UNITS:
                            exps(g, u + 1)
                        for x in mine[2:]:
                            take(x[1], uses[x], *group[x[0]])
                    if has_next:
                        take("query3", uses[("next", "query3")], g + 1, 1 - p)
                    copy_raw(g, UNITS - 1)
                    if has_next:
                        exps(g + 1, 0)
                    if has_prev:
                        out_gate(uses[("prev", "out_logits")])
                for x, k in front_uses().items():
                    take(x[1], k, 0, 0)
                exps(0, 0)
                over_groups_lagged(e, body)
                g, uses = GROUPS - 1, tail_uses()
                head_gate(g, 2)
                take("gate_turn3", uses[("prev", "gate_turn3")], g, 1)
                head_gate(g, 3)
                for name in ("ff_turn", "ff1", "out_turn"):
                    take(name, uses[("prev", name)], g, 1)
                out_gate(uses[("prev", "out_logits")])


WEIGHTS = 16 * (5 + 5 + 4 + 5 * NH)


def l3_gnn(nc, w, a):
    graph_attention(nc, w, a, "l3g", "L3_gnn_W", False)


E3 = 6
R3 = D // 2
PAD = 8


def l3_ffn(nc, w, a):
    with ExitStack() as c:
        sb = lambda n, shape, dt=F32: c.enter_context(nc.sbuf_tensor("l3f_" + n, shape, dt))
        ps = lambda n, shape: c.enter_context(nc.psum_tensor("l3f_" + n, shape, F32))
        w1 = sb("w1", [P, E3, D]); w2 = sb("w2", [P, E3, D]); w3 = sb("w3", [P, E3, D])
        b1 = sb("b1", [P, E3]); b2 = sb("b2", [P, E3]); b3 = sb("b3", [E3, D])
        rw1 = sb("rw1", [P, R3]); rb1 = sb("rb1", [R3, 1]); rw2 = sb("rw2", [R3, E3]); rb2 = sb("rb2", [P, E3])
        iota = sb("iota", [P, E3])
        r_t = sb("r_t", [R3, 2, GW])
        lg = sb("lg", [P, 2, GT, E3])
        row_max = sb("row_max", [P, 2, GT])
        logits = sb("logits", [P, 2, GT, E3])
        expo = sb("expo", [P, 2, GT, E3])
        total = sb("total", [P, 2, GT])
        inv_total = sb("inv_total", [P, 2, GT])
        prob = sb("prob", [P, 2, GT, PAD])
        best = sb("best", [P, 2, GT, 8])
        best_at = sb("best_at", [P, 2, GT, 8], U32)
        best_f = sb("best_f", [P, 2, GT, 8])
        diff = sb("diff", [P, 2, GT, 2])
        top = sb("top", [P, 2, GT, 2])
        top_total = sb("top_total", [P, 2, GT])
        inv_top = sb("inv_top", [P, 2, GT])
        weight = sb("weight", [P, 2, GT, 2])
        hit = sb("hit", [P, 2, 2, GT, E3])
        mask = sb("mask", [P, 2, GT, E3])
        mask_t = sb("mask_t", [E3, 2, GW])
        h1 = sb("h1", [P, 2, GW]); h2 = sb("h2", [P, 2, GW])
        ps_1 = [ps(f"ps_1{i}", [P, 512]) for i in range(2)]
        ps_2 = [ps(f"ps_2{i}", [P, 512]) for i in range(2)]
        ps_y = [ps(f"ps_y{i}", [P, 512]) for i in range(2)]
        ps_t = ps("ps_t", [P, 512])
        ps_m = ps("ps_m", [P, 512])
        s = named_semaphores(nc, c, "l3f", NORM_SEMS + " router experts const pads r_psum r_ready logit_psum lg_ready max_ready logit_ready"
                             " exp_ready chain diff_ready top_ready mask_ready mask_psum mask_t_ready bias_psum bias_added h1_psum h1_ready h2_psum h2_ready"
                             " y_psum y_added")
        LINKS = 8
        with nc.Block() as block:
            @block.sync
            def _(e):
                for dst, src in ((rw1[:, :], a["L3_ffn_router_w1"]), (rb1[:, :], a["L3_ffn_router_b1"].rearrange("(p a) -> p a", a=1)),
                                 (rw2[:, :], a["L3_ffn_router_w2"]), (rb2[:, :], a["L3_ffn_router_b2"].partition_broadcast(P)),
                                 (b1[:, :], a["L3_ffn_b1_t"]), (b2[:, :], a["L3_ffn_b2_t"]), (b3[:, :], a["L3_ffn_expert_b3"])):
                    e.dma_start(dst, src).then_inc(s["router"], 16)
                for dst, src in ((w1[:, :, :], a["L3_ffn_expert_w1"].rearrange("e d h -> d e h")),
                                 (w2[:, :, :], a["L3_ffn_expert_w2"].rearrange("e d h -> d e h")),
                                 (w3[:, :, :], a["L3_ffn_expert_w3"].rearrange("e d h -> d e h"))):
                    e.dma_start(dst, src).then_inc(s["experts"], 16)

            def wide(v, n):
                return v.unsqueeze(2).broadcast_to([P, GT, n])

            def route_logits(e, g, p):
                e.wait_ge(s["logit_psum"], g + 1)
                e.tensor_tensor(lg[:, p], ps_m[:, 0:GT * E3].rearrange("p (t e) -> p t e", e=E3),
                                rb2[:, :].unsqueeze(1).broadcast_to([P, GT, E3]), ALU.add).then_inc(s["lg_ready"], 1)
                e.wait_ge(s["lg_ready"], g + 1)
                e.tensor_reduce(row_max[:, p, :], lg[:, p], AX.X, ALU.max).then_inc(s["max_ready"], 1)
                e.wait_ge(s["max_ready"], g + 1)
                e.tensor_tensor(logits[:, p], lg[:, p], wide(row_max[:, p, :], E3), ALU.subtract).then_inc(s["logit_ready"], 1)

            def route_best(e, g, p):
                at = g * LINKS
                e.wait_ge(s["exp_ready"], g + 1)
                e.tensor_reduce(total[:, p, :], expo[:, p], AX.X, ALU.add).then_inc(s["chain"], 1)
                e.wait_ge(s["chain"], at + 1)
                e.reciprocal(inv_total[:, p, :], total[:, p, :]).then_inc(s["chain"], 1)
                e.wait_ge(s["chain"], at + 2)
                e.tensor_tensor(prob[:, p, :, 0:E3], expo[:, p], wide(inv_total[:, p, :], E3), ALU.mult).then_inc(s["chain"], 1)
                wait_apart(e, w, s["chain"], at + 3)
                for t in range(GT):
                    last = e.max(best[:, p, t, :], prob[:, p, t, :])
                last.then_inc(s["chain"], 1)
                wait_apart(e, w, s["chain"], at + 4)
                e.tensor_tensor(diff[:, p], best[:, p, :, 0:2], wide(best[:, p, :, 0], 2), ALU.subtract).then_inc(s["diff_ready"], 1)
                for t in range(GT):
                    last = e.max_index(best_at[:, p, t, :], best[:, p, t, :], prob[:, p, t, :])
                last.then_inc(s["chain"], 1)
                e.wait_ge(s["chain"], at + 5)
                e.tensor_copy(best_f[:, p], best_at[:, p])

            def route_mask(e, g, p):
                at = g * LINKS
                e.wait_ge(s["top_ready"], g + 1)
                e.tensor_tensor(top_total[:, p, :], top[:, p, :, 0], top[:, p, :, 1], ALU.add).then_inc(s["chain"], 1)
                e.wait_ge(s["chain"], at + 6)
                e.reciprocal(inv_top[:, p, :], top_total[:, p, :]).then_inc(s["chain"], 1)
                e.wait_ge(s["chain"], at + 7)
                e.tensor_tensor(weight[:, p], top[:, p], wide(inv_top[:, p, :], 2), ALU.mult).then_inc(s["chain"], 1)
                e.wait_ge(s["chain"], at + 8)
                for t in range(GT):
                    for k in range(2):
                        last = e.tensor_scalar(hit[:, p, k, t, :], iota[:, :], best_f[:, p, t, k:k + 1],
                                               weight[:, p, t, k:k + 1], ALU.is_equal, ALU.mult)
                last.then_inc(s["pads"], 1)
                e.wait_ge(s["pads"], g + 2)
                e.tensor_tensor(mask[:, p], hit[:, p, 0], hit[:, p, 1], ALU.add).then_inc(s["mask_ready"], 1)

            @block.vector
            def _(e):
                e.sem_inc(s["y_added"], 2)
                e.wait_ge(s["const"], 1)
                e.wait_ge(s["pads"], 1)
                e.wait_ge(s["router"], 112)

                def apply(g, p, first=False):
                    if not first:
                        e.wait_ge(s["xt_psum"], g - 1)
                    norm_apply(e, s, w, g, p)

                def body(g, p, has_prev, has_next, has_second):
                    e.wait_ge(s["bias_psum"], g + 1)
                    xg = w.x[:, span(g, GW)]
                    e.tensor_tensor(xg, xg, ps_t[:, :], ALU.add).then_inc(s["bias_added"], 1)
                    e.wait_ge(s["mask_ready"], g + 1)
                    e.wait_ge(s["bias_added"], g + 1)
                    for x in range(E3):
                        k = g * E3 + x
                        e.wait_ge(s["y_psum"], k + 3)
                        if x:
                            e.wait_ge(s["y_added"], k + 2)
                        for t in range(GT):
                            xt = w.x[:, span(g, GW, t * D, D)]
                            last = e.scalar_tensor_tensor(xt, ps_y[x % 2][:, t * D:(t + 1) * D], mask[:, p, t, x:x + 1], xt,
                                                          ALU.mult, ALU.add)
                        last.then_inc(s["y_added"], 1)
                        if has_second and x == 0:
                            norm_stats(e, s, w, g + 2, p)
                        if has_next and x == 1:
                            route_logits(e, g + 1, 1 - p)
                        if has_second and x == 1:
                            apply(g + 2, p)
                        if has_next and x == 2:
                            route_best(e, g + 1, 1 - p)
                        if has_next and x == 3:
                            route_mask(e, g + 1, 1 - p)
                norm_stats(e, s, w, 0, 0)
                norm_stats(e, s, w, 1, 1)
                apply(0, 0, True)
                apply(1, 1, True)
                route_logits(e, 0, 0)
                route_best(e, 0, 0)
                route_mask(e, 0, 0)
                over_groups_ahead(e, body)

            @block.gpsimd
            def _(e):
                e.iota(iota[:, :], pattern=[[1, E3]], base=0, channel_multiplier=0, allow_small_or_imprecise_dtypes=True).then_inc(s["const"], 1)
                e.memset(prob[:, :, :, E3:PAD], -1.0).then_inc(s["pads"], 1)

                def body(g, p, has_prev, has_next, has_second):
                    if has_second:
                        norm_rstd(e, s, w, g + 2, p)
                norm_rstd(e, s, w, 0, 0)
                norm_rstd(e, s, w, 1, 1)
                over_groups_ahead(e, body)

            @block.tensor
            def _(e):
                e.sem_inc(s["y_psum"], 2)
                e.wait_ge(s["router"], 112)

                def transposes(g, p, first=False):
                    if not first:
                        e.wait_ge(s["bias_added"], g)
                    norm_transpose(e, s, w, g, p, ps_t)

                def router(g, p, first=False):
                    e.wait_ge(s["xt_ready"], g + 1)
                    if not first:
                        e.wait_ge(s["lg_ready"], g)
                    e.matmul(ps_m[0:R3, :], rw1[:, :], w.xt[:, p, :], start=True, stop=True).then_inc(s["r_psum"], 1)

                def router_logits(g, p):
                    e.wait_ge(s["r_ready"], g + 1)
                    for t in range(GT):
                        last = e.matmul(ps_m[:, t * E3:(t + 1) * E3], r_t[:, p, t * P:(t + 1) * P], rw2[:, :], start=True, stop=True)
                    last.then_inc(s["logit_psum"], 1)

                def bias_of(g, p):
                    e.wait_ge(s["mask_ready"], g + 1)
                    e.wait_ge(s["xt_ready"], g + 1)
                    for t in range(GT):
                        last = e.transpose(ps_t[0:E3, t * P:(t + 1) * P], mask[:, p, t, :], w.ident[:, :])
                    last.then_inc(s["mask_psum"], 1)
                    e.wait_ge(s["mask_t_ready"], g + 1)
                    for t in range(GT):
                        last = e.matmul(ps_t[:, t * D:(t + 1) * D], mask_t[:, p, t * P:(t + 1) * P], b3[:, :], start=True, stop=True)
                    last.then_inc(s["bias_psum"], 1)

                def layer1(g, p, x):
                    e.wait_ge(s["h1_ready"], g * E3 + x + 1)
                    e.matmul(ps_1[x % 2][:, :], w1[:, x, :], w.xt[:, p, :], start=True, stop=True).then_inc(s["h1_psum"], 1)

                def layer2(g, p, x):
                    e.wait_ge(s["h2_ready"], g * E3 + x + 1)
                    e.wait_ge(s["h1_ready"], g * E3 + x + 3)
                    e.matmul(ps_2[x % 2][:, :], w2[:, x, :], h1[:, x % 2, :], start=True, stop=True).then_inc(s["h2_psum"], 1)

                def layer3(g, p, x):
                    e.wait_ge(s["y_added"], g * E3 + x + 1)
                    e.wait_ge(s["h2_ready"], g * E3 + x + 3)
                    for t in range(GT):
                        last = e.matmul(ps_y[x % 2][:, t * D:(t + 1) * D], h2[:, x % 2, t * P:(t + 1) * P], w3[:, x, :], start=True, stop=True)
                    last.then_inc(s["y_psum"], 1)

                def body(g, p, has_next):
                    layer1(g, p, 0)
                    bias_of(g, p)
                    for x in range(E3):
                        if x + 1 < E3:
                            layer1(g, p, x + 1)
                        layer2(g, p, x)
                        if has_next and x == 0:
                            transposes(g + 1, 1 - p)
                        if has_next and x == 1:
                            router(g + 1, 1 - p)
                        if has_next and x == 2:
                            router_logits(g + 1, 1 - p)
                        if x:
                            layer3(g, p, x - 1)
                    layer3(g, p, E3 - 1)
                transposes(0, 0, True)
                router(0, 0, True)
                router_logits(0, 0)
                e.wait_ge(s["experts"], 48)
                over_groups(e, body)

            @block.scalar
            def _(e):
                e.sem_inc(s["h1_ready"], 2)
                e.sem_inc(s["h2_ready"], 2)
                e.preload_act_table(ACT.Exp)
                e.wait_ge(s["router"], 112)

                def copy_xt(g, p):
                    norm_copy(e, s, w, g, p, ps_t[:, :])

                def router(g, p):
                    e.wait_ge(s["r_psum"], g + 1)
                    e.activation(r_t[:, p, :], ps_m[0:R3, :], ACT.Relu, bias=rb1[:, 0:1]).then_inc(s["r_ready"], 1)

                def exps(g, p):
                    e.wait_ge(s["logit_ready"], g + 1)
                    e.activation(expo[:, p], logits[:, p], ACT.Exp).then_inc(s["exp_ready"], 1)

                def top_exps(g, p):
                    e.wait_ge(s["diff_ready"], g + 1)
                    e.activation(top[:, p], diff[:, p], ACT.Exp).then_inc(s["top_ready"], 1)

                def body(g, p, has_next):
                    for x in range(E3):
                        e.wait_ge(s["h1_psum"], g * E3 + x + 1)
                        e.wait_ge(s["h2_psum"], g * E3 + x + 1)
                        e.activation(h1[:, x % 2, :], ps_1[x % 2][:, :], ACT.Relu, bias=b1[:, x:x + 1]).then_inc(s["h1_ready"], 1)
                        if x == 0:
                            e.wait_ge(s["mask_psum"], g + 1)
                            e.activation(mask_t[:, p, :], ps_t[0:E3, :], ACT.Copy).then_inc(s["mask_t_ready"], 1)
                        if has_next and x == 3:
                            exps(g + 1, 1 - p)
                        if has_next and x == 4:
                            top_exps(g + 1, 1 - p)
                        e.wait_ge(s["h2_psum"], g * E3 + x + 3)
                        e.wait_ge(s["y_psum"], g * E3 + x + 1)
                        e.activation(h2[:, x % 2, :], ps_2[x % 2][:, :], ACT.Relu, bias=b2[:, x:x + 1]).then_inc(s["h2_ready"], 1)
                        if has_next and x == 0:
                            copy_xt(g + 1, 1 - p)
                        if has_next and x == 1:
                            router(g + 1, 1 - p)
                e.sem_inc(s["h2_psum"], 2)
                copy_xt(0, 0)
                router(0, 0)
                exps(0, 0)
                top_exps(0, 0)
                over_groups(e, body)


def store(nc, w, out):
    with nc.Block() as block:
        @block.sync
        def _(e):
            e.dma_start(out.rearrange("b (h p) d -> p (b h) d", p=P),
                        w.x[:, :].rearrange("p (t d) -> p t d", d=D)).then_inc(w.stored, 16)
            e.wait_ge(w.stored, 16)


def four_layers(nc, a, out):
    with ExitStack() as c:
        w = Resident(nc, c)
        constants(nc, w)
        l0_gnn(nc, w, a)
        l0_ffn(nc, w, a)
        l1_gnn(nc, w, a)
        l1_ffn(nc, w, a)
        l2_gnn(nc, w, a)
        l2_ffn(nc, w, a)
        l3_gnn(nc, w, a)
        l3_ffn(nc, w, a)
        store(nc, w, out)


def laid_out(i):
    o = {k: np.asarray(v) for k, v in i.items()}
    o["adj_t"] = o["adj"].transpose(0, 2, 1)
    o["L0_gnn_Wt"] = o["L0_gnn_W"].T
    o["L0_ffn_b1"] = np.concatenate([o["L0_ffn_b1p"], o["L0_ffn_b1s"][None]]).reshape(EA, C0, P).transpose(2, 0, 1)
    o["L1_ffn_pack"] = np.concatenate([o["L1_ffn_W1"], o["L1_ffn_W2"].reshape(E1, C1, P, D).transpose(0, 2, 1, 3).reshape(E1, P, C1 * D),
                                       o["L1_ffn_b1"].reshape(E1, C1, P).transpose(0, 2, 1)], axis=2)
    o["L2_ffn_hl_w_t"] = o["L2_ffn_hl_w"].reshape(D, D).T
    o["L2_ffn_wq_t"] = o["L2_ffn_wq"].transpose(0, 3, 1, 2)
    o["L2_ffn_wk_t"] = o["L2_ffn_wk"].transpose(0, 2, 1)
    o["L2_ffn_wv_t"] = o["L2_ffn_wv"].transpose(0, 2, 1)
    o["L2_ffn_gate_w_t"] = o["L2_ffn_gate_w"].transpose(2, 0, 1)
    o["L2_ffn_fc1_t"] = o["L2_ffn_fc1_w"].T
    o["L2_ffn_fc2_t"] = o["L2_ffn_fc2_w"].T
    o["L2_ffn_fgate_t"] = o["L2_ffn_fgate_w"].T
    o["L3_ffn_b1_t"] = o["L3_ffn_expert_b1"].T
    o["L3_ffn_b2_t"] = o["L3_ffn_expert_b2"].T
    return {k: np.ascontiguousarray(v) for k, v in o.items() if k not in LAID_OUT_ONLY}


LAID_OUT_ONLY = ("L0_gnn_W", "L0_ffn_b1p", "L0_ffn_b1s", "L1_ffn_W1", "L1_ffn_W2", "L1_ffn_b1", "L2_ffn_hl_w", "L2_ffn_wq", "L2_ffn_wk",
                 "L2_ffn_wv", "L2_ffn_gate_w", "L2_ffn_fc1_w", "L2_ffn_fc2_w", "L2_ffn_fgate_w", "L3_ffn_expert_b1", "L3_ffn_expert_b2")


def kernel(**inputs):
    import concourse.bacc as bacc
    from concourse.bass_utils import run_bass_kernel_spmd

    nc = bacc.Bacc("TRN2", target_bir_lowering=False, num_devices=1)
    arrays, a = {}, {}
    for name, array in laid_out(inputs).items():
        arrays[f"in_{name}"] = array
        a[name] = nc.dram_tensor(f"in_{name}", array.shape, mybir.dt.from_np(array.dtype), kind="ExternalInput").ap()
    out = nc.dram_tensor("out", (B, N, D), F32, kind="ExternalOutput").ap()
    four_layers(nc, a, out)
    r = run_bass_kernel_spmd(nc, [arrays], core_ids=[0])
    return r.results[0]["out"]
```
